# Optimizing a Trainium2 kernel written in Bass

```python
import numpy as np
import jax
import jax.numpy as jnp

def _softmax(x, axis=-1):
    return jax.nn.softmax(x, axis=axis)

def _gelu(x):
    return jax.nn.gelu(x, approximate=True)

def _silu(x):
    return jax.nn.silu(x)

def _sigmoid(x):
    return jax.nn.sigmoid(x)

def _layernorm(x, axis=-1, eps=1e-05):
    m = jnp.mean(x, axis=axis, keepdims=True)
    v = jnp.var(x, axis=axis, keepdims=True)
    return (x - m) / jnp.sqrt(v + eps)

def _scatter_add(tgt, idx, src, axis=0):
    return tgt.at[idx].add(src)

def _segment_sum(src, seg, n):
    return jax.ops.segment_sum(src, seg, n)
kernel_name = 'mk_gps_d1_gnn_r8_b50737'

def setup_inputs(seed: int=0):
    np.random.seed(seed)
    _w = jnp.asarray

    def _rec_inputs():
        import jax
        import jax.numpy as jnp
        _gk = jax.random.key(seed)
        x = -0.0003713 + 1 * jax.random.normal(jax.random.fold_in(_gk, 1), (6250, 256), jnp.float32)
        _s = jax.random.randint(jax.random.fold_in(_gk, 2), (100000,), 0, 6250, jnp.int32)
        _d = jax.random.randint(jax.random.fold_in(_gk, 3), (100000,), 0, 6250, jnp.int32)
        _loop = jnp.arange(6250, dtype=jnp.int32)
        src = jnp.concatenate([_s, _d, _loop])
        dst = jnp.concatenate([_d, _s, _loop])
        _o = jnp.argsort(dst, stable=True)
        src = src[_o]
        dst = dst[_o]
        return (x, src, dst)
    x, src, dst = _rec_inputs()

    def _L0_gnn_setup():
        import jax, jax.numpy as jnp
        import numpy as np
        N_NODES = 6250
        EPS = 1e-12
        key = jax.random.key(seed)
        k1, k2, k3 = jax.random.split(key, 3)
        d_in, d_out, n_edges = (256, 256, 100000)
        input_matrix = jax.random.normal(k1, (N_NODES, d_in), dtype=jnp.float32)
        adjacency_coo_matrix = jax.random.randint(k2, (2, n_edges), 0, N_NODES, dtype=jnp.int64)
        W = jax.random.normal(k3, (2 * d_in, d_out), dtype=jnp.float32) * (1.0 / np.sqrt(2 * d_in))
        b = jnp.zeros((d_out,), dtype=jnp.float32)
        return {'input_matrix': input_matrix, 'adjacency_coo_matrix': adjacency_coo_matrix, 'W': W, 'b': b}
    _L0_gnn_all = _L0_gnn_setup()
    _L0_gnn_in = {k: v for k, v in _L0_gnn_all.items() if k in ('W', 'b')}
    del _L0_gnn_all

    def _L0_mix_setup():
        import jax, jax.numpy as jnp
        import numpy as np
        HEADS, DIM_HEAD = (8, 64)
        EPS = 1e-05

        def instance_norm(t):
            mu = jnp.mean(t, axis=-1, keepdims=True)
            var = jnp.mean((t - mu) ** 2, axis=-1, keepdims=True)
            return (t - mu) * jax.lax.rsqrt(var + EPS)
        key = jax.random.key(seed)
        k1, k2, k3, k4 = jax.random.split(key, 4)
        B, N, D = (8, 1024, 256)
        inner = HEADS * DIM_HEAD
        x = jax.random.normal(k1, (B, N, D), jnp.float32)
        w_qkv = jax.random.normal(k2, (3 * inner, D), jnp.float32) / np.sqrt(D).astype(np.float32)
        w_out = jax.random.normal(k3, (D, inner), jnp.float32) / np.sqrt(inner).astype(np.float32)
        b_out = 0.01 * jax.random.normal(k4, (D,), jnp.float32)
        return {'x': x, 'w_qkv': w_qkv, 'w_out': w_out, 'b_out': b_out}
    _L0_mix_all = _L0_mix_setup()
    _L0_mix_in = {k: v for k, v in _L0_mix_all.items() if k in ('w_qkv', 'w_out', 'b_out')}
    del _L0_mix_all

    def _L0_ffn_setup():
        import jax, jax.numpy as jnp
        import numpy as np
        B, N, D = (16, 512, 256)
        NUM_EXPERTS, TOP_K, HEADS = (4, 2, 4)
        N_EDGES = 131072
        LN_EPS = 1e-05

        def _layernorm(x, g, b):
            mu = x.mean(-1, keepdims=True)
            var = ((x - mu) ** 2).mean(-1, keepdims=True)
            return (x - mu) * jax.lax.rsqrt(var + LN_EPS) * g + b

        def _forward(x, edge_index, W_gat, att_src, att_dst, b_gat, ln_gamma, ln_beta, W1, b1, W2, b2):
            Bc, Nc, Dc = x.shape
            M = Bc * Nc
            x_flat = x.reshape(M, Dc)
            h = (x_flat @ W_gat).reshape(M, HEADS, NUM_EXPERTS)
            loops = jnp.arange(M, dtype=edge_index.dtype)
            src = jnp.concatenate([edge_index[0], loops])
            dst = jnp.concatenate([edge_index[1], loops])
            a_src = (h * att_src).sum(-1)
            a_dst = (h * att_dst).sum(-1)
            e = jax.nn.leaky_relu(a_src[src] + a_dst[dst], negative_slope=0.2)
            e_max = jax.ops.segment_max(e, dst, num_segments=M)
            ee = jnp.exp(e - e_max[dst])
            denom = jax.ops.segment_sum(ee, dst, num_segments=M)
            alpha = ee / (denom[dst] + 1e-16)
            msg = h[src] * alpha[:, :, None]
            agg = jax.ops.segment_sum(msg, dst, num_segments=M).reshape(M, HEADS * NUM_EXPERTS) + b_gat
            scores = _layernorm(agg, ln_gamma, ln_beta).reshape(M, HEADS, NUM_EXPERTS).mean(1)
            scores = scores.reshape(Bc, Nc, NUM_EXPERTS)
            topk_s, topk_i = jax.lax.top_k(scores, TOP_K)
            w = jax.nn.softmax(topk_s, axis=-1)
            out = jnp.zeros_like(x)
            for ei in range(NUM_EXPERTS):
                g = jnp.where(topk_i == ei, w, 0.0).sum(-1)
                hh = jax.nn.gelu(x @ W1[ei] + b1[ei], approximate=False)
                out = out + g[..., None] * (hh @ W2[ei] + b2[ei])
            return out
        key = jax.random.key(seed)
        ks = jax.random.split(key, 8)
        s = 0.05
        return {'x': jax.random.normal(ks[0], (B, N, D), jnp.float32), 'W_gat': jax.random.normal(ks[1], (D, HEADS * NUM_EXPERTS), jnp.float32) * s, 'att_src': jax.random.normal(ks[2], (HEADS, NUM_EXPERTS), jnp.float32) * s, 'att_dst': jax.random.normal(ks[3], (HEADS, NUM_EXPERTS), jnp.float32) * s, 'b_gat': jnp.zeros((HEADS * NUM_EXPERTS,), jnp.float32), 'ln_gamma': jnp.ones((HEADS * NUM_EXPERTS,), jnp.float32), 'ln_beta': jnp.zeros((HEADS * NUM_EXPERTS,), jnp.float32), 'W1': jax.random.normal(ks[4], (NUM_EXPERTS, D, 2 * D), jnp.float32) * s, 'b1': jnp.zeros((NUM_EXPERTS, 2 * D), jnp.float32), 'W2': jax.random.normal(ks[5], (NUM_EXPERTS, 2 * D, D), jnp.float32) * s, 'b2': jnp.zeros((NUM_EXPERTS, D), jnp.float32), 'edge_index': jax.random.randint(ks[6], (2, N_EDGES), 0, B * N, jnp.int32)}
    _L0_ffn_all = _L0_ffn_setup()
    _L0_ffn_in = {k: v for k, v in _L0_ffn_all.items() if k in ('W_gat', 'att_src', 'att_dst', 'b_gat', 'ln_gamma', 'ln_beta', 'W1', 'b1', 'W2', 'b2', 'edge_index')}
    del _L0_ffn_all
    return {'x': x, 'src': src, 'dst': dst, 'L0_gnn_W': _L0_gnn_in['W'], 'L0_gnn_b': _L0_gnn_in['b'], 'L0_mix_w_qkv': _L0_mix_in['w_qkv'], 'L0_mix_w_out': _L0_mix_in['w_out'], 'L0_mix_b_out': _L0_mix_in['b_out'], 'L0_ffn_W_gat': _L0_ffn_in['W_gat'], 'L0_ffn_att_src': _L0_ffn_in['att_src'], 'L0_ffn_att_dst': _L0_ffn_in['att_dst'], 'L0_ffn_b_gat': _L0_ffn_in['b_gat'], 'L0_ffn_ln_gamma': _L0_ffn_in['ln_gamma'], 'L0_ffn_ln_beta': _L0_ffn_in['ln_beta'], 'L0_ffn_W1': _L0_ffn_in['W1'], 'L0_ffn_b1': _L0_ffn_in['b1'], 'L0_ffn_W2': _L0_ffn_in['W2'], 'L0_ffn_b2': _L0_ffn_in['b2'], 'L0_ffn_edge_index': _L0_ffn_in['edge_index']}

def reference(x, src, dst, L0_gnn_W, L0_gnn_b, L0_mix_w_qkv, L0_mix_w_out, L0_mix_b_out, L0_ffn_W_gat, L0_ffn_att_src, L0_ffn_att_dst, L0_ffn_b_gat, L0_ffn_ln_gamma, L0_ffn_ln_beta, L0_ffn_W1, L0_ffn_b1, L0_ffn_W2, L0_ffn_b2, L0_ffn_edge_index):
    import jax
    import jax.numpy as jnp

    def _L0_gnn_ref(input_matrix, adjacency_coo_matrix, W, b):
        import jax, jax.numpy as jnp
        import numpy as np
        N_NODES = 6250
        EPS = 1e-12
        src = adjacency_coo_matrix[0]
        dst = adjacency_coo_matrix[1]
        neigh_sum = jax.ops.segment_sum(input_matrix[src], dst, num_segments=N_NODES)
        deg = jax.ops.segment_sum(jnp.ones_like(dst, dtype=input_matrix.dtype), dst, num_segments=N_NODES)
        neigh_mean = neigh_sum / jnp.maximum(deg, 1.0)[:, None]
        h = jnp.concatenate([input_matrix, neigh_mean], axis=-1)
        out = jax.nn.relu(h @ W + b)
        norm = jnp.maximum(jnp.linalg.norm(out, axis=-1, keepdims=True), EPS)
        return out / norm

    def _L0_mix_ref(x, w_qkv, w_out, b_out):
        import jax, jax.numpy as jnp
        import numpy as np
        HEADS, DIM_HEAD = (8, 64)
        EPS = 1e-05

        def instance_norm(t):
            mu = jnp.mean(t, axis=-1, keepdims=True)
            var = jnp.mean((t - mu) ** 2, axis=-1, keepdims=True)
            return (t - mu) * jax.lax.rsqrt(var + EPS)
        B, N, _ = x.shape
        H, Dh = (HEADS, DIM_HEAD)
        qkv = jnp.einsum('bnd,ed->bne', x, w_qkv)
        q, k, v = jnp.split(qkv, 3, axis=-1)

        def to_heads(t):
            return t.reshape(B, N, H, Dh).transpose(0, 2, 1, 3)
        q, k, v = (to_heads(q), to_heads(k), to_heads(v))
        k = instance_norm(k)
        v = instance_norm(v)
        dots = jnp.einsum('bhnd,bhne->bhde', k, v)
        out = jnp.einsum('bhnd,bhde->bhne', q, dots) / N
        out = out.transpose(0, 2, 1, 3).reshape(B, N, H * Dh)
        return jnp.einsum('bne,de->bnd', out, w_out) + b_out

    def _L0_ffn_ref(x, W_gat, att_src, att_dst, b_gat, ln_gamma, ln_beta, W1, b1, W2, b2, edge_index):
        import jax, jax.numpy as jnp
        import numpy as np
        B, N, D = (16, 512, 256)
        NUM_EXPERTS, TOP_K, HEADS = (4, 2, 4)
        N_EDGES = 131072
        LN_EPS = 1e-05

        def _layernorm(x, g, b):
            mu = x.mean(-1, keepdims=True)
            var = ((x - mu) ** 2).mean(-1, keepdims=True)
            return (x - mu) * jax.lax.rsqrt(var + LN_EPS) * g + b

        def _forward(x, edge_index, W_gat, att_src, att_dst, b_gat, ln_gamma, ln_beta, W1, b1, W2, b2):
            Bc, Nc, Dc = x.shape
            M = Bc * Nc
            x_flat = x.reshape(M, Dc)
            h = (x_flat @ W_gat).reshape(M, HEADS, NUM_EXPERTS)
            loops = jnp.arange(M, dtype=edge_index.dtype)
            src = jnp.concatenate([edge_index[0], loops])
            dst = jnp.concatenate([edge_index[1], loops])
            a_src = (h * att_src).sum(-1)
            a_dst = (h * att_dst).sum(-1)
            e = jax.nn.leaky_relu(a_src[src] + a_dst[dst], negative_slope=0.2)
            e_max = jax.ops.segment_max(e, dst, num_segments=M)
            ee = jnp.exp(e - e_max[dst])
            denom = jax.ops.segment_sum(ee, dst, num_segments=M)
            alpha = ee / (denom[dst] + 1e-16)
            msg = h[src] * alpha[:, :, None]
            agg = jax.ops.segment_sum(msg, dst, num_segments=M).reshape(M, HEADS * NUM_EXPERTS) + b_gat
            scores = _layernorm(agg, ln_gamma, ln_beta).reshape(M, HEADS, NUM_EXPERTS).mean(1)
            scores = scores.reshape(Bc, Nc, NUM_EXPERTS)
            topk_s, topk_i = jax.lax.top_k(scores, TOP_K)
            w = jax.nn.softmax(topk_s, axis=-1)
            out = jnp.zeros_like(x)
            for ei in range(NUM_EXPERTS):
                g = jnp.where(topk_i == ei, w, 0.0).sum(-1)
                hh = jax.nn.gelu(x @ W1[ei] + b1[ei], approximate=False)
                out = out + g[..., None] * (hh @ W2[ei] + b2[ei])
            return out
        return _forward(x, edge_index, W_gat, att_src, att_dst, b_gat, ln_gamma, ln_beta, W1, b1, W2, b2)
    edge_index = jnp.stack([src, dst])
    xn = _layernorm(x, axis=-1)
    x = x + _L0_gnn_ref(xn, edge_index, L0_gnn_W, L0_gnn_b) + _L0_mix_ref(xn[None], L0_mix_w_qkv, L0_mix_w_out, L0_mix_b_out)[0]
    x = x + _L0_ffn_ref(_layernorm(x, axis=-1)[None], L0_ffn_W_gat, L0_ffn_att_src, L0_ffn_att_dst, L0_ffn_b_gat, L0_ffn_ln_gamma, L0_ffn_ln_beta, L0_ffn_W1, L0_ffn_b1, L0_ffn_W2, L0_ffn_b2, L0_ffn_edge_index)[0]
    return x

_drawn_inputs = setup_inputs


def setup_inputs(seed=0):
    import zlib

    import numpy as np

    out = dict(_drawn_inputs(seed))
    spreads = {'L0_gnn_b': (0.0, 0.502),
     'L0_ffn_b_gat': (0.0, 0.1),
     'L0_ffn_ln_gamma': (1.0, 0.2),
     'L0_ffn_ln_beta': (0.0, 0.1),
     'L0_ffn_b1': (0.0, 0.1),
     'L0_ffn_b2': (0.0, 0.1)}
    factors = {}
    for name, (base, spread) in spreads.items():
        noise = np.random.default_rng([zlib.crc32(name.encode()), seed]).standard_normal(out[name].shape)
        drawn = base * np.exp(spread * noise) if base else spread * noise
        out[name] = jnp.asarray(drawn.astype(out[name].dtype))
    for name, factor in factors.items():
        out[name] = (out[name] * factor).astype(out[name].dtype)
    return out
```

```python
from contextlib import ExitStack

import concourse.bass as bass
from concourse import mybir

F32 = mybir.dt.float32
I32 = mybir.dt.int32
ALU = mybir.AluOpType
ACT = mybir.ActivationFunctionType
AX = mybir.AxisListType.X

P = 128
GNN_EPS, LN_EPS, DEN_EPS = 1e-12, 1e-5, 1e-16
SLOPE = 0.2


def hold(eng, sem, value):
    eng.wait_ge(sem, value)
    if not isinstance(value, int):
        eng.nop(nofuse=True)


def after(b, k):
    return not isinstance(b, int) or b >= k


def chain(eng, sem, b, per):
    count = [0]

    def link(ins):
        count[0] += 1
        assert per is None or count[0] <= per
        ins.then_inc(sem, 1)
        hold(eng, sem, b * (per or 0) + count[0])

    return link


def steps(eng, stages, n):
    most = max(lag for lag, _ in stages)

    def fixed(s):
        for lag, body in stages:
            if 0 <= s - lag < n:
                body(s - lag, (s - lag) % 2, (s - lag) // 2)

    rounds = (n - most - 2) // 2
    first = n - 2 * rounds
    for s in range(first):
        fixed(s)
    with eng.Fori(0, rounds) as r:
        for u in range(2):
            for lag, body in stages:
                c = first + u - lag
                body(r * 2 + c, c % 2, r + c // 2)
    for s in range(n, n + most):
        fixed(s)


def build(nc, x, src, dst, gnn_w, gnn_b, w_qkv, w_out, b_out, w_gat, att_src, att_dst, b_gat,
          ln_g, ln_b, w1, b1, w2, b2, edges, out):
    N, D = x.shape
    E = src.shape[0]
    NB = -(-N // P)
    NP = NB * P
    LAST = N - (NB - 1) * P
    KD = D // P
    INNER = w_out.shape[1]
    DH = 64
    HM = INNER // DH
    NE, _, FF = w1.shape
    FT = FF // P
    HT = NE * FT
    GH = att_src.shape[0]
    GW = GH * NE
    PAY = GW + GH
    ET = -(-E // P)
    RT = edges.shape[1] // P
    assert RT * P == edges.shape[1]
    C = 7
    NC = NB // C
    assert NB == NC * C and KD == 2 and PAY == 20

    dram = lambda name, shape, dt=F32: nc.dram_tensor(name, shape, dt, kind="Internal").ap()
    XN = dram("xn_table", [NP, D])
    XP = dram("x_padded", [NP, D])
    SRC = dram("src_padded", [ET * P, 1], I32)
    DST = dram("dst_padded", [ET * P, 1], I32)
    RSRC = dram("router_src", [RT * P, 1], I32)
    RDST = dram("router_dst", [RT * P, 1], I32)
    ACC = dram("neighbour_sum", [NP, D + 1])
    TAB = dram("router_table", [NP, PAY])
    MAXT = dram("max_table", [NP, GH])
    MD = dram("shift_table", [NP, 2 * GH])
    AGG = dram("attention_sum", [NP, PAY])

    def by_block(t):
        return t.rearrange("(b p) c -> p b c", p=P)

    top = ExitStack()
    sem = lambda name: top.enter_context(nc.semaphore(name))
    sb = lambda st, name, shape, dt=F32: st.enter_context(nc.sbuf_tensor(name, shape, dt))
    ps = lambda st, name, shape: st.enter_context(nc.psum_tensor(name, shape, F32))

    with top:
        X = sb(top, "x_rows", [P, NB, D])
        XT = sb(top, "x_cols", [P, KD, NP])
        ident = sb(top, "ident", [P, P])
        lower = sb(top, "lower", [P, P])
        mix = sb(top, "mix_matrix", [P, KD, D])
        wg = sb(top, "gnn_w_sb", [P, 2 * KD, D])
        zero = sb(top, "zero", [P, D + 1])
        bg = sb(top, "gnn_b_rows", [P, D])
        bo = sb(top, "b_out_rows", [P, D])
        wgat = sb(top, "w_gat_sb", [P, KD, GW])
        att = sb(top, "att_rows", [P, 2, GW])
        gb = sb(top, "gate_rows", [P, 3, GW])
        T = sb(top, "router_rows", [P, NB, PAY])
        AD = sb(top, "a_dst_rows", [P, NB, GH])
        MXS = sb(top, "max_rows", [P, NB, GH])
        gate = sb(top, "gates", [P, NB, NE])

        with ExitStack() as st:
            sq = sb(st, "squares", [P, C, D])
            lnm = sb(st, "ln_mean", [P, NC, C])
            lnv = sb(st, "ln_var", [P, NC, C])
            lns = sb(st, "ln_std", [P, NC, C])
            wkv_n = sb(st, "wkv_rows", [P, 8, D])
            wkv = sb(st, "wkv_cols", [P, KD, 2 * INNER])
            wkm = sb(st, "wkv_mean", [P, KD, 2 * HM])
            wq = sb(st, "wq_rows", [P, 4, D])
            wo_n = sb(st, "w_out_rows", [P, KD, INNER])
            wo = sb(st, "w_out_cols", [P, 4, D])
            kvsq = sb(st, "kv_squares", [P, 2, 2 * INNER])
            kss = sb(st, "kv_sums", [P, 2, 2 * HM])
            kpr = sb(st, "kv_var_product", [P, 2, HM])
            kst = sb(st, "kv_std_product", [P, 2, HM])
            kri = sb(st, "kv_scale", [P, 2, HM])
            ks = sb(st, "k_scaled", [P, 2, INNER])
            vs = sb(st, "v_rows", [P, 2, INNER])
            dots = sb(st, "dots_diag", [P, 4, P])
            bt = sb(st, "b_cols", [P, 4, D])
            xs = sb(st, "x_stage", [P, 2, D])
            xc_ = sb(st, "x_cols_stage", [P, 2, KD * P])
            pkv = ps(st, "ps_kv", [P, 2, 2 * INNER])
            pt = ps(st, "ps_t", [P, 2, 512])
            pd = ps(st, "ps_dots", [P, 4, P])

            x_in = [sem(f"x_in{c}") for c in range(NC)]
            w_in, pad_in, tabs_out, x_zero = sem("w_in"), sem("pad_in"), sem("tabs_out"), sem("x_zero")
            consts, ident_z, lower_z = sem("consts"), sem("ident_z"), sem("lower_z")
            dchain, ln_var_ok, ln_std_ok, ln_ok = sem("dve_chain"), sem("ln_var_ok"), sem("ln_std_ok"), sem("ln_ok")
            wt_ok, wt_used, wkv_ok = sem("wt_ok"), sem("wt_used"), sem("wkv_ok")
            xt_ps, xt_ok, xs_ok, xt_kept = sem("xt_ps"), sem("xt_ok"), sem("xs_ok"), sem("xt_kept")
            kv_ok, kvsq_ok, v_ok, kss_ok, kpr_ok = sem("kv_ok"), sem("kvsq_ok"), sem("v_ok"), sem("kss_ok"), sem("kpr_ok")
            kst_ok, kri_ok, ks_ok, dots_ok = sem("kst_ok"), sem("kri_ok"), sem("ks_ok"), sem("dots_ok")
            dd_ok, bt_ps, bt_ok, mix_ps, mix_ok = sem("dd_ok"), sem("bt_ps"), sem("bt_ok"), sem("mix_ps"), sem("mix_ok")
            dz_ok, kve_ok, fill_ok = sem("dz_ok"), sem("kve_ok"), sem("fill_ok")
            e_in, e_ok, e_out = sem("redges_in"), sem("redges_ok"), sem("redges_out")
            re = sb(st, "router_edges", [P, 2, RT], I32)
            fill = sb(st, "edge_fill", [P, 2], I32)
            block = st.enter_context(nc.Block())

            W_LOADS = 14

            @block.sync
            def _(sp):
                sp.dma_start(re[:, :, :], edges.rearrange("k (p t) -> p k t", p=P)).then_inc(e_in, 16)
                sp.wait_ge(x_zero, 1)
                for c in range(NC):
                    r0, r1 = c * C * P, min((c + 1) * C * P, N)
                    full = (r1 - r0) // P
                    sp.dma_start(X[:, c * C:c * C + full, :], by_block(x[r0:r0 + full * P, :])).then_inc(x_in[c], 16)
                    if full < C:
                        sp.dma_start(X[0:LAST, NB - 1, :], x[(NB - 1) * P:N, :]).then_inc(x_in[c], 16)
                full_e = (ET - 1) * P
                for a, t in ((src, SRC), (dst, DST)):
                    sp.dma_start(t[0:full_e, 0].rearrange("(a b) -> a b", b=P), a[0:full_e].rearrange("(a b) -> a b", b=P)).then_inc(pad_in, 16)
                    sp.dma_start(t[full_e:E, :], a[full_e:E].rearrange("(a b) -> a b", b=1)).then_inc(pad_in, 16)
                sp.dma_start(XP[0:N, :], x).then_inc(pad_in, 16)
                sp.wait_ge(fill_ok, 3)
                sp.dma_start(XP[N:NP, :], zero[0:NP - N, 0:D]).then_inc(pad_in, 16)
                sp.dma_start(SRC[E:ET * P, :], fill[0:ET * P - E, 0:1]).then_inc(pad_in, 16)
                sp.dma_start(DST[E:ET * P, :], fill[0:ET * P - E, 1:2]).then_inc(pad_in, 16)
                sp.wait_ge(e_ok, 2)
                for k, t in ((0, RSRC), (1, RDST)):
                    sp.dma_start(t.rearrange("(p t) c -> p (t c)", p=P), re[:, k, :]).then_inc(e_out, 16)
                sp.wait_ge(e_out, 32)
                for c in range(NC):
                    sp.wait_ge(ln_ok, (c + 1) * C)
                    sp.dma_start(by_block(XN[c * C * P:(c + 1) * C * P, :]), X[:, c * C:(c + 1) * C, :]).then_inc(tabs_out, 16)
                sp.wait_ge(tabs_out, 16 * NC)
                sp.wait_ge(pad_in, 16 * 8)

            @block.gpsimd
            def _(pool):
                nc.gpsimd.memset(ident[:, :], 0.0).then_inc(ident_z, 1)
                nc.gpsimd.memset(lower[:, :], 1.0).then_inc(lower_z, 1)
                pool.wait_ge(ident_z, 1)
                nc.gpsimd.affine_select(out=ident[:, :], in_=ident[:, :], compare_op=ALU.not_equal, fill=1.0,
                                        base=0, pattern=[[-1, P]], channel_multiplier=1).then_inc(consts, 1)
                pool.wait_ge(lower_z, 1)
                nc.gpsimd.affine_select(out=lower[:, :], in_=lower[:, :], compare_op=ALU.is_gt, fill=0.0,
                                        base=0, pattern=[[-1, P]], channel_multiplier=1).then_inc(consts, 1)

                def stage(b, q, m):
                    hold(pool, ln_ok, b + 1)
                    if after(b, 2):
                        hold(pool, xt_ps, b - 1)
                    nc.gpsimd.tensor_copy(xs[:, q, :], X[:, bass.ds(b, 1), :].rearrange("p a b -> p (a b)")).then_inc(xs_ok, 1)

                def keep(b, q, m):
                    hold(pool, xt_ok, b + 1)
                    nc.gpsimd.tensor_copy(XT[:, :, bass.ds(b * P, P)], xc_[:, q, :].rearrange("p (k n) -> p k n", k=KD)).then_inc(xt_kept, 1)

                steps(pool, [(0, stage), (1, keep)], NB)

            @block.vector
            def _(dve):
                n = [0]

                def link(ins):
                    n[0] += 1
                    ins.then_inc(dchain, 1)
                    dve.wait_ge(dchain, n[0])

                nc.vector.memset(X[:, NB - 1, :], 0.0).then_inc(x_zero, 1)
                nc.vector.memset(zero[:, :], 0.0).then_inc(fill_ok, 1)
                nc.vector.memset(fill[:, 0:1], 0).then_inc(fill_ok, 1)
                nc.vector.memset(fill[:, 1:2], NP - 1).then_inc(fill_ok, 1)
                nc.vector.memset(dots[:, :, :], 0.0).then_inc(dz_ok, 1)
                dve.wait_ge(e_in, 16)
                nc.vector.tensor_scalar(re[:, 0, :], re[:, 0, :], float(N - 1), None, ALU.min).then_inc(e_ok, 1)
                nc.vector.tensor_scalar(re[:, 1, :], re[:, 1, :], float(NP - 1), None, ALU.min).then_inc(e_ok, 1)
                for c in range(NC):
                    xc = X[:, c * C:(c + 1) * C, :]
                    dve.wait_ge(x_in[c], 16 if c < NC - 1 else 32)
                    link(nc.vector.tensor_reduce(lnm[:, c, :], xc, AX, ALU.add))
                    link(nc.vector.tensor_scalar(lnm[:, c, :], lnm[:, c, :], 1.0 / D, None, ALU.mult))
                    link(nc.vector.tensor_tensor(xc, xc, lnm[:, c, :].unsqueeze(2).to_broadcast([P, C, D]), ALU.subtract))
                    link(nc.vector.tensor_tensor(sq[:, :, :], xc, xc, ALU.mult))
                    link(nc.vector.tensor_reduce(lnv[:, c, :], sq[:, :, :], AX, ALU.add))
                    nc.vector.tensor_scalar(lnv[:, c, :], lnv[:, c, :], 1.0 / D, LN_EPS, ALU.mult, ALU.add).then_inc(ln_var_ok, 1)
                    dve.wait_ge(ln_std_ok, c + 1)
                    link(nc.vector.reciprocal(lns[:, c, :], lns[:, c, :]))
                    nc.vector.tensor_tensor(xc, xc, lns[:, c, :].unsqueeze(2).to_broadcast([P, C, D]), ALU.mult).then_inc(ln_ok, C)
                dve.wait_ge(wt_used, 4)
                wh = wkv[:, :, :].rearrange("p k (h e) -> p (k h) e", e=DH)
                wm = wkm[:, :, :].rearrange("p k h -> p (k h)")
                link(nc.vector.tensor_reduce(wm, wh, AX, ALU.add))
                link(nc.vector.tensor_scalar(wm, wm, 1.0 / DH, None, ALU.mult))
                nc.vector.tensor_tensor(wh, wh, wm.unsqueeze(2).to_broadcast([P, KD * 2 * HM, DH]), ALU.subtract).then_inc(wkv_ok, 1)

                def variances(b, q, m):
                    hold(dve, kvsq_ok, b + 1)
                    nc.vector.tensor_reduce(kss[:, q, :], kvsq[:, q, :].rearrange("p (h e) -> p h e", e=DH), AX, ALU.add).then_inc(kss_ok, 1)
                    hold(dve, kss_ok, b + 1)
                    link2(nc.vector.tensor_scalar(kss[:, q, :], kss[:, q, :], 1.0 / DH, LN_EPS, ALU.mult, ALU.add), b)
                    nc.vector.tensor_tensor(kpr[:, q, :], kss[:, q, 0:HM], kss[:, q, HM:2 * HM], ALU.mult).then_inc(kpr_ok, 1)

                def link2(ins, b):
                    ins.then_inc(kve_ok, 1)
                    hold(dve, kve_ok, b + 1)

                def scale_k(b, q, m):
                    hold(dve, kst_ok, b + 1)
                    nc.vector.reciprocal(kri[:, q, :], kst[:, q, :]).then_inc(kri_ok, 1)
                    hold(dve, kri_ok, b + 1)
                    if after(b, 2):
                        hold(dve, dots_ok, b - 1)
                    nc.vector.tensor_tensor(ks[:, q, :].rearrange("p (h e) -> p h e", e=DH),
                                            pkv[:, q, 0:INNER].rearrange("p (h e) -> p h e", e=DH),
                                            kri[:, q, :].unsqueeze(2).to_broadcast([P, HM, DH]), ALU.mult).then_inc(ks_ok, 1)

                steps(dve, [(0, variances), (1, scale_k)], NB)
                dve.wait_ge(dots_ok, NB)
                dve.wait_ge(dz_ok, 1)
                nc.vector.tensor_scalar(dots[0:DH, :, 0:DH], pd[0:DH, :, 0:DH], 1.0 / N, None, ALU.mult).then_inc(dd_ok, 1)
                nc.vector.tensor_scalar(dots[DH:P, :, DH:P], pd[DH:P, :, DH:P], 1.0 / N, None, ALU.mult).then_inc(dd_ok, 1)

            @block.scalar
            def _(act):
                loads = [(wkv_n[:, :, :], w_qkv[INNER:3 * INNER, :].rearrange("(j p) d -> p j d", p=P)),
                         (wq[:, :, :], w_qkv[0:INNER, :].rearrange("(j p) d -> p j d", p=P)),
                         (wo_n[:, :, :], w_out.rearrange("(j p) d -> p j d", p=P)),
                         (wg[:, :, :], gnn_w.rearrange("(j p) d -> p j d", p=P)),
                         (wgat[:, :, :], w_gat.rearrange("(j p) d -> p j d", p=P)),
                         (bg[:, :], gnn_b.partition_broadcast(P)), (bo[:, :], b_out.partition_broadcast(P)),
                         (att[:, 0, :], att_src.rearrange("a b -> (a b)").partition_broadcast(P)),
                         (att[:, 1, :], att_dst.rearrange("a b -> (a b)").partition_broadcast(P)),
                         (gb[:, 0, :], b_gat.partition_broadcast(P)), (gb[:, 1, :], ln_g.partition_broadcast(P)),
                         (gb[:, 2, :], ln_b.partition_broadcast(P))]
                for to, fr in loads:
                    act.dma_start(to, fr).then_inc(w_in, 16)
                act.wait_ge(w_in, 16 * len(loads))
                for g in range(4):
                    act.wait_ge(wt_ok, g + 1)
                    nc.scalar.copy(wkv[:, g // 2, (g % 2) * 512:(g % 2 + 1) * 512], pt[:, g % 2, :]).then_inc(wt_used, 1)
                for g in range(2):
                    act.wait_ge(wt_ok, 5 + g)
                    nc.scalar.copy(wo[:, 2 * g:2 * g + 2, :].rearrange("p a b -> p (a b)"), pt[:, g % 2, :]).then_inc(wt_used, 1)
                for c in range(NC):
                    act.wait_ge(ln_var_ok, c + 1)
                    nc.scalar.activation(lns[:, c, :], lnv[:, c, :], ACT.Sqrt).then_inc(ln_std_ok, 1)

                def columns(b, q, m):
                    hold(act, xt_ps, b + 1)
                    if after(b, 2):
                        hold(act, kv_ok, b - 1)
                        hold(act, xt_kept, b - 1)
                    nc.scalar.copy(xc_[:, q, :], pt[:, q, 0:KD * P]).then_inc(xt_ok, 1)

                def squares(b, q, m):
                    hold(act, kv_ok, b + 1)
                    if after(b, 2):
                        hold(act, kss_ok, b - 1)
                    nc.scalar.activation(kvsq[:, q, :], pkv[:, q, :], ACT.Square).then_inc(kvsq_ok, 1)
                    if after(b, 2):
                        hold(act, dots_ok, b - 1)
                    nc.scalar.copy(vs[:, q, :], pkv[:, q, INNER:2 * INNER]).then_inc(v_ok, 1)

                def roots(b, q, m):
                    hold(act, kpr_ok, b + 1)
                    nc.scalar.activation(kst[:, q, :], kpr[:, q, :], ACT.Sqrt).then_inc(kst_ok, 1)

                steps(act, [(0, columns), (1, squares), (1, roots)], NB)
                act.wait_ge(bt_ps, 1)
                nc.scalar.copy(bt[:, :, :].rearrange("p a b -> p (a b)"), pkv[:, 0, :]).then_inc(bt_ok, 1)
                act.wait_ge(mix_ps, 1)
                nc.scalar.copy(mix[:, :, :].rearrange("p a b -> p (a b)"), pt[:, 0, :]).then_inc(mix_ok, 1)
                act.wait_ge(mix_ok, 1)

            @block.tensor
            def _(pe):
                pe.wait_ge(consts, 2)
                pe.wait_ge(w_in, 16 * 12)
                for g in range(4):
                    if g >= 2:
                        pe.wait_ge(wt_used, g - 1)
                    for j in range(4):
                        mm = nc.tensor.transpose(pt[:, g % 2, j * P:(j + 1) * P],
                                                 wkv_n[:, (g % 2) * 4 + j, (g // 2) * P:(g // 2 + 1) * P], ident[:, :])
                    mm.then_inc(wt_ok, 1)
                for g in range(2):
                    pe.wait_ge(wt_used, g + 3)
                    for j in range(4):
                        mm = nc.tensor.transpose(pt[:, g % 2, j * P:(j + 1) * P],
                                                 wo_n[:, j % 2, (2 * g + j // 2) * P:(2 * g + j // 2 + 1) * P], ident[:, :])
                    mm.then_inc(wt_ok, 1)
                pe.wait_ge(wt_used, 6)

                def turn(b, q, m):
                    hold(pe, xs_ok, b + 1)
                    if after(b, 2):
                        hold(pe, xt_ok, b - 1)
                    for k in range(KD):
                        mm = nc.tensor.transpose(pt[:, q, k * P:(k + 1) * P], xs[:, q, k * P:(k + 1) * P], ident[:, :])
                    mm.then_inc(xt_ps, 1)

                pe.wait_ge(wkv_ok, 1)
                pe.wait_ge(fill_ok, 3)
                nc.tensor.matmul(pd[:, :, :].rearrange("p a b -> p (a b)"), zero[:, 0:P], wkv[:, 0, 0:512], start=True, stop=True, skip_group_check=True)

                def kv(b, q, m):
                    hold(pe, xt_ok, b + 1)
                    if after(b, 2):
                        hold(pe, v_ok, b - 1)
                        hold(pe, ks_ok, b - 1)
                    for half in range(2):
                        for k in range(KD):
                            mm = nc.tensor.matmul(pkv[:, q, half * INNER:(half + 1) * INNER], xc_[:, q, k * P:(k + 1) * P],
                                                  wkv[:, k, half * INNER:(half + 1) * INNER], start=k == 0, stop=k == KD - 1)
                    mm.then_inc(kv_ok, 1)

                def product(b, q, m):
                    hold(pe, ks_ok, b + 1)
                    hold(pe, v_ok, b + 1)
                    for h in range(4):
                        mm = nc.tensor.matmul(pd[:, h, :], ks[:, q, h * P:(h + 1) * P], vs[:, q, h * P:(h + 1) * P],
                                              start=False, stop=True, skip_group_check=True)
                    mm.then_inc(dots_ok, 1)

                steps(pe, [(0, turn), (1, kv), (3, product)], NB)
                pe.wait_ge(dd_ok, 2)
                for h in range(4):
                    mm = nc.tensor.matmul(pkv[:, 0, h * D:(h + 1) * D], dots[:, h, :], wq[:, h, :], start=True, stop=True)
                mm.then_inc(bt_ps, 1)
                pe.wait_ge(bt_ok, 1)
                for m in range(KD):
                    for h in range(4):
                        mm = nc.tensor.matmul(pt[:, 0, m * D:(m + 1) * D], bt[:, h, m * P:(m + 1) * P], wo[:, h, :], start=h == 0, stop=h == 3)
                mm.then_inc(mix_ps, 1)


        BIG = 1.0e6
        LOW = -1.0e30

        def edge_pass(kind):
            table, tw = (XN, D) if kind == "sum" else (TAB, PAY)
            acc, aw = {"sum": (ACC, D + 1), "max": (MAXT, GH), "soft": (AGG, PAY)}[kind]
            esrc, edst, tiles = (SRC, DST, ET) if kind == "sum" else (RSRC, RDST, RT)
            gw = D + 1 if kind == "sum" else PAY
            with ExitStack() as st:
                si = sb(st, f"{kind}_src", [P, 1], I32)
                di = sb(st, f"{kind}_dst", [P, 1], I32)
                db = sb(st, f"{kind}_dst_row", [P, P], I32)
                ui = sb(st, f"{kind}_rows_out", [P, 1], I32)
                df = sb(st, f"{kind}_dst_f", [P, 1])
                dbf = sb(st, f"{kind}_dst_row_f", [P, P])
                same = sb(st, f"{kind}_same", [P, P])
                before = sb(st, f"{kind}_before", [P, P])
                cnt = sb(st, f"{kind}_count", [P, 2])
                got = sb(st, f"{kind}_gathered", [P, gw])
                old = sb(st, f"{kind}_old", [P, aw])
                new = sb(st, f"{kind}_new", [P, aw])
                shift = sb(st, f"{kind}_shift", [P, 2 * GH])
                pay = sb(st, f"{kind}_payload", [P, PAY])
                wts = sb(st, f"{kind}_scores", [P, 2, GH])
                spread = sb(st, f"{kind}_spread", [P, GH, P])
                low = sb(st, f"{kind}_low", [P, GH])
                psum = ps(st, f"{kind}_ps", [P, 512])
                names = ["init", "ready", "idx", "gat", "oldr", "shr", "chain", "same_ok", "rows_ok", "pay_ok", "exp_in", "exp_ok", "mm_ok", "new_ok", "scat"]
                s = {k: sem(f"{kind}_{k}") for k in names}
                block = st.enter_context(nc.Block())

                @block.sync
                def _(sp):
                    sp.wait_ge(s["ready"], 1)
                    fill = (low if kind == "max" else zero)[:, 0:aw]
                    sp.dma_start(by_block(acc), fill.unsqueeze(1).to_broadcast([P, NB, aw])).then_inc(s["init"], 16)

                    def load(t):
                        sp.dma_start(si[:, :], esrc[bass.ds(t * P, P), :]).then_inc(s["idx"], 16)
                        sp.dma_start(di[:, :], edst[bass.ds(t * P, P), :]).then_inc(s["idx"], 16)
                        sp.dma_start(db[:, :], edst[bass.ds(t * P, P), :].rearrange("a b -> (a b)").partition_broadcast(P)).then_inc(s["idx"], 16)

                    load(0)
                    with sp.Fori(1, tiles) as t:
                        hold(sp, s["scat"], t * 16)
                        load(t)
                    sp.wait_ge(s["init"], 16)
                    sp.wait_ge(s["scat"], 16 * tiles)

                @block.gpsimd
                def _(pool):
                    pool.wait_ge(s["init"], 16)
                    with pool.Fori(0, tiles) as t:
                        hold(pool, s["idx"], t * 48 + 48)
                        nc.gpsimd.indirect_dma_start(got[:, 0:tw], None, table, bass.IndirectOffsetOnAxis(ap=si[:, 0:1], axis=0)).then_inc(s["gat"], 16)
                        nc.gpsimd.indirect_dma_start(old[:, :], None, acc, bass.IndirectOffsetOnAxis(ap=di[:, 0:1], axis=0)).then_inc(s["oldr"], 16)
                        if kind == "soft":
                            nc.gpsimd.indirect_dma_start(shift[:, :], None, MD, bass.IndirectOffsetOnAxis(ap=di[:, 0:1], axis=0)).then_inc(s["shr"], 16)
                        hold(pool, s["new_ok"], t + 1)
                        nc.gpsimd.indirect_dma_start(acc, bass.IndirectOffsetOnAxis(ap=ui[:, 0:1], axis=0), new[:, :], None,
                                                     bounds_check=NP - 1, oob_is_err=False).then_inc(s["scat"], 16)

                @block.vector
                def _(dve):
                    nc.vector.memset(low[:, :], LOW)
                    nc.vector.memset(got[:, gw - 1:gw], 1.0)
                    dve.drain().then_inc(s["ready"], 1)
                    dve.wait_ge(s["ready"], 1)
                    L = {"sum": 5, "max": 7, "soft": 10}[kind]
                    with dve.Fori(0, tiles) as t:
                        k = [0]

                        def link(ins):
                            k[0] += 1
                            ins.then_inc(s["chain"], 1)
                            hold(dve, s["chain"], t * L + k[0])

                        hold(dve, s["idx"], t * 48 + 48)
                        link(nc.vector.tensor_copy(df[:, :], di[:, :]))
                        link(nc.vector.tensor_copy(dbf[:, :], db[:, :]))
                        nc.vector.tensor_scalar(same[:, :], dbf[:, :], df[:, 0:1], None, ALU.is_equal).then_inc(s["same_ok"], 1)
                        hold(dve, s["same_ok"], t + 1)
                        link(nc.vector.tensor_tensor(before[:, :], same[:, :], lower[:, :], ALU.mult))
                        link(nc.vector.tensor_reduce(cnt[:, 0:1], before[:, :], AX, ALU.max))
                        link(nc.vector.tensor_scalar(cnt[:, 1:2], cnt[:, 0:1], BIG, df[:, 0:1], ALU.mult, ALU.add))
                        nc.vector.tensor_copy(ui[:, :], cnt[:, 1:2]).then_inc(s["rows_ok"], 1)
                        hold(dve, s["gat"], t * 16 + 16)
                        if kind == "max":
                            link(nc.vector.tensor_scalar(before[:, :], same[:, :], -1.0, -LOW, ALU.add, ALU.mult))
                            hold(dve, s["mm_ok"], t + 1)
                            link(nc.vector.tensor_tensor(spread[:, :, :], psum[:, :].rearrange("p (h e) -> p h e", h=GH),
                                                         before[:, :].unsqueeze(1).to_broadcast([P, GH, P]), ALU.add))
                            nc.vector.tensor_reduce(new[:, :], spread[:, :, :], AX, ALU.max).then_inc(s["pay_ok"], 1)
                            hold(dve, s["pay_ok"], t + 1)
                            hold(dve, s["oldr"], t * 16 + 16)
                            hold(dve, s["rows_ok"], t + 1)
                            nc.vector.tensor_tensor(new[:, :], new[:, :], old[:, :], ALU.max).then_inc(s["new_ok"], 1)
                        else:
                            if kind == "soft":
                                hold(dve, s["shr"], t * 16 + 16)
                                link(nc.vector.tensor_tensor(wts[:, 0, :], got[:, GW:PAY], shift[:, 0:GH], ALU.add))
                                link(nc.vector.tensor_scalar(wts[:, 1, :], wts[:, 0, :], SLOPE, None, ALU.mult))
                                link(nc.vector.tensor_tensor(wts[:, 0, :], wts[:, 0, :], wts[:, 1, :], ALU.max))
                                link(nc.vector.tensor_tensor(wts[:, 1, :], wts[:, 0, :], shift[:, GH:2 * GH], ALU.subtract))
                                dve.sem_inc(s["exp_in"], 1)
                                hold(dve, s["exp_ok"], t + 1)
                                link(nc.vector.tensor_tensor(pay[:, 0:GW].rearrange("p (h e) -> p h e", h=GH), got[:, 0:GW].rearrange("p (h e) -> p h e", h=GH),
                                                             pay[:, GW:PAY].unsqueeze(2).to_broadcast([P, GH, NE]), ALU.mult))
                                dve.sem_inc(s["pay_ok"], 1)
                            hold(dve, s["mm_ok"], t + 1)
                            hold(dve, s["oldr"], t * 16 + 16)
                            hold(dve, s["rows_ok"], t + 1)
                            nc.vector.tensor_tensor(new[:, :], psum[:, 0:aw], old[:, :], ALU.add).then_inc(s["new_ok"], 1)
                        assert k[0] == L

                @block.scalar
                def _(act):
                    if kind == "soft":
                        with act.Fori(0, tiles) as t:
                            hold(act, s["exp_in"], t + 1)
                            nc.scalar.activation(pay[:, GW:PAY], wts[:, 1, :], ACT.Exp).then_inc(s["exp_ok"], 1)

                @block.tensor
                def _(pe):
                    pe.wait_ge(s["ready"], 1)
                    with pe.Fori(0, tiles) as t:
                        hold(pe, s["same_ok"], t + 1)
                        hold(pe, s["gat"], t * 16 + 16)
                        if kind == "max":
                            for h in range(GH):
                                mm = nc.tensor.matmul(psum[:, h * P:(h + 1) * P], got[:, GW + h:GW + h + 1].to_broadcast([P, P]), ident[:, :], start=True, stop=True)
                        elif kind == "sum":
                            mm = nc.tensor.matmul(psum[:, 0:aw], same[:, :], got[:, :], start=True, stop=True)
                        else:
                            hold(pe, s["pay_ok"], t + 1)
                            mm = nc.tensor.matmul(psum[:, 0:aw], same[:, :], pay[:, :], start=True, stop=True)
                        mm.then_inc(s["mm_ok"], 1)

        edge_pass("sum")

        with ExitStack() as st:
            nm = sb(st, "neigh_rows", [P, 2, D + 1])
            xr = sb(st, "x_again", [P, 2, D])
            nt = sb(st, "neigh_cols", [P, 2, KD * P])
            r1 = sb(st, "gnn_rows", [P, 2, D])
            r2 = sb(st, "gnn_squares", [P, 2, D])
            u1 = sb(st, "mix_rows", [P, 2, D])
            nr = sb(st, "norms", [P, 2, 6])
            bs = sb(st, "ln_stats", [P, 2, 6])
            mv = sb(st, "ln_mean_var", [P, 2, 2])
            xn = sb(st, "x1_normed", [P, 2, D])
            xts = sb(st, "x_cols_stage2", [P, 2, KD * P])
            xt1 = sb(st, "x1_cols_stage", [P, 2, KD * P])
            ta = sb(st, "att_products", [P, NB, GW])
            pt = ps(st, "ps_turn", [P, 2, 512])
            pg = ps(st, "ps_node", [P, 2, 512])
            p1 = ps(st, "ps_turn_x1", [P, 2, 512])
            ph = ps(st, "ps_router", [P, 2, 512])
            nin = [sem("node_in0"), sem("node_in1")]
            names = ["mean", "nt_ps", "nt_ok", "g_ok", "r_ok", "u_ok", "ss", "nrm", "x1", "vps", "std", "xn", "xt_ps",
                     "xt_ok", "h_ps", "h_ok", "cA", "cB", "cC", "cD", "cE", "xts", "kept"]
            s = {k: sem(f"node_{k}") for k in names}
            block = st.enter_context(nc.Block())

            @block.sync
            def _(sp):
                def load(b, q, m):
                    if after(b, 2):
                        hold(sp, s["nt_ps"], b - 1)
                        hold(sp, s["u_ok"], b - 1)
                    sp.dma_start(nm[:, q, :], ACC[bass.ds(b * P, P), :]).then_inc(nin[q], 16)
                    sp.dma_start(xr[:, q, :], XP[bass.ds(b * P, P), :]).then_inc(nin[q], 16)

                steps(sp, [(0, load)], NB)

            @block.gpsimd
            def _(pool):
                def stage(b, q, m):
                    if after(b, 2):
                        hold(pool, s["g_ok"], b - 1)
                    nc.gpsimd.tensor_copy(xts[:, q, :].rearrange("p (k n) -> p k n", k=KD), XT[:, :, bass.ds(b * P, P)]).then_inc(s["xts"], 1)

                def keep(b, q, m):
                    hold(pool, s["xt_ok"], b + 1)
                    hold(pool, s["xts"], b + 1)
                    nc.gpsimd.tensor_copy(XT[:, :, bass.ds(b * P, P)], xt1[:, q, :].rearrange("p (k n) -> p k n", k=KD)).then_inc(s["kept"], 1)

                steps(pool, [(0, stage), (4, keep)], NB)

            @block.tensor
            def _(pe):
                def turn(b, q, m):
                    hold(pe, s["mean"], b + 1)
                    if after(b, 2):
                        hold(pe, s["nt_ok"], b - 1)
                    for k in range(KD):
                        mm = nc.tensor.transpose(pt[:, q, k * P:(k + 1) * P], nm[:, q, k * P:(k + 1) * P], ident[:, :])
                    mm.then_inc(s["nt_ps"], 1)

                def node(b, q, m):
                    hold(pe, s["nt_ok"], b + 1)
                    hold(pe, s["xts"], b + 1)
                    if after(b, 2):
                        hold(pe, s["u_ok"], b - 1)
                    for k in range(KD):
                        nc.tensor.matmul(pg[:, q, 0:D], xts[:, q, k * P:(k + 1) * P], wg[:, k, :], start=k == 0, stop=False)
                    for k in range(KD):
                        nc.tensor.matmul(pg[:, q, 0:D], nt[:, q, k * P:(k + 1) * P], wg[:, KD + k, :], start=False, stop=k == KD - 1)
                    for k in range(KD):
                        mm = nc.tensor.matmul(pg[:, q, D:2 * D], xts[:, q, k * P:(k + 1) * P], mix[:, k, :], start=k == 0, stop=k == KD - 1)
                    mm.then_inc(s["g_ok"], 1)

                def turn_x1(b, q, m):
                    hold(pe, s["xn"], b + 1)
                    if after(b, 2):
                        hold(pe, s["xt_ok"], b - 1)
                    for k in range(KD):
                        mm = nc.tensor.transpose(p1[:, q, k * P:(k + 1) * P], xn[:, q, k * P:(k + 1) * P], ident[:, :])
                    mm.then_inc(s["xt_ps"], 1)

                def router(b, q, m):
                    hold(pe, s["xt_ok"], b + 1)
                    if after(b, 2):
                        hold(pe, s["h_ok"], b - 1)
                    for k in range(KD):
                        mm = nc.tensor.matmul(ph[:, q, 0:GW], xt1[:, q, k * P:(k + 1) * P], wgat[:, k, :], start=k == 0, stop=k == KD - 1)
                    mm.then_inc(s["h_ps"], 1)

                steps(pe, [(0, turn), (1, node), (3, turn_x1), (4, router)], NB)

            @block.scalar
            def _(act):
                def columns(b, q, m):
                    hold(act, s["nt_ps"], b + 1)
                    if after(b, 2):
                        hold(act, s["g_ok"], b - 1)
                    nc.scalar.copy(nt[:, q, :], pt[:, q, 0:KD * P]).then_inc(s["nt_ok"], 1)

                def norms(b, q, m):
                    hold(act, s["r_ok"], b + 1)
                    nc.scalar.activation(r2[:, q, :], r1[:, q, :], ACT.Square, accum_out=nr[:, q, 0:1]).then_inc(s["ss"], 1)
                    hold(act, s["ss"], b + 1)
                    nc.scalar.activation(nr[:, q, 1:2], nr[:, q, 0:1], ACT.Sqrt).then_inc(s["nrm"], 1)

                def stds(b, q, m):
                    hold(act, s["vps"], b + 1)
                    nc.scalar.activation(nr[:, q, 4:5], nr[:, q, 5:6], ACT.Sqrt).then_inc(s["std"], 1)

                def columns_x1(b, q, m):
                    hold(act, s["xt_ps"], b + 1)
                    if after(b, 2):
                        hold(act, s["h_ps"], b - 1)
                        hold(act, s["kept"], b - 1)
                    nc.scalar.copy(xt1[:, q, :], p1[:, q, 0:KD * P]).then_inc(s["xt_ok"], 1)

                steps(act, [(0, columns), (1, norms), (2, stds), (3, columns_x1)], NB)

            @block.vector
            def _(dve):
                def mean(b, q, m):
                    hold(dve, nin[q], m * 32 + 32)
                    link = chain(dve, s["cA"], b, 2)
                    link(nc.vector.tensor_scalar(nm[:, q, D:D + 1], nm[:, q, D:D + 1], 1.0, None, ALU.max))
                    link(nc.vector.reciprocal(nm[:, q, D:D + 1], nm[:, q, D:D + 1]))
                    nc.vector.tensor_scalar(nm[:, q, 0:D], nm[:, q, 0:D], nm[:, q, D:D + 1], None, ALU.mult).then_inc(s["mean"], 1)

                def rows(b, q, m):
                    hold(dve, s["g_ok"], b + 1)
                    if after(b, 2):
                        hold(dve, s["ss"], b - 1)
                        hold(dve, s["x1"], b - 1)
                    link = chain(dve, s["cB"], b, 2)
                    link(nc.vector.tensor_tensor(r1[:, q, :], pg[:, q, 0:D], bg[:, :], ALU.add))
                    nc.vector.tensor_scalar(r1[:, q, :], r1[:, q, :], 0.0, None, ALU.max).then_inc(s["r_ok"], 1)
                    link(nc.vector.tensor_tensor(u1[:, q, :], pg[:, q, D:2 * D], xr[:, q, :], ALU.add))
                    nc.vector.tensor_tensor(u1[:, q, :], u1[:, q, :], bo[:, :], ALU.add).then_inc(s["u_ok"], 1)

                def update(b, q, m):
                    hold(dve, s["nrm"], b + 1)
                    hold(dve, s["u_ok"], b + 1)
                    link = chain(dve, s["cC"], b, 4)
                    link(nc.vector.tensor_scalar(nr[:, q, 2:3], nr[:, q, 1:2], GNN_EPS, None, ALU.max))
                    link(nc.vector.reciprocal(nr[:, q, 3:4], nr[:, q, 2:3]))
                    x1 = X[:, bass.ds(b, 1), :].rearrange("p a b -> p (a b)")
                    nc.vector.scalar_tensor_tensor(out=x1, in0=r1[:, q, :], scalar=nr[:, q, 3:4], in1=u1[:, q, :], op0=ALU.mult, op1=ALU.add).then_inc(s["x1"], 1)
                    hold(dve, s["x1"], b + 1)
                    link(nc.vector.bn_stats(bs[:, q, :], x1))
                    link(nc.vector.bn_aggr(mv[:, q, :], bs[:, q, :]))
                    nc.vector.tensor_scalar(nr[:, q, 5:6], mv[:, q, 1:2], LN_EPS, None, ALU.add).then_inc(s["vps"], 1)

                def norm(b, q, m):
                    hold(dve, s["std"], b + 1)
                    if after(b, 2):
                        hold(dve, s["xt_ps"], b - 1)
                    link = chain(dve, s["cD"], b, 1)
                    link(nc.vector.reciprocal(nr[:, q, 4:5], nr[:, q, 4:5]))
                    x1 = X[:, bass.ds(b, 1), :].rearrange("p a b -> p (a b)")
                    nc.vector.tensor_scalar(xn[:, q, :], x1, mv[:, q, 0:1], nr[:, q, 4:5], ALU.subtract, ALU.mult).then_inc(s["xn"], 1)

                def router(b, q, m):
                    hold(dve, s["h_ps"], b + 1)
                    nc.vector.tensor_copy(T[:, bass.ds(b, 1), 0:GW].rearrange("p a b -> p (a b)"), ph[:, q, 0:GW]).then_inc(s["h_ok"], 1)

                steps(dve, [(0, mean), (1, rows), (2, update), (3, norm), (4, router)], NB)
                dve.wait_ge(s["h_ok"], NB)
                n = 0
                for k, to in ((0, T[:, :, GW:PAY]), (1, AD[:, :, :])):
                    nc.vector.tensor_tensor(ta[:, :, :], T[:, :, 0:GW], att[:, k, :].unsqueeze(1).to_broadcast([P, NB, GW]), ALU.mult).then_inc(s["cE"], 1)
                    n += 1
                    dve.wait_ge(s["cE"], n)
                    nc.vector.tensor_reduce(to, ta[:, :, :].rearrange("p b (h e) -> p b h e", e=NE), AX, ALU.add).then_inc(s["cE"], 1)
                    n += 1
                    dve.wait_ge(s["cE"], n)

        with ExitStack() as st:
            out_ok = sem("table_out")
            block = st.enter_context(nc.Block())

            @block.sync
            def _(sp):
                sp.dma_start(by_block(TAB), T[:, :, :]).then_inc(out_ok, 16)
                sp.wait_ge(out_ok, 16)

        edge_pass("max")

        with ExitStack() as st:
            ms = sb(st, "score_max", [P, NB, 2 * GH])
            m2 = sb(st, "score_slope", [P, NB, GH])
            m_in, m_ch, m_out = sem("shift_in"), sem("shift_chain"), sem("shift_out")
            block = st.enter_context(nc.Block())

            @block.sync
            def _(sp):
                sp.dma_start(MXS[:, :, :], by_block(MAXT)).then_inc(m_in, 16)
                sp.wait_ge(m_ch, 6)
                sp.dma_start(by_block(MD), ms[:, :, :]).then_inc(m_out, 16)
                sp.wait_ge(m_out, 16)

            @block.vector
            def _(dve):
                dve.wait_ge(m_in, 16)
                link = chain(dve, m_ch, 0, 6)
                link(nc.vector.tensor_tensor(MXS[:, :, :], MXS[:, :, :], T[:, :, GW:PAY], ALU.max))
                link(nc.vector.tensor_tensor(MXS[:, :, :], MXS[:, :, :], AD[:, :, :], ALU.add))
                link(nc.vector.tensor_scalar(m2[:, :, :], MXS[:, :, :], SLOPE, None, ALU.mult))
                link(nc.vector.tensor_tensor(MXS[:, :, :], MXS[:, :, :], m2[:, :, :], ALU.max))
                link(nc.vector.tensor_copy(ms[:, :, 0:GH], AD[:, :, :]))
                link(nc.vector.tensor_copy(ms[:, :, GH:2 * GH], MXS[:, :, :]))

        edge_pass("soft")

        with ExitStack() as st:
            ag = sb(st, "attention", [P, NB, PAY])
            z = sb(st, "own_score", [P, NB, 2, GH])
            y = sb(st, "router_out", [P, NB, GW])
            y2 = sb(st, "router_sq", [P, NB, GW])
            v = sb(st, "router_stats", [P, 4, NB])
            sc = sb(st, "expert_scores", [P, NB, NE])
            rk = sb(st, "expert_ranks", [P, NB, NE])
            cm = sb(st, "expert_compare", [P, NB, NE])
            g_in, g_ch, e1, e2, q1 = sem("gate_in"), sem("gate_chain"), sem("gate_exp1"), sem("gate_exp2"), sem("gate_sqrt")
            a1, a2, a3 = sem("gate_at_exp1"), sem("gate_at_exp2"), sem("gate_at_sqrt")
            block = st.enter_context(nc.Block())

            @block.sync
            def _(sp):
                sp.dma_start(ag[:, :, :], by_block(AGG)).then_inc(g_in, 16)

            @block.scalar
            def _(act):
                act.wait_ge(a1, 1)
                nc.scalar.activation(z[:, :, 0, :], z[:, :, 1, :], ACT.Exp).then_inc(e1, 1)
                act.wait_ge(a3, 1)
                nc.scalar.activation(v[:, 3, :], v[:, 2, :], ACT.Sqrt).then_inc(q1, 1)
                act.wait_ge(a2, 1)
                nc.scalar.activation(sc[:, :, :], cm[:, :, :], ACT.Exp).then_inc(e2, 1)

            @block.vector
            def _(dve):
                link = chain(dve, g_ch, 0, None)
                TT, TS = nc.vector.tensor_tensor, nc.vector.tensor_scalar
                heads = lambda t: t.rearrange("p b (h e) -> p b h e", e=NE)
                wide = lambda t, n: t.unsqueeze(len(t.shape)).to_broadcast([*t.shape, n])
                link(TT(z[:, :, 0, :], T[:, :, GW:PAY], AD[:, :, :], ALU.add))
                link(TS(z[:, :, 1, :], z[:, :, 0, :], SLOPE, None, ALU.mult))
                link(TT(z[:, :, 0, :], z[:, :, 0, :], z[:, :, 1, :], ALU.max))
                TT(z[:, :, 1, :], z[:, :, 0, :], MXS[:, :, :], ALU.subtract).then_inc(a1, 1)
                dve.wait_ge(e1, 1)
                dve.wait_ge(g_in, 16)
                link(TT(heads(y[:, :, :]), heads(T[:, :, 0:GW]), wide(z[:, :, 0, :], NE), ALU.mult))
                link(TT(y[:, :, :], y[:, :, :], ag[:, :, 0:GW], ALU.add))
                link(TT(z[:, :, 1, :], z[:, :, 0, :], ag[:, :, GW:PAY], ALU.add))
                link(TS(z[:, :, 1, :], z[:, :, 1, :], DEN_EPS, None, ALU.add))
                link(nc.vector.reciprocal(z[:, :, 0, :], z[:, :, 1, :]))
                link(TT(heads(y[:, :, :]), heads(y[:, :, :]), wide(z[:, :, 0, :], NE), ALU.mult))
                row = lambda k: gb[:, k, :].unsqueeze(1).to_broadcast([P, NB, GW])
                link(TT(y[:, :, :], y[:, :, :], row(0), ALU.add))
                link(nc.vector.tensor_reduce(v[:, 0, :], y[:, :, :], AX, ALU.add))
                link(TS(v[:, 1, :], v[:, 0, :], 1.0 / GW, None, ALU.mult))
                link(TT(y[:, :, :], y[:, :, :], wide(v[:, 1, :], GW), ALU.subtract))
                link(TT(y2[:, :, :], y[:, :, :], y[:, :, :], ALU.mult))
                link(nc.vector.tensor_reduce(v[:, 0, :], y2[:, :, :], AX, ALU.add))
                TS(v[:, 2, :], v[:, 0, :], 1.0 / GW, LN_EPS, ALU.mult, ALU.add).then_inc(a3, 1)
                dve.wait_ge(q1, 1)
                link(nc.vector.reciprocal(v[:, 0, :], v[:, 3, :]))
                link(TT(y[:, :, :], y[:, :, :], wide(v[:, 0, :], GW), ALU.mult))
                link(TT(y[:, :, :], y[:, :, :], row(1), ALU.mult))
                link(TT(y[:, :, :], y[:, :, :], row(2), ALU.add))
                link(nc.vector.tensor_reduce(sc[:, :, :], y[:, :, :].rearrange("p b (h e) -> p b e h", e=NE), AX, ALU.add))
                link(TS(sc[:, :, :], sc[:, :, :], 1.0 / GH, None, ALU.mult))
                link(nc.vector.memset(rk[:, :, :], 0.0))
                for j in range(NE):
                    for a, b, op in ((0, j, ALU.is_gt), (j + 1, NE, ALU.is_ge)):
                        if a < b:
                            link(TT(cm[:, :, a:b], sc[:, :, j:j + 1].to_broadcast([P, NB, b - a]), sc[:, :, a:b], op))
                            link(TT(rk[:, :, a:b], rk[:, :, a:b], cm[:, :, a:b], ALU.add))
                link(TS(rk[:, :, :], rk[:, :, :], 1.5, None, ALU.is_lt))
                link(nc.vector.tensor_reduce(v[:, 0, :], sc[:, :, :], AX, ALU.max))
                TT(cm[:, :, :], sc[:, :, :], wide(v[:, 0, :], NE), ALU.subtract).then_inc(a2, 1)
                dve.wait_ge(e2, 1)
                link(TT(gate[:, :, :], sc[:, :, :], rk[:, :, :], ALU.mult))
                link(nc.vector.tensor_reduce(v[:, 1, :], gate[:, :, :], AX, ALU.add))
                link(nc.vector.reciprocal(v[:, 2, :], v[:, 1, :]))
                link(TT(gate[:, :, :], gate[:, :, :], wide(v[:, 2, :], NE), ALU.mult))

        with ExitStack() as st:
            w1s = sb(st, "w1_sb", [P, KD, NE, FF])
            w2s = sb(st, "w2_sb", [P, HT, D])
            b1r = sb(st, "b1_rows", [HT, P])
            b1c = sb(st, "b1_cols", [P, HT])
            b2r = sb(st, "b2_row", [1, NE * D])
            one = sb(st, "ones", [1, P])
            hid = sb(st, "hidden", [P, 2, HT * P])
            phid = ps(st, "ps_hidden", [P, 4, 512])
            py = ps(st, "ps_expert_out", [P, 2, NE * D])
            names = ["b1_ps", "b1_ok", "one", "chain", "hps0", "hps1", "hps2", "hps3", "hid", "y_ps", "y_ok", "hb0", "hb1", "hb2", "hb3"]
            s = {k: sem(f"expert_{k}") for k in names}
            w_in, o_out = sem("expert_w_in"), sem("expert_out")
            block = st.enter_context(nc.Block())

            @block.sync
            def _(sp):
                for e in range(NE):
                    sp.dma_start(w1s[:, :, e, :], w1[e].rearrange("(k p) f -> p k f", p=P)).then_inc(w_in, 16)
                sp.dma_start(w2s[:, :, :], w2.rearrange("e (t p) d -> p (e t) d", p=P)).then_inc(w_in, 16)
                sp.dma_start(b1r[:, :], b1.rearrange("e (t p) -> (e t) p", p=P)).then_inc(w_in, 16)
                sp.dma_start(b2r[0:1, :], b2.rearrange("(a e) d -> a (e d)", a=1)).then_inc(w_in, 16)
                for c in range(NC):
                    sp.wait_ge(s["y_ok"], (c + 1) * C)
                    r0, r1 = c * C * P, min((c + 1) * C * P, N)
                    full = (r1 - r0) // P
                    sp.dma_start(by_block(out[r0:r0 + full * P, :]), X[:, c * C:c * C + full, :]).then_inc(o_out, 16)
                    if full < C:
                        sp.dma_start(out[(NB - 1) * P:N, :], X[0:LAST, NB - 1, :]).then_inc(o_out, 16)
                sp.wait_ge(o_out, 16 * (NC + 1))

            @block.tensor
            def _(pe):
                pe.wait_ge(w_in, 16 * (NE + 3))
                nc.tensor.transpose(py[:, 0, 0:HT], b1r[:, :], ident[0:HT, 0:HT]).then_inc(s["b1_ps"], 1)
                pe.wait_ge(s["b1_ok"], 1)
                pe.wait_ge(s["one"], 1)

                def hidden(b, q, m):
                    for g in range(4):
                        if after(b, 1):
                            hold(pe, s[f"hb{g}"], b)
                        for t in range(4 * g, 4 * g + 4):
                            for k in range(KD):
                                mm = nc.tensor.matmul(phid[:, g, (t % 4) * P:(t % 4 + 1) * P],
                                                      w1s[:, k, t // FT, (t % FT) * P:(t % FT + 1) * P],
                                                      XT[:, k, bass.ds(b * P, P)], start=k == 0, stop=k == KD - 1)
                        mm.then_inc(s[f"hps{g}"], 1)

                def outputs(b, q, m):
                    hold(pe, s["hid"], b * 16 + 16)
                    if after(b, 2):
                        hold(pe, s["y_ok"], b - 1)
                    for e in range(NE):
                        y = py[:, q, e * D:(e + 1) * D]
                        nc.tensor.matmul(y, one[0:1, :], b2r[0:1, e * D:(e + 1) * D], start=True, stop=False)
                        for t in range(FT):
                            mm = nc.tensor.matmul(y, hid[:, q, (e * FT + t) * P:(e * FT + t + 1) * P], w2s[:, e * FT + t, :], start=False, stop=t == FT - 1)
                    mm.then_inc(s["y_ps"], 1)

                steps(pe, [(0, hidden), (1, outputs)], NB)

            @block.scalar
            def _(act):
                act.wait_ge(s["b1_ps"], 1)
                nc.scalar.copy(b1c[:, :], py[:, 0, 0:HT]).then_inc(s["b1_ok"], 1)
                act.wait_ge(s["b1_ok"], 1)

                def gelu(b, q, m):
                    if after(b, 2):
                        hold(act, s["y_ps"], b - 1)
                    for g in range(4):
                        hold(act, s[f"hps{g}"], b + 1)
                        for t in range(4 * g, 4 * g + 4):
                            i = nc.scalar.activation(hid[:, q, t * P:(t + 1) * P], phid[:, g, (t % 4) * P:(t % 4 + 1) * P], ACT.Gelu, bias=b1c[:, t:t + 1])
                            i.then_inc(s["hid"], 1)
                        hold(act, s["hid"], b * 16 + (4 * g + 4))
                        act.sem_inc(s[f"hb{g}"], 1)

                steps(act, [(0, gelu)], NB)

            @block.vector
            def _(dve):
                nc.vector.memset(one[:, :], 1.0).then_inc(s["one"], 1)

                def combine(b, q, m):
                    hold(dve, s["y_ps"], b + 1)
                    link = chain(dve, s["chain"], b, 3)
                    x1 = X[:, bass.ds(b, 1), :].rearrange("p a b -> p (a b)")
                    for e in range(NE):
                        g = gate[:, bass.ds(b, 1), e:e + 1].rearrange("p a b -> p (a b)")
                        i = nc.vector.scalar_tensor_tensor(out=x1, in0=py[:, q, e * D:(e + 1) * D], scalar=g, in1=x1, op0=ALU.mult, op1=ALU.add)
                        if e < NE - 1:
                            link(i)
                        else:
                            i.then_inc(s["y_ok"], 1)

                steps(dve, [(0, combine)], NB)


_INS = ["x", "src", "dst", "L0_gnn_W", "L0_gnn_b", "L0_mix_w_qkv", "L0_mix_w_out", "L0_mix_b_out", "L0_ffn_W_gat",
        "L0_ffn_att_src", "L0_ffn_att_dst", "L0_ffn_b_gat", "L0_ffn_ln_gamma", "L0_ffn_ln_beta", "L0_ffn_W1",
        "L0_ffn_b1", "L0_ffn_W2", "L0_ffn_b2", "L0_ffn_edge_index"]
_OUTS = [((6250, 256), "float32")]


def kernel(**inputs):
    import numpy as _np
    import concourse.bacc as _bacc
    from concourse import mybir as _mybir
    from concourse.bass_utils import run_bass_kernel_spmd as _run

    nc = _bacc.Bacc("TRN2", target_bir_lowering=False, num_devices=1)
    arrays, args = {}, []
    for name in _INS:
        a = _np.ascontiguousarray(inputs[name])
        arrays[f"in_{name}_dram"] = a
        args.append(nc.dram_tensor(f"in_{name}_dram", a.shape, _mybir.dt.from_np(a.dtype), kind="ExternalInput").ap())
    for i, (shape, dtype) in enumerate(_OUTS):
        dt = _mybir.dt.from_np(_np.dtype(dtype))
        args.append(nc.dram_tensor(f"out_{i}_dram", shape, dt, kind="ExternalOutput").ap())
    build(nc, *args)
    r = _run(nc, [arrays], core_ids=[0])
    return r.results[0]["out_0_dram"]
```

```python
from contextlib import ExitStack

import concourse.bass as bass
from concourse import mybir

F32 = mybir.dt.float32
F16 = mybir.dt.float16
BF16 = mybir.dt.bfloat16
I32 = mybir.dt.int32
ALU = mybir.AluOpType
ACT = mybir.ActivationFunctionType
AX = mybir.AxisListType.X

P = 128
GNN_EPS, LN_EPS, DEN_EPS = 1e-12, 1e-5, 1e-16
SLOPE = 0.2


def hold(eng, sem, value):
    eng.wait_ge(sem, value)
    if not isinstance(value, int):
        eng.nop(nofuse=True)


def after(b, k):
    return not isinstance(b, int) or b >= k


def chain(eng, sem, b, per):
    count = [0]

    def link(ins):
        count[0] += 1
        assert per is None or count[0] <= per
        ins.then_inc(sem, 1)
        hold(eng, sem, b * (per or 0) + count[0])

    return link


def steps(eng, stages, n):
    most = max(lag for lag, _ in stages)

    def fixed(s):
        for lag, body in stages:
            if 0 <= s - lag < n:
                body(s - lag, (s - lag) % 2, (s - lag) // 2)

    rounds = (n - most - 2) // 2
    first = n - 2 * rounds
    for s in range(first):
        fixed(s)
    with eng.Fori(0, rounds) as r:
        for u in range(2):
            for lag, body in stages:
                c = first + u - lag
                body(r * 2 + c, c % 2, r + c // 2)
    for s in range(n, n + most):
        fixed(s)


def build(nc, x, src, dst, gnn_w, gnn_b, w_qkv, w_out, b_out, w_gat, att_src, att_dst, b_gat,
          ln_g, ln_b, w1, b1, w2, b2, edges, out):
    N, D = x.shape
    E = src.shape[0]
    NB = -(-N // P)
    NP = NB * P
    LAST = N - (NB - 1) * P
    KD = D // P
    INNER = w_out.shape[1]
    DH = 64
    HM = INNER // DH
    NE, _, FF = w1.shape
    FT = FF // P
    HT = NE * FT
    GH = att_src.shape[0]
    GW = GH * NE
    PAY = GW + GH
    ET = -(-E // P)
    RT = edges.shape[1] // P
    assert RT * P == edges.shape[1]
    C = 7
    NC = NB // C
    assert NB == NC * C and KD == 2 and PAY == 20

    dram = lambda name, shape, dt=F32: nc.dram_tensor(name, shape, dt, kind="Internal").ap()
    XN = dram("xn_table", [NP, D])
    XP = dram("x_padded", [NP, D])
    SRC = dram("src_padded", [ET * P, 1], I32)
    DST = dram("dst_padded", [ET * P, 1], I32)
    RSRC = dram("router_src", [RT * P, 1], I32)
    RDST = dram("router_dst", [RT * P, 1], I32)
    EF = ET * P + P
    SRCF = dram("src_float", [EF, 1])
    DSTF = dram("dst_float", [EF, 1])
    RSD = dram("row_start", [NP + 1, 1])
    RDF = dram("router_dst_float", [RT * P])
    RDL = dram("router_dst_low", [RT * P], BF16)
    SL = dram("router_src_sorted", [RT * P, 1], I32)
    RK = 40
    GD = dram("router_rows_sorted", [RT * P + RK * P, PAY])
    ACC = dram("neighbour_sum", [NP + P, D + 1])
    TAB = dram("router_table", [NP, PAY])
    MAXT = dram("max_table", [NP, GH])
    MD = dram("shift_table", [NP, 2 * GH])
    AGG = dram("attention_sum", [NP, PAY])

    def where(eng, k):
        return eng.If(eng.value_load(slow[0:1, k:k + 1], min_val=0, max_val=1) != 0)

    def by_block(t):
        return t.rearrange("(b p) c -> p b c", p=P)

    top = ExitStack()
    live = []

    def sem(name):
        live.append(nc.alloc_semaphore(name=name))
        return live[-1]

    def phase(st):
        def done():
            nc.clear_and_free_semaphores(list(live))
            nc.all_engine_barrier()
            live.clear()
        st.callback(done)
        return st.enter_context(nc.Block())

    sb = lambda st, name, shape, dt=F32: st.enter_context(nc.sbuf_tensor(name, shape, dt))
    ps = lambda st, name, shape: st.enter_context(nc.psum_tensor(name, shape, F32))

    top.enter_context(nc.allow_non_contiguous_dma(reason="columns of small tables"))
    with top:
        slow = sb(top, "slow_flags", [1, 2], I32)
        XT = sb(top, "x_cols", [P, KD, NP])
        ident = sb(top, "ident", [P, P])
        upper = sb(top, "upper", [P, P])
        ones = sb(top, "ones_square", [P, P])
        rsi2 = sb(top, "router_starts", [P, NB], I32)
        rdeg = sb(top, "router_degree", [P, NB])
        ag = sb(top, "attention", [P, NB, PAY])
        lower = sb(top, "lower", [P, P])
        mix = sb(top, "mix_matrix", [P, KD, D])
        wg = sb(top, "gnn_w_sb", [P, 2 * KD, D])
        zero = sb(top, "zero", [P, D + 1])
        bg = sb(top, "gnn_b_rows", [P, D])
        bo = sb(top, "b_out_rows", [P, D])
        wgat = sb(top, "w_gat_sb", [P, KD, GW])
        att = sb(top, "att_rows", [P, 2, GW])
        gb = sb(top, "gate_rows", [P, 3, GW])
        T = sb(top, "router_rows", [P, NB, PAY])
        AD = sb(top, "a_dst_rows", [P, NB, GH])
        MXS = sb(top, "max_rows", [P, NB, GH])
        gate = sb(top, "gates", [P, NB, NE])

        with ExitStack() as st:
            sq = sb(st, "squares", [P, C, D])
            X = sb(st, "x_rows", [P, NB, D])
            lnm = sb(st, "ln_mean", [P, NC, C])
            lnv = sb(st, "ln_var", [P, NC, C])
            lns = sb(st, "ln_std", [P, NC, C])
            wkv_n = sb(st, "wkv_rows", [P, 8, D])
            wkv = sb(st, "wkv_cols", [P, KD, 2 * INNER])
            wkm = sb(st, "wkv_mean", [P, KD, 2 * HM])
            wq = sb(st, "wq_rows", [P, 4, D])
            wo_n = sb(st, "w_out_rows", [P, KD, INNER])
            wo = sb(st, "w_out_cols", [P, 4, D])
            kvsq = sb(st, "kv_squares", [P, 2, 2 * INNER])
            kss = sb(st, "kv_sums", [P, 2, 2 * HM])
            kpr = sb(st, "kv_var_product", [P, 2, HM])
            kst = sb(st, "kv_std_product", [P, 2, HM])
            kri = sb(st, "kv_scale", [P, 2, HM])
            ks = sb(st, "k_scaled", [P, 2, INNER])
            vs = sb(st, "v_rows", [P, 2, INNER])
            dots = sb(st, "dots_diag", [P, 4, P])
            bt = sb(st, "b_cols", [P, 4, D])
            xs = sb(st, "x_stage", [P, 2, D])
            xc_ = sb(st, "x_cols_stage", [P, 2, KD * P])
            pkv = ps(st, "ps_kv", [P, 2, 2 * INNER])
            pt = ps(st, "ps_t", [P, 2, 512])
            pd = ps(st, "ps_dots", [P, 4, P])

            x_in = [sem(f"x_in{c}") for c in range(NC)]
            w_in, pad_in, tabs_out, x_zero = sem("w_in"), sem("pad_in"), sem("tabs_out"), sem("x_zero")
            consts, ident_z, lower_z = sem("consts"), sem("ident_z"), sem("lower_z")
            dchain, ln_var_ok, ln_std_ok, ln_ok = sem("dve_chain"), sem("ln_var_ok"), sem("ln_std_ok"), sem("ln_ok")
            wt_ok, wt_used, wkv_ok = sem("wt_ok"), sem("wt_used"), sem("wkv_ok")
            xt_ps, xt_ok, xs_ok, xt_kept = sem("xt_ps"), sem("xt_ok"), sem("xs_ok"), sem("xt_kept")
            kv_ok, kvsq_ok, v_ok, kss_ok, kpr_ok = sem("kv_ok"), sem("kvsq_ok"), sem("v_ok"), sem("kss_ok"), sem("kpr_ok")
            kst_ok, kri_ok, ks_ok, dots_ok = sem("kst_ok"), sem("kri_ok"), sem("ks_ok"), sem("dots_ok")
            dd_ok, bt_ps, bt_ok, mix_ps, mix_ok = sem("dd_ok"), sem("bt_ps"), sem("bt_ok"), sem("mix_ps"), sem("mix_ok")
            dz_ok, kve_ok, fill_ok = sem("dz_ok"), sem("kve_ok"), sem("fill_ok")
            e_in, e_ok, e_out = sem("redges_in"), sem("redges_ok"), sem("redges_out")
            re = sb(st, "router_edges", [P, 2, RT], I32)
            fill = sb(st, "edge_fill", [P, 2], I32)
            block = phase(st)

            W_LOADS = 14

            @block.sync
            def _(sp):
                sp.dma_start(re[:, :, :], edges.rearrange("k (p t) -> p k t", p=P)).then_inc(e_in, 16)
                sp.wait_ge(x_zero, 1)
                for c in range(NC):
                    r0, r1 = c * C * P, min((c + 1) * C * P, N)
                    full = (r1 - r0) // P
                    sp.dma_start(X[:, c * C:c * C + full, :], by_block(x[r0:r0 + full * P, :])).then_inc(x_in[c], 16)
                    if full < C:
                        sp.dma_start(X[0:LAST, NB - 1, :], x[(NB - 1) * P:N, :]).then_inc(x_in[c], 16)
                full_e = (ET - 1) * P
                for a, t in ((src, SRC), (dst, DST)):
                    sp.dma_start(t[0:full_e, 0].rearrange("(a b) -> a b", b=P), a[0:full_e].rearrange("(a b) -> a b", b=P)).then_inc(pad_in, 16)
                    sp.dma_start(t[full_e:E, :], a[full_e:E].rearrange("(a b) -> a b", b=1)).then_inc(pad_in, 16)
                sp.dma_start(XP[0:N, :], x).then_inc(pad_in, 16)
                sp.wait_ge(fill_ok, 3)
                sp.dma_start(XP[N:NP, :], zero[0:NP - N, 0:D]).then_inc(pad_in, 16)
                sp.dma_start(SRC[E:ET * P, :], fill[0:ET * P - E, 0:1]).then_inc(pad_in, 16)
                sp.dma_start(DST[E:ET * P, :], fill[0:ET * P - E, 1:2]).then_inc(pad_in, 16)
                sp.wait_ge(e_ok, 2)
                for k, t in ((0, RSRC), (1, RDST)):
                    sp.dma_start(t.rearrange("(p t) c -> p (t c)", p=P), re[:, k, :]).then_inc(e_out, 16)
                sp.wait_ge(e_out, 32)
                for c in range(NC):
                    sp.wait_ge(ln_ok, (c + 1) * C)
                    sp.dma_start(by_block(XN[c * C * P:(c + 1) * C * P, :]), X[:, c * C:(c + 1) * C, :]).then_inc(tabs_out, 16)
                sp.wait_ge(tabs_out, 16 * NC)
                sp.wait_ge(pad_in, 16 * 8)

            @block.gpsimd
            def _(pool):
                nc.gpsimd.memset(ident[:, :], 0.0).then_inc(ident_z, 1)
                nc.gpsimd.memset(lower[:, :], 1.0).then_inc(lower_z, 1)
                pool.wait_ge(ident_z, 1)
                nc.gpsimd.affine_select(out=ident[:, :], in_=ident[:, :], compare_op=ALU.not_equal, fill=1.0,
                                        base=0, pattern=[[-1, P]], channel_multiplier=1).then_inc(consts, 1)
                pool.wait_ge(lower_z, 1)
                nc.gpsimd.affine_select(out=lower[:, :], in_=lower[:, :], compare_op=ALU.is_gt, fill=0.0,
                                        base=0, pattern=[[-1, P]], channel_multiplier=1).then_inc(consts, 1)
                nc.gpsimd.memset(upper[:, :], 1.0).then_inc(ident_z, 1)
                nc.gpsimd.memset(ones[:, :], 1.0).then_inc(ident_z, 1)
                pool.wait_ge(ident_z, 3)
                nc.gpsimd.affine_select(out=upper[:, :], in_=upper[:, :], compare_op=ALU.is_gt, fill=0.0,
                                        base=0, pattern=[[1, P]], channel_multiplier=-1).then_inc(consts, 1)

                def stage(b, q, m):
                    hold(pool, ln_ok, b + 1)
                    if after(b, 2):
                        hold(pool, xt_ps, b - 1)
                    nc.gpsimd.tensor_copy(xs[:, q, :], X[:, bass.ds(b, 1), :].rearrange("p a b -> p (a b)")).then_inc(xs_ok, 1)

                def keep(b, q, m):
                    hold(pool, xt_ok, b + 1)
                    nc.gpsimd.tensor_copy(XT[:, :, bass.ds(b * P, P)], xc_[:, q, :].rearrange("p (k n) -> p k n", k=KD)).then_inc(xt_kept, 1)

                steps(pool, [(0, stage), (1, keep)], NB)

            @block.vector
            def _(dve):
                n = [0]

                def link(ins):
                    n[0] += 1
                    ins.then_inc(dchain, 1)
                    dve.wait_ge(dchain, n[0])

                nc.vector.memset(X[:, NB - 1, :], 0.0).then_inc(x_zero, 1)
                nc.vector.memset(zero[:, :], 0.0).then_inc(fill_ok, 1)
                nc.vector.memset(fill[:, 0:1], 0).then_inc(fill_ok, 1)
                nc.vector.memset(fill[:, 1:2], NP - 1).then_inc(fill_ok, 1)
                nc.vector.memset(dots[:, :, :], 0.0).then_inc(dz_ok, 1)
                dve.wait_ge(e_in, 16)
                nc.vector.tensor_scalar(re[:, 0, :], re[:, 0, :], float(N - 1), None, ALU.min).then_inc(e_ok, 1)
                nc.vector.tensor_scalar(re[:, 1, :], re[:, 1, :], float(NP - 1), None, ALU.min).then_inc(e_ok, 1)
                for c in range(NC):
                    xc = X[:, c * C:(c + 1) * C, :]
                    dve.wait_ge(x_in[c], 16 if c < NC - 1 else 32)
                    link(nc.vector.tensor_reduce(lnm[:, c, :], xc, AX, ALU.add))
                    link(nc.vector.tensor_scalar(lnm[:, c, :], lnm[:, c, :], 1.0 / D, None, ALU.mult))
                    link(nc.vector.tensor_tensor(xc, xc, lnm[:, c, :].unsqueeze(2).to_broadcast([P, C, D]), ALU.subtract))
                    link(nc.vector.tensor_tensor(sq[:, :, :], xc, xc, ALU.mult))
                    link(nc.vector.tensor_reduce(lnv[:, c, :], sq[:, :, :], AX, ALU.add))
                    nc.vector.tensor_scalar(lnv[:, c, :], lnv[:, c, :], 1.0 / D, LN_EPS, ALU.mult, ALU.add).then_inc(ln_var_ok, 1)
                    dve.wait_ge(ln_std_ok, c + 1)
                    link(nc.vector.reciprocal(lns[:, c, :], lns[:, c, :]))
                    nc.vector.tensor_tensor(xc, xc, lns[:, c, :].unsqueeze(2).to_broadcast([P, C, D]), ALU.mult).then_inc(ln_ok, C)
                dve.wait_ge(wt_used, 4)
                wh = wkv[:, :, :].rearrange("p k (h e) -> p (k h) e", e=DH)
                wm = wkm[:, :, :].rearrange("p k h -> p (k h)")
                link(nc.vector.tensor_reduce(wm, wh, AX, ALU.add))
                link(nc.vector.tensor_scalar(wm, wm, 1.0 / DH, None, ALU.mult))
                nc.vector.tensor_tensor(wh, wh, wm.unsqueeze(2).to_broadcast([P, KD * 2 * HM, DH]), ALU.subtract).then_inc(wkv_ok, 1)

                def variances(b, q, m):
                    hold(dve, kvsq_ok, b + 1)
                    nc.vector.tensor_reduce(kss[:, q, :], kvsq[:, q, :].rearrange("p (h e) -> p h e", e=DH), AX, ALU.add).then_inc(kss_ok, 1)
                    hold(dve, kss_ok, b + 1)
                    link2(nc.vector.tensor_scalar(kss[:, q, :], kss[:, q, :], 1.0 / DH, LN_EPS, ALU.mult, ALU.add), b)
                    nc.vector.tensor_tensor(kpr[:, q, :], kss[:, q, 0:HM], kss[:, q, HM:2 * HM], ALU.mult).then_inc(kpr_ok, 1)

                def link2(ins, b):
                    ins.then_inc(kve_ok, 1)
                    hold(dve, kve_ok, b + 1)

                def scale_k(b, q, m):
                    hold(dve, kst_ok, b + 1)
                    nc.vector.reciprocal(kri[:, q, :], kst[:, q, :]).then_inc(kri_ok, 1)
                    hold(dve, kri_ok, b + 1)
                    if after(b, 2):
                        hold(dve, dots_ok, b - 1)
                    nc.vector.tensor_tensor(ks[:, q, :].rearrange("p (h e) -> p h e", e=DH),
                                            pkv[:, q, 0:INNER].rearrange("p (h e) -> p h e", e=DH),
                                            kri[:, q, :].unsqueeze(2).to_broadcast([P, HM, DH]), ALU.mult).then_inc(ks_ok, 1)

                steps(dve, [(0, variances), (1, scale_k)], NB)
                dve.wait_ge(dots_ok, NB)
                dve.wait_ge(dz_ok, 1)
                nc.vector.tensor_scalar(dots[0:DH, :, 0:DH], pd[0:DH, :, 0:DH], 1.0 / N, None, ALU.mult).then_inc(dd_ok, 1)
                nc.vector.tensor_scalar(dots[DH:P, :, DH:P], pd[DH:P, :, DH:P], 1.0 / N, None, ALU.mult).then_inc(dd_ok, 1)

            @block.scalar
            def _(act):
                loads = [(wkv_n[:, :, :], w_qkv[INNER:3 * INNER, :].rearrange("(j p) d -> p j d", p=P)),
                         (wq[:, :, :], w_qkv[0:INNER, :].rearrange("(j p) d -> p j d", p=P)),
                         (wo_n[:, :, :], w_out.rearrange("(j p) d -> p j d", p=P)),
                         (wg[:, :, :], gnn_w.rearrange("(j p) d -> p j d", p=P)),
                         (wgat[:, :, :], w_gat.rearrange("(j p) d -> p j d", p=P)),
                         (bg[:, :], gnn_b.partition_broadcast(P)), (bo[:, :], b_out.partition_broadcast(P)),
                         (att[:, 0, :], att_src.rearrange("a b -> (a b)").partition_broadcast(P)),
                         (att[:, 1, :], att_dst.rearrange("a b -> (a b)").partition_broadcast(P)),
                         (gb[:, 0, :], b_gat.partition_broadcast(P)), (gb[:, 1, :], ln_g.partition_broadcast(P)),
                         (gb[:, 2, :], ln_b.partition_broadcast(P))]
                for to, fr in loads:
                    act.dma_start(to, fr).then_inc(w_in, 16)
                act.wait_ge(w_in, 16 * len(loads))
                for g in range(4):
                    act.wait_ge(wt_ok, g + 1)
                    nc.scalar.copy(wkv[:, g // 2, (g % 2) * 512:(g % 2 + 1) * 512], pt[:, g % 2, :]).then_inc(wt_used, 1)
                for g in range(2):
                    act.wait_ge(wt_ok, 5 + g)
                    nc.scalar.copy(wo[:, 2 * g:2 * g + 2, :].rearrange("p a b -> p (a b)"), pt[:, g % 2, :]).then_inc(wt_used, 1)
                for c in range(NC):
                    act.wait_ge(ln_var_ok, c + 1)
                    nc.scalar.activation(lns[:, c, :], lnv[:, c, :], ACT.Sqrt).then_inc(ln_std_ok, 1)

                def columns(b, q, m):
                    hold(act, xt_ps, b + 1)
                    if after(b, 2):
                        hold(act, kv_ok, b - 1)
                        hold(act, xt_kept, b - 1)
                    nc.scalar.copy(xc_[:, q, :], pt[:, q, 0:KD * P]).then_inc(xt_ok, 1)

                def squares(b, q, m):
                    hold(act, kv_ok, b + 1)
                    if after(b, 2):
                        hold(act, kss_ok, b - 1)
                    nc.scalar.activation(kvsq[:, q, :], pkv[:, q, :], ACT.Square).then_inc(kvsq_ok, 1)
                    if after(b, 2):
                        hold(act, dots_ok, b - 1)
                    nc.scalar.copy(vs[:, q, :], pkv[:, q, INNER:2 * INNER]).then_inc(v_ok, 1)

                def roots(b, q, m):
                    hold(act, kpr_ok, b + 1)
                    nc.scalar.activation(kst[:, q, :], kpr[:, q, :], ACT.Sqrt).then_inc(kst_ok, 1)

                steps(act, [(0, columns), (1, squares), (1, roots)], NB)
                act.wait_ge(bt_ps, 1)
                nc.scalar.copy(bt[:, :, :].rearrange("p a b -> p (a b)"), pkv[:, 0, :]).then_inc(bt_ok, 1)
                act.wait_ge(mix_ps, 1)
                nc.scalar.copy(mix[:, :, :].rearrange("p a b -> p (a b)"), pt[:, 0, :]).then_inc(mix_ok, 1)
                act.wait_ge(mix_ok, 1)

            @block.tensor
            def _(pe):
                pe.wait_ge(consts, 3)
                pe.wait_ge(w_in, 16 * 12)
                for g in range(4):
                    if g >= 2:
                        pe.wait_ge(wt_used, g - 1)
                    for j in range(4):
                        mm = nc.tensor.transpose(pt[:, g % 2, j * P:(j + 1) * P],
                                                 wkv_n[:, (g % 2) * 4 + j, (g // 2) * P:(g // 2 + 1) * P], ident[:, :])
                    mm.then_inc(wt_ok, 1)
                for g in range(2):
                    pe.wait_ge(wt_used, g + 3)
                    for j in range(4):
                        mm = nc.tensor.transpose(pt[:, g % 2, j * P:(j + 1) * P],
                                                 wo_n[:, j % 2, (2 * g + j // 2) * P:(2 * g + j // 2 + 1) * P], ident[:, :])
                    mm.then_inc(wt_ok, 1)
                pe.wait_ge(wt_used, 6)

                def turn(b, q, m):
                    hold(pe, xs_ok, b + 1)
                    if after(b, 2):
                        hold(pe, xt_ok, b - 1)
                    for k in range(KD):
                        mm = nc.tensor.transpose(pt[:, q, k * P:(k + 1) * P], xs[:, q, k * P:(k + 1) * P], ident[:, :])
                    mm.then_inc(xt_ps, 1)

                pe.wait_ge(wkv_ok, 1)
                pe.wait_ge(fill_ok, 3)
                nc.tensor.matmul(pd[:, :, :].rearrange("p a b -> p (a b)"), zero[:, 0:P], wkv[:, 0, 0:512], start=True, stop=True, skip_group_check=True)

                def kv(b, q, m):
                    hold(pe, xt_ok, b + 1)
                    if after(b, 2):
                        hold(pe, v_ok, b - 1)
                        hold(pe, ks_ok, b - 1)
                    for half in range(2):
                        for k in range(KD):
                            mm = nc.tensor.matmul(pkv[:, q, half * INNER:(half + 1) * INNER], xc_[:, q, k * P:(k + 1) * P],
                                                  wkv[:, k, half * INNER:(half + 1) * INNER], start=k == 0, stop=k == KD - 1)
                    mm.then_inc(kv_ok, 1)

                def product(b, q, m):
                    hold(pe, ks_ok, b + 1)
                    hold(pe, v_ok, b + 1)
                    for h in range(4):
                        mm = nc.tensor.matmul(pd[:, h, :], ks[:, q, h * P:(h + 1) * P], vs[:, q, h * P:(h + 1) * P],
                                              start=False, stop=True, skip_group_check=True)
                    mm.then_inc(dots_ok, 1)

                steps(pe, [(0, turn), (1, kv), (3, product)], NB)
                pe.wait_ge(dd_ok, 2)
                for h in range(4):
                    mm = nc.tensor.matmul(pkv[:, 0, h * D:(h + 1) * D], dots[:, h, :], wq[:, h, :], start=True, stop=True)
                mm.then_inc(bt_ps, 1)
                pe.wait_ge(bt_ok, 1)
                for m in range(KD):
                    for h in range(4):
                        mm = nc.tensor.matmul(pt[:, 0, m * D:(m + 1) * D], bt[:, h, m * P:(m + 1) * P], wo[:, h, :], start=h == 0, stop=h == 3)
                mm.then_inc(mix_ps, 1)



        def edge_pass(kind):
            flag = 0 if kind == "sum" else 1
            table, tw = (XN, D) if kind == "sum" else (TAB, PAY)
            acc, aw = {"sum": (ACC, D + 1), "max": (MAXT, GH), "soft": (AGG, PAY)}[kind]
            esrc, edst, tiles = (SRC, DST, ET) if kind == "sum" else (RSRC, RDST, RT)
            gw = D + 1 if kind == "sum" else PAY
            with ExitStack() as st:
                si = sb(st, f"{kind}_src", [P, 1], I32)
                di = sb(st, f"{kind}_dst", [P, 1], I32)
                db = sb(st, f"{kind}_dst_row", [P, P], I32)
                ui = sb(st, f"{kind}_rows_out", [P, 1], I32)
                df = sb(st, f"{kind}_dst_f", [P, 1])
                dbf = sb(st, f"{kind}_dst_row_f", [P, P])
                same = sb(st, f"{kind}_same", [P, P])
                before = sb(st, f"{kind}_before", [P, P])
                cnt = sb(st, f"{kind}_count", [P, 2])
                got = sb(st, f"{kind}_gathered", [P, gw])
                old = sb(st, f"{kind}_old", [P, aw])
                new = sb(st, f"{kind}_new", [P, aw])
                shift = sb(st, f"{kind}_shift", [P, 2 * GH])
                pay = sb(st, f"{kind}_payload", [P, PAY])
                wts = sb(st, f"{kind}_scores", [P, 2, GH])
                spread = sb(st, f"{kind}_spread", [P, GH, P])
                low = sb(st, f"{kind}_low", [P, GH])
                psum = ps(st, f"{kind}_ps", [P, 512])
                names = ["init", "ready", "idx", "gat", "oldr", "shr", "chain", "same_ok", "rows_ok", "pay_ok", "exp_in", "exp_ok", "mm_ok", "new_ok", "scat"]
                s = {k: sem(f"{kind}_{k}") for k in names}
                block = phase(st)

                @block.sync
                def _(sp):
                    with where(sp, flag):
                        sp.wait_ge(s["ready"], 1)
                        fill = (low if kind == "max" else zero)[:, 0:aw]
                        sp.dma_start(by_block(acc[0:NP, :]), fill.unsqueeze(1).to_broadcast([P, NB, aw])).then_inc(s["init"], 16)

                        def load(t):
                            sp.dma_start(si[:, :], esrc[bass.ds(t * P, P), :]).then_inc(s["idx"], 16)
                            sp.dma_start(di[:, :], edst[bass.ds(t * P, P), :]).then_inc(s["idx"], 16)
                            sp.dma_start(db[:, :], edst[bass.ds(t * P, P), :].rearrange("a b -> (a b)").partition_broadcast(P)).then_inc(s["idx"], 16)

                        load(0)
                        with sp.Fori(1, tiles) as t:
                            hold(sp, s["scat"], t * 16)
                            load(t)
                        sp.wait_ge(s["init"], 16)
                        sp.wait_ge(s["scat"], 16 * tiles)

                @block.gpsimd
                def _(pool):
                    with where(pool, flag):
                        pool.wait_ge(s["init"], 16)
                        with pool.Fori(0, tiles) as t:
                            hold(pool, s["idx"], t * 48 + 48)
                            nc.gpsimd.indirect_dma_start(got[:, 0:tw], None, table, bass.IndirectOffsetOnAxis(ap=si[:, 0:1], axis=0)).then_inc(s["gat"], 16)
                            nc.gpsimd.indirect_dma_start(old[:, :], None, acc, bass.IndirectOffsetOnAxis(ap=di[:, 0:1], axis=0)).then_inc(s["oldr"], 16)
                            if kind == "soft":
                                nc.gpsimd.indirect_dma_start(shift[:, :], None, MD, bass.IndirectOffsetOnAxis(ap=di[:, 0:1], axis=0)).then_inc(s["shr"], 16)
                            hold(pool, s["new_ok"], t + 1)
                            nc.gpsimd.indirect_dma_start(acc, bass.IndirectOffsetOnAxis(ap=ui[:, 0:1], axis=0), new[:, :], None,
                                                         bounds_check=NP - 1, oob_is_err=False).then_inc(s["scat"], 16)

                @block.vector
                def _(dve):
                    with where(dve, flag):
                        nc.vector.memset(low[:, :], LOW)
                        nc.vector.memset(got[:, gw - 1:gw], 1.0)
                        dve.drain().then_inc(s["ready"], 1)
                        dve.wait_ge(s["ready"], 1)
                        L = {"sum": 5, "max": 7, "soft": 10}[kind]
                        with dve.Fori(0, tiles) as t:
                            k = [0]

                            def link(ins):
                                k[0] += 1
                                ins.then_inc(s["chain"], 1)
                                hold(dve, s["chain"], t * L + k[0])

                            hold(dve, s["idx"], t * 48 + 48)
                            link(nc.vector.tensor_copy(df[:, :], di[:, :]))
                            link(nc.vector.tensor_copy(dbf[:, :], db[:, :]))
                            nc.vector.tensor_scalar(same[:, :], dbf[:, :], df[:, 0:1], None, ALU.is_equal).then_inc(s["same_ok"], 1)
                            hold(dve, s["same_ok"], t + 1)
                            link(nc.vector.tensor_tensor(before[:, :], same[:, :], lower[:, :], ALU.mult))
                            link(nc.vector.tensor_reduce(cnt[:, 0:1], before[:, :], AX, ALU.max))
                            link(nc.vector.tensor_scalar(cnt[:, 1:2], cnt[:, 0:1], BIG, df[:, 0:1], ALU.mult, ALU.add))
                            nc.vector.tensor_copy(ui[:, :], cnt[:, 1:2]).then_inc(s["rows_ok"], 1)
                            hold(dve, s["gat"], t * 16 + 16)
                            if kind == "max":
                                link(nc.vector.tensor_scalar(before[:, :], same[:, :], -1.0, -LOW, ALU.add, ALU.mult))
                                hold(dve, s["mm_ok"], t + 1)
                                link(nc.vector.tensor_tensor(spread[:, :, :], psum[:, :].rearrange("p (h e) -> p h e", h=GH),
                                                             before[:, :].unsqueeze(1).to_broadcast([P, GH, P]), ALU.add))
                                nc.vector.tensor_reduce(new[:, :], spread[:, :, :], AX, ALU.max).then_inc(s["pay_ok"], 1)
                                hold(dve, s["pay_ok"], t + 1)
                                hold(dve, s["oldr"], t * 16 + 16)
                                hold(dve, s["rows_ok"], t + 1)
                                nc.vector.tensor_tensor(new[:, :], new[:, :], old[:, :], ALU.max).then_inc(s["new_ok"], 1)
                            else:
                                if kind == "soft":
                                    hold(dve, s["shr"], t * 16 + 16)
                                    link(nc.vector.tensor_tensor(wts[:, 0, :], got[:, GW:PAY], shift[:, 0:GH], ALU.add))
                                    link(nc.vector.tensor_scalar(wts[:, 1, :], wts[:, 0, :], SLOPE, None, ALU.mult))
                                    link(nc.vector.tensor_tensor(wts[:, 0, :], wts[:, 0, :], wts[:, 1, :], ALU.max))
                                    link(nc.vector.tensor_tensor(wts[:, 1, :], wts[:, 0, :], shift[:, GH:2 * GH], ALU.subtract))
                                    dve.sem_inc(s["exp_in"], 1)
                                    hold(dve, s["exp_ok"], t + 1)
                                    link(nc.vector.tensor_tensor(pay[:, 0:GW].rearrange("p (h e) -> p h e", h=GH), got[:, 0:GW].rearrange("p (h e) -> p h e", h=GH),
                                                                 pay[:, GW:PAY].unsqueeze(2).to_broadcast([P, GH, NE]), ALU.mult))
                                    dve.sem_inc(s["pay_ok"], 1)
                                hold(dve, s["mm_ok"], t + 1)
                                hold(dve, s["oldr"], t * 16 + 16)
                                hold(dve, s["rows_ok"], t + 1)
                                nc.vector.tensor_tensor(new[:, :], psum[:, 0:aw], old[:, :], ALU.add).then_inc(s["new_ok"], 1)
                            assert k[0] == L

                @block.scalar
                def _(act):
                    with where(act, flag):
                        if kind == "soft":
                            with act.Fori(0, tiles) as t:
                                hold(act, s["exp_in"], t + 1)
                                nc.scalar.activation(pay[:, GW:PAY], wts[:, 1, :], ACT.Exp).then_inc(s["exp_ok"], 1)

                @block.tensor
                def _(pe):
                    with where(pe, flag):
                        pe.wait_ge(s["ready"], 1)
                        with pe.Fori(0, tiles) as t:
                            hold(pe, s["same_ok"], t + 1)
                            hold(pe, s["gat"], t * 16 + 16)
                            if kind == "max":
                                for h in range(GH):
                                    mm = nc.tensor.matmul(psum[:, h * P:(h + 1) * P], got[:, GW + h:GW + h + 1].to_broadcast([P, P]), ident[:, :], start=True, stop=True)
                            elif kind == "sum":
                                mm = nc.tensor.matmul(psum[:, 0:aw], same[:, :], got[:, :], start=True, stop=True)
                            else:
                                hold(pe, s["pay_ok"], t + 1)
                                mm = nc.tensor.matmul(psum[:, 0:aw], same[:, :], pay[:, :], start=True, stop=True)
                            mm.then_inc(s["mm_ok"], 1)


        BIG = 1.0e6
        LOW = -1.0e30

        with ExitStack() as st:
            ei = sb(st, "edges_int", [P, 2, ET], I32)
            ef = sb(st, "edges_float", [P, 2, ET])
            tail = sb(st, "edges_tail", [P, 2])
            l_in, l_ok, l_out = sem("list_in"), sem("list_ok"), sem("list_out")
            block = phase(st)

            @block.sync
            def _(sp):
                for k, t in ((0, SRC), (1, DST)):
                    sp.dma_start(ei[:, k, :], t.rearrange("(p t) c -> p (t c)", p=P)).then_inc(l_in, 16)
                sp.wait_ge(l_ok, 4)
                for k, t in ((0, SRCF), (1, DSTF)):
                    sp.dma_start(t[0:ET * P, :].rearrange("(p t) c -> p (t c)", p=P), ef[:, k, :]).then_inc(l_out, 16)
                    sp.dma_start(t[ET * P:EF, :], tail[:, k:k + 1]).then_inc(l_out, 16)
                sp.wait_ge(l_out, 64)

            @block.vector
            def _(dve):
                nc.vector.memset(tail[:, 0:1], 0.0).then_inc(l_ok, 1)
                nc.vector.memset(tail[:, 1:2], float(NP - 1)).then_inc(l_ok, 1)
                dve.wait_ge(l_in, 32)
                for k in range(2):
                    nc.vector.tensor_copy(ef[:, k, :], ei[:, k, :]).then_inc(l_ok, 1)

        RUN = 512
        KEYS = ET * P // RUN
        SLOT = 64
        assert KEYS * RUN == ET * P and KEYS <= 512
        NPAIR = (NB + 1) // 2
        gst = ExitStack()
        deg = sb(gst, "in_degree", [P, 2 * NPAIR])
        hit = sb(gst, "src_high", [P, NPAIR, P], BF16)
        lot = sb(gst, "src_low", [P, NPAIR, P], BF16)
        with ExitStack() as st:
            krow = sb(st, "keys", [1, KEYS])
            onesr = sb(st, "ones_row", [1, P])
            dcol = sb(st, "node_ids", [P, NB])
            junk = sb(st, "search_junk", [P, RUN])
            coarse = sb(st, "coarse_count", [P, NB])
            offf = sb(st, "run_offset", [P, NB])
            offi = sb(st, "run_offset_int", [P, NB], I32)
            fine = sb(st, "fine_count", [P, NB])
            rs = sb(st, "row_starts", [P, NB])
            rsi = sb(st, "row_starts_int", [P, NB], I32)
            rn = sb(st, "row_ends", [P, NB])
            runs = sb(st, "dst_runs", [P, 4, RUN])
            slots = sb(st, "src_slots", [P, 2 * NPAIR, SLOT])
            sint = sb(st, "src_slots_int", [P, 2 * NPAIR, SLOT], I32)
            sint2 = sb(st, "src_slots_part", [P, 2 * NPAIR, SLOT], I32)
            hi = sb(st, "slots_high", [P, 2 * NPAIR, SLOT])
            lo = sb(st, "slots_low", [P, 2 * NPAIR, SLOT])
            kio = sb(st, "slot_ids", [P, SLOT])
            ea = sb(st, "sort_check_a", [P, ET])
            eb = sb(st, "sort_check_b", [P, ET])
            bad = sb(st, "bad", [P, 4])
            ends = sb(st, "list_end", [1, 1])
            pk = ps(st, "ps_keys", [P, 512])
            ptr = ps(st, "ps_slots", [P, 4, 512])
            names = ["keys", "chk_in", "ones", "pk_ok", "iota", "coarse", "off", "fine", "ch", "rs", "rs_out", "rn_in", "rsi", "end",
                     "masked", "pt_ok", "pt_used", "badp", "badr"]
            s = {k: sem(f"search_{k}") for k in names}
            run_in = [sem(f"search_run{i}") for i in range(4)]
            slot_in = sem("search_slots")
            block = phase(st)

            @block.sync
            def _(sp):
                with nc.allow_non_contiguous_dma(reason="every 512th destination"):
                    sp.dma_start(krow[0:1, :].unsqueeze(2), DSTF[0:KEYS * RUN, :].rearrange("(j r) c -> c j r", r=RUN)[:, :, 0:1]).then_inc(s["keys"], 16)
                sp.dma_start(ea[:, :], DSTF[0:ET * P, :].rearrange("(p t) c -> p (t c)", p=P)).then_inc(s["chk_in"], 16)
                sp.dma_start(eb[:, :], DSTF[1:ET * P + 1, :].rearrange("(p t) c -> p (t c)", p=P)).then_inc(s["chk_in"], 16)
                sp.wait_ge(s["rs"], 1)
                sp.wait_ge(s["end"], 1)
                sp.dma_start(RSD[0:NP, :].rearrange("(b p) c -> p b c", p=P), rs[:, :].unsqueeze(2)).then_inc(s["rs_out"], 16)
                sp.dma_start(RSD[NP:NP + 1, :], ends[0:1, 0:1]).then_inc(s["rs_out"], 16)
                sp.wait_ge(s["rs_out"], 32)
                sp.dma_start(rn[:, :].unsqueeze(2), RSD[1:NP + 1, :].rearrange("(b p) c -> p b c", p=P)).then_inc(s["rn_in"], 16)

            @block.gpsimd
            def _(pool):
                nc.gpsimd.iota(dcol[:, :], pattern=[[P, NB]], base=0, channel_multiplier=1, allow_small_or_imprecise_dtypes=True).then_inc(s["iota"], 1)
                nc.gpsimd.iota(kio[:, :], pattern=[[1, SLOT]], base=0, channel_multiplier=0, allow_small_or_imprecise_dtypes=True).then_inc(s["iota"], 1)
                pool.wait_ge(s["off"], 1)
                for b in range(NB):
                    if b >= 4:
                        pool.wait_ge(s["fine"], b - 3)
                    nc.gpsimd.indirect_dma_start(runs[:, b % 4, :], None, DSTF[0:ET * P, :],
                                                 bass.IndirectOffsetOnAxis(ap=offi[:, b:b + 1], axis=0)).then_inc(run_in[b % 4], 16)
                pool.wait_ge(s["rsi"], 1)
                for b in range(NB):
                    nc.gpsimd.indirect_dma_start(slots[:, b, :], None, SRCF, bass.IndirectOffsetOnAxis(ap=rsi[:, b:b + 1], axis=0)).then_inc(slot_in, 16)
                pool.wait_ge(s["badp"], 1)
                nc.gpsimd.partition_all_reduce(bad[:, 3:4], bad[:, 2:3], P, bass.bass_isa.ReduceOp.max).then_inc(s["badr"], 1)

            @block.tensor
            def _(pe):
                pe.wait_ge(s["ones"], 1)
                pe.wait_ge(s["keys"], 16)
                nc.tensor.matmul(pk[:, 0:KEYS], onesr[0:1, :], krow[0:1, :], start=True, stop=True).then_inc(s["pk_ok"], 1)
                pe.wait_ge(s["masked"], 1)
                n = 0
                for part in (hi, lo):
                    for g in range(0, NPAIR, 4):
                        if n >= 4:
                            pe.wait_ge(s["pt_used"], n - 3)
                        for m in range(g, min(g + 4, NPAIR)):
                            mm = nc.tensor.transpose(ptr[:, n % 4, (m - g) * P:(m - g + 1) * P],
                                                     part[:, 2 * m:2 * m + 2, :].rearrange("p a b -> p (a b)"), ident[:, :])
                        mm.then_inc(s["pt_ok"], 1)
                        n += 1

            @block.scalar
            def _(act):
                n = 0
                for part in (hit, lot):
                    for g in range(0, NPAIR, 4):
                        w = min(4, NPAIR - g)
                        act.wait_ge(s["pt_ok"], n + 1)
                        nc.scalar.copy(part[:, g:g + w, :].rearrange("p a b -> p (a b)"), ptr[:, n % 4, 0:w * P]).then_inc(s["pt_used"], 1)
                        n += 1

            @block.vector
            def _(dve):
                link = chain(dve, s["ch"], 0, None)
                TT, TS = nc.vector.tensor_tensor, nc.vector.tensor_scalar
                nc.vector.memset(onesr[:, :], 1.0).then_inc(s["ones"], 1)
                nc.vector.memset(ends[:, :], float(E)).then_inc(s["end"], 1)
                dve.wait_ge(s["pk_ok"], 1)
                dve.wait_ge(s["iota"], 2)
                for b in range(NB):
                    link(TS(junk[:, 0:KEYS], pk[:, 0:KEYS], dcol[:, b:b + 1], 0.0, ALU.is_lt, ALU.add, accum_out=coarse[:, b:b + 1]))
                link(TS(offf[:, :], coarse[:, :], -1.0, 0.0, ALU.add, ALU.max))
                link(TS(offf[:, :], offf[:, :], float(RUN), None, ALU.mult))
                nc.vector.tensor_copy(offi[:, :], offf[:, :]).then_inc(s["off"], 1)
                for b in range(NB):
                    dve.wait_ge(run_in[b % 4], 16 * (b // 4 + 1))
                    TS(junk[:, :], runs[:, b % 4, :], dcol[:, b:b + 1], 0.0, ALU.is_lt, ALU.add, accum_out=fine[:, b:b + 1]).then_inc(s["fine"], 1)
                    dve.wait_ge(s["fine"], b + 1)
                link(TT(rs[:, :], offf[:, :], fine[:, :], ALU.add))
                link(nc.vector.tensor_copy(rsi[:, :], rs[:, :]))
                dve.sem_inc(s["rs"], 1)
                dve.sem_inc(s["rsi"], 1)
                link(nc.vector.memset(deg[:, :], 0.0))
                dve.wait_ge(s["rn_in"], 16)
                link(TT(deg[:, 0:NB], rn[:, :], rs[:, :], ALU.subtract))
                dve.wait_ge(s["chk_in"], 32)
                link(TT(ea[:, :], ea[:, :], eb[:, :], ALU.is_gt))
                link(nc.vector.tensor_reduce(bad[:, 0:1], ea[:, :], AX, ALU.max))
                link(nc.vector.tensor_reduce(bad[:, 1:2], deg[:, 0:NB - 1], AX, ALU.max))
                link(TT(bad[0:LAST, 1:2], bad[0:LAST, 1:2], deg[0:LAST, NB - 1:NB], ALU.max))
                link(TS(bad[:, 1:2], bad[:, 1:2], float(SLOT), None, ALU.is_gt))
                TT(bad[:, 2:3], bad[:, 0:1], bad[:, 1:2], ALU.max).then_inc(s["badp"], 1)
                dve.wait_ge(s["badr"], 1)
                link(nc.vector.tensor_copy(slow[0:1, 0:1], bad[0:1, 3:4]))
                dve.wait_ge(slot_in, 16 * NB)
                link(nc.vector.memset(slots[:, NB:2 * NPAIR, :], 0.0))
                link(nc.vector.tensor_copy(sint[:, :, :], slots[:, :, :]))
                link(TS(sint2[:, :, :], sint[:, :, :], 7, None, ALU.logical_shift_right))
                link(nc.vector.tensor_copy(hi[:, :, :], sint2[:, :, :]))
                link(TS(sint2[:, :, :], sint[:, :, :], P - 1, None, ALU.bitwise_and))
                link(nc.vector.tensor_copy(lo[:, :, :], sint2[:, :, :]))
                link(TT(slots[:, :, :], kio[:, :].unsqueeze(1).to_broadcast([P, 2 * NPAIR, SLOT]),
                        deg[:, :].unsqueeze(2).to_broadcast([P, 2 * NPAIR, SLOT]), ALU.is_ge))
                link(TS(slots[:, :, :], slots[:, :, :], 64.0, None, ALU.mult))
                link(TT(hi[:, :, :], hi[:, :, :], slots[:, :, :], ALU.add))
                dve.sem_inc(s["masked"], 1)

        J = 8
        NG = RT // J
        TC = RT // P
        assert NG * J == RT and TC * P == RT and (J + 1) * NB <= 512
        with ExitStack() as st:
            en = sb(st, "edge_rows", [P, 2, TC, P], I32)
            ep = sb(st, "edge_part", [P, TC, P], I32)
            ef = sb(st, "edge_rows_f", [P, 4, TC, P])
            lob = sb(st, "edge_low_rows", [P, TC, P], BF16)
            full = sb(st, "edge_dst", [P, RT])
            hic = sb(st, "edge_dst_high", [P, RT], BF16)
            loc = sb(st, "edge_dst_low", [P, RT], BF16)
            sic = sb(st, "edge_src", [P, RT], I32)
            past = sb(st, "edge_dropped", [P, RT])
            iob = sb(st, "low_ids_s", [P, P], BF16)
            pid = sb(st, "partition_ids", [P, 1])
            zi = sb(st, "zero_int", [P, RT], I32)
            dlo = sb(st, "dst_low_onehot", [P, 2, J, P], BF16)
            dhi = sb(st, "dst_high_onehot", [P, 2, J, NB], BF16)
            dlt = sb(st, "dst_low_onehot_cols", [P, 2, J * P])
            brf = sb(st, "dst_spread", [P, 2, J * P])
            brl = sb(st, "dst_low_spread", [P, 2, J * P], BF16)
            cp = sb(st, "places", [P, 2, (J + 1) * NB])
            r0 = sb(st, "rank_in_tile", [P, 2, J])
            tz = sb(st, "looked_up", [P, 2, J * NB])
            z = sb(st, "rank_before", [P, 2, J])
            po = sb(st, "place", [P, 2, J], I32)
            sv = sb(st, "src_out", [P, 2, J], I32)
            junk = sb(st, "sort_junk", [P, 2, J, P])
            dg = sb(st, "dst_counts", [P, NB])
            cs = sb(st, "block_counts", [P, 2, NB])
            on = sb(st, "ones_nb", [P, NB])
            bad = sb(st, "router_bad", [P, 4])
            ptr = ps(st, "ps_edges", [P, 2, 512])
            pcn = ps(st, "ps_node_counts", [P, 512])
            prs = ps(st, "ps_starts", [P, 2, 64])
            pc = ps(st, "ps_places", [P, 2, 512])
            pz = ps(st, "ps_lookup", [P, 2, 512])
            names = ["in", "ch", "parts", "tabs", "pt_ok", "pt_used", "iota", "dz", "oh", "cnt", "rs_ps", "cp0", "oh2", "cols", "pc", "cp", "pz",
                     "tz", "z", "rk", "po", "r0", "sl0", "fin", "badp", "badr", "cntall"]
            s = {k: sem(f"sort_{k}") for k in names}
            br_in = [sem("sort_spread0"), sem("sort_spread1")]
            sc_ok = [sem("sort_scatter0"), sem("sort_scatter1")]
            block = phase(st)

            @block.sync
            def _(sp):
                for k in range(2):
                    sp.dma_start(en[:, k, :, :], edges[k:k + 1, :].rearrange("k (c t p) -> t (k c) p", p=P, c=TC)).then_inc(s["in"], 16)
                sp.wait_ge(s["parts"], 1)
                sp.dma_start(RDF.rearrange("(c t p) -> t c p", p=P, c=TC), ef[:, 1, :, :]).then_inc(s["tabs"], 16)
                sp.dma_start(RDL.rearrange("(c t p) -> t c p", p=P, c=TC), lob[:, :, :]).then_inc(s["tabs"], 16)
                sp.wait_ge(s["dz"], 1)
                sp.dma_start(SL.rearrange("(p t) c -> p (t c)", p=P), zi[:, :]).then_inc(s["sl0"], 16)
                sp.wait_ge(s["tabs"], 32)

                def spread(g, q, m):
                    if after(g, 2):
                        hold(sp, s["oh2"], g * 11 - 11)
                    sp.dma_start(brf[:, q, :], RDF[bass.ds(g * (J * P), J * P)].partition_broadcast(P)).then_inc(br_in[q], 16)
                    sp.dma_start(brl[:, q, :], RDL[bass.ds(g * (J * P), J * P)].partition_broadcast(P)).then_inc(br_in[q], 16)

                steps(sp, [(0, spread)], NG)
                sp.wait_ge(s["sl0"], 16)

            @block.gpsimd
            def _(pool):
                nc.gpsimd.iota(iob[:, :], pattern=[[1, P]], base=0, channel_multiplier=0, allow_small_or_imprecise_dtypes=True).then_inc(s["iota"], 1)
                nc.gpsimd.iota(pid[:, :], pattern=[[0, 1]], base=0, channel_multiplier=1, allow_small_or_imprecise_dtypes=True).then_inc(s["iota"], 1)
                pool.wait_ge(s["badp"], 1)
                nc.gpsimd.partition_all_reduce(bad[:, 3:4], bad[:, 2:3], P, bass.bass_isa.ReduceOp.max).then_inc(s["badr"], 1)
                pool.wait_ge(s["sl0"], 16)

                def scatter(g, q, m):
                    hold(pool, s["po"], g + 1)
                    for j in range(J):
                        nc.gpsimd.indirect_dma_start(SL, bass.IndirectOffsetOnAxis(ap=po[:, q, j:j + 1], axis=0), sv[:, q, j:j + 1], None,
                                                     bounds_check=RT * P - 1, oob_is_err=False).then_inc(sc_ok[q], 16)

                steps(pool, [(1, scatter)], NG)
                for q in range(2):
                    pool.wait_ge(sc_ok[q], 16 * J * NG // 2)

            @block.vector
            def _(dve):
                link = chain(dve, s["ch"], 0, None)
                TT, TS = nc.vector.tensor_tensor, nc.vector.tensor_scalar
                nc.vector.memset(zi[:, :], 0).then_inc(s["dz"], 1)
                link(nc.vector.memset(on[:, :], 1.0))
                dve.wait_ge(s["in"], 32)
                link(TS(en[:, 0, :, :], en[:, 0, :, :], float(N - 1), None, ALU.min))
                link(TS(en[:, 1, :, :], en[:, 1, :, :], float(NP - 1), None, ALU.min))
                link(nc.vector.tensor_copy(ef[:, 0:2, :, :].rearrange("p a b c -> p (a b c)"), en[:, :, :, :].rearrange("p a b c -> p (a b c)")))
                link(TS(ep[:, :, :], en[:, 1, :, :], 7, None, ALU.logical_shift_right))
                link(nc.vector.tensor_copy(ef[:, 2, :, :], ep[:, :, :]))
                link(TS(ep[:, :, :], en[:, 1, :, :], P - 1, None, ALU.bitwise_and))
                link(nc.vector.tensor_copy(ef[:, 3, :, :], ep[:, :, :]))
                link(nc.vector.tensor_copy(lob[:, :, :], ep[:, :, :]))
                dve.sem_inc(s["parts"], 1)
                dve.wait_ge(s["pt_used"], 4 * TC // 4)
                link(TS(past[:, :], full[:, :], float(N), BIG, ALU.is_ge, ALU.mult))
                dve.wait_ge(s["iota"], 2)

                def onehots(g, q, sem_):
                    cols = lambda t: t[:, bass.ds(g * J, J)].unsqueeze(2)
                    TT(dlo[:, q, :, :], cols(loc).to_broadcast([P, J, P]), iob[:, :].unsqueeze(1).to_broadcast([P, J, P]), ALU.is_equal).then_inc(sem_, 1)
                    TT(dhi[:, q, :, :], cols(hic).to_broadcast([P, J, NB]), iob[:, 0:NB].unsqueeze(1).to_broadcast([P, J, NB]), ALU.is_equal).then_inc(sem_, 1)

                def count(g, q, m):
                    if after(g, 2):
                        hold(dve, s["cnt"], g - 1)
                    onehots(g, q, s["oh"])

                steps(dve, [(0, count)], NG)
                dve.wait_ge(s["cnt"], NG)
                dve.wait_ge(s["cntall"], 1)
                link(nc.vector.memset(dg[:, :], 0.0))
                link(nc.vector.tensor_copy(dg[:, 0:NB - 1], pcn[:, 0:NB - 1]))
                link(nc.vector.tensor_copy(dg[0:LAST, NB - 1:NB], pcn[0:LAST, NB - 1:NB]))
                link(nc.vector.tensor_copy(rdeg[:, :], dg[:, :]))
                link(nc.vector.tensor_reduce(bad[:, 1:2], dg[:, :], AX, ALU.max))
                TS(bad[:, 2:3], bad[:, 1:2], float(RK), None, ALU.is_gt).then_inc(s["badp"], 1)
                dve.wait_ge(s["rs_ps"], 1)
                link(nc.vector.tensor_copy(cs[:, 0, :], prs[:, 1, 0:NB]))
                link(nc.vector.tensor_tensor_scan(cs[:, 1, :], on[:, :], cs[:, 0, :], 0.0, ALU.mult, ALU.add))
                link(TT(cs[:, 1, :], cs[:, 1, :], cs[:, 0, :], ALU.subtract))
                link(TT(cs[:, 0, :], cs[:, 1, :], prs[:, 0, 0:NB], ALU.add))
                link(nc.vector.tensor_copy(rsi2[:, :], cs[:, 0, :]))
                nc.vector.tensor_copy(cp[:, 1, J * NB:(J + 1) * NB], cs[:, 0, :]).then_inc(s["cp0"], 1)
                dve.wait_ge(s["badr"], 1)
                link(nc.vector.tensor_copy(slow[0:1, 1:2], bad[0:1, 3:4]))

                def place(g, q, m):
                    if after(g, 2):
                        hold(dve, s["po"], g - 1)
                        hold(dve, s["pz"], g - 1)
                    hold(dve, br_in[q], m * 32 + 32)
                    onehots(g, q, s["oh2"])
                    TS(dlt[:, q, :], brl[:, q, :], pid[:, 0:1], None, ALU.is_equal).then_inc(s["oh2"], 1)
                    for j in range(J):
                        nc.vector.scalar_tensor_tensor(out=junk[:, q, j, :], in0=brf[:, q, j * P:(j + 1) * P], scalar=fcol(g, j), in1=lower[:, :],
                                                       op0=ALU.is_equal, op1=ALU.mult, accum_out=r0[:, q, j:j + 1]).then_inc(s["oh2"], 1)

                def fcol(g, j):
                    return full[:, bass.ds(g * J + j, 1)]

                def rank(g, q, m):
                    hold(dve, s["pz"], g + 1)
                    hold(dve, s["oh2"], g * 11 + 11)
                    if after(g, 2):
                        hold(dve, sc_ok[q], m * 16 * J)
                    TT(tz[:, q, :], dhi[:, q, :, :].rearrange("p a b -> p (a b)"), pz[:, q, 0:J * NB], ALU.mult).then_inc(s["tz"], 1)
                    nc.vector.tensor_copy(sv[:, q, :], sic[:, bass.ds(g * J, J)]).then_inc(s["tz"], 1)
                    hold(dve, s["tz"], g * 2 + 2)
                    l = chain(dve, s["rk"], g, 3)
                    l(nc.vector.tensor_reduce(z[:, q, :], tz[:, q, :].rearrange("p (a b) -> p a b", a=J), AX, ALU.add))
                    l(TT(z[:, q, :], z[:, q, :], r0[:, q, :], ALU.add))
                    l(TT(z[:, q, :], z[:, q, :], past[:, bass.ds(g * J, J)], ALU.add))
                    nc.vector.tensor_copy(po[:, q, :], z[:, q, :]).then_inc(s["po"], 1)

                steps(dve, [(0, place), (1, rank)], NG)

            @block.scalar
            def _(act):
                n = 0
                for to in (sic, full, hic, loc):
                    for c in range(0, TC, 4):
                        act.wait_ge(s["pt_ok"], n + 1)
                        nc.scalar.copy(to[:, c * P:(c + 4) * P], ptr[:, n % 2, :]).then_inc(s["pt_used"], 1)
                        n += 1

                def places(g, q, m):
                    hold(act, s["pc"], g + 1)
                    if after(g, 2):
                        hold(act, s["pz"], g - 1)
                    nc.scalar.copy(cp[:, q, :], pc[:, q, 0:(J + 1) * NB]).then_inc(s["cp"], 1)

                steps(act, [(0, places)], NG)

            @block.tensor
            def _(pe):
                pe.wait_ge(s["parts"], 1)
                n = 0
                for k in range(4):
                    for c in range(0, TC, 4):
                        if n >= 2:
                            pe.wait_ge(s["pt_used"], n - 1)
                        for i in range(4):
                            mm = nc.tensor.transpose(ptr[:, n % 2, i * P:(i + 1) * P], ef[:, k, c + i, :], ident[:, :])
                        mm.then_inc(s["pt_ok"], 1)
                        n += 1
                nc.tensor.matmul(pcn[:, 0:NB], ident[:, :], zero[:, 0:NB], start=True, stop=True, skip_group_check=True)

                def count(g, q, m):
                    hold(pe, s["oh"], g * 2 + 2)
                    for j in range(J):
                        mm = nc.tensor.matmul(pcn[:, 0:NB], dlo[:, q, j, :], dhi[:, q, j, :], start=False, stop=True, skip_group_check=True)
                    mm.then_inc(s["cnt"], 1)

                steps(pe, [(0, count)], NG)
                pe.drain().then_inc(s["cntall"], 1)
                pe.wait_ge(s["badp"], 1)
                nc.tensor.matmul(prs[:, 0, 0:NB], upper[:, :], dg[:, :], start=True, stop=True)
                nc.tensor.matmul(prs[:, 1, 0:NB], ones[:, :], dg[:, :], start=True, stop=True).then_inc(s["rs_ps"], 1)
                pe.wait_ge(s["cp0"], 1)

                def prefix(g, q, m):
                    if after(g, 1):
                        hold(pe, s["cp"], g)
                    hold(pe, s["oh2"], g * 11 + 2)
                    nc.tensor.matmul(pc[:, q, 0:(J + 1) * NB].rearrange("p (a b) -> p a b", b=NB), ident[:, :],
                                     cp[:, 1 - q, J * NB:(J + 1) * NB].unsqueeze(1).to_broadcast([P, J + 1, NB]), start=True, stop=True, skip_group_check=True)
                    for j in range(J):
                        mm = nc.tensor.matmul(pc[:, q, (j + 1) * NB:(J + 1) * NB].rearrange("p (a b) -> p a b", b=NB), dlo[:, q, j, :],
                                              dhi[:, q, j:j + 1, :].to_broadcast([P, J - j, NB]), start=False, stop=True, skip_group_check=True)
                    mm.then_inc(s["pc"], 1)

                def lookup(g, q, m):
                    hold(pe, s["cp"], g + 1)
                    hold(pe, s["oh2"], g * 11 + 3)
                    if after(g, 2):
                        hold(pe, s["po"], g - 1)
                    for j in range(J):
                        mm = nc.tensor.matmul(pz[:, q, j * NB:(j + 1) * NB], dlt[:, q, j * P:(j + 1) * P], cp[:, q, j * NB:(j + 1) * NB], start=True, stop=True)
                    mm.then_inc(s["pz"], 1)

                steps(pe, [(0, prefix), (1, lookup)], NG)

        UP, DOWN = 1024.0, 2048.0
        G = 8
        ROUNDS = P // G
        with ExitStack() as st:
            xhl = sb(st, "x_parts", [P, NB, 2 * D], F16)
            xq = sb(st, "x_chunk", [P, 2, 2, D])
            xd = sb(st, "x_rest", [P, 2, D])
            at = sb(st, "counts", [P, 2, P, 2 * NB], F16)
            ohl = sb(st, "low_onehot", [P, 2, 2 * G, P], BF16)
            ohh = sb(st, "high_onehot", [P, 2, 2 * G, 2 * NB], BF16)
            iol = sb(st, "low_ids", [P, P], BF16)
            hs = sb(st, "sum_high", [P, 2, D])
            ns = sb(st, "sums", [P, 2, D])
            pb = ps(st, "ps_counts", [P, 2, 2, 512])
            pm = ps(st, "ps_sums", [P, 2, 512])
            names = ["iota", "xhi", "xd", "xlo", "hz", "oh", "cnt_ps", "cnt_ok", "sum_ps", "hs", "ns", "deg_out"]
            s = {k: sem(f"sum_{k}f") for k in names}
            x_in = [sem("sum_x_in0"), sem("sum_x_in1")]
            ns_out = [sem("sum_out0"), sem("sum_out1")]
            block = phase(st)
            XC = 2
            assert (NB + 1) % XC == 0

            def xcols(c):
                return c * XC, min((c + 1) * XC, NB)

            NX = (NB + 1) // XC

            @block.sync
            def _(sp):
                for c in range(NX):
                    a, b = xcols(c)
                    if c >= 2:
                        sp.wait_ge(s["xlo"], c - 1)
                    sp.dma_start(xq[:, c % 2, 0:b - a, :], by_block(XN[a * P:b * P, :])).then_inc(x_in[c % 2], 16)
                with nc.allow_non_contiguous_dma(reason="a column of degrees"):
                    sp.dma_start(ACC[:, D:D + 1].rearrange("(b p) c -> p b c", p=P), deg[:, :].unsqueeze(2)).then_inc(s["deg_out"], 16)

                def store(m, q, h):
                    for j in range(2):
                        hold(sp, s["ns"], m * 2 + (j + 1))
                        sp.dma_start(ACC[bass.ds((m * 2 + j) * P, P), 0:D], ns[:, j, :]).then_inc(ns_out[j], 16)

                steps(sp, [(0, store)], NPAIR)
                for j in range(2):
                    sp.wait_ge(ns_out[j], 16 * NPAIR)
                sp.wait_ge(s["deg_out"], 16)

            @block.gpsimd
            def _(pool):
                nc.gpsimd.iota(iol[:, :], pattern=[[1, P]], base=0, channel_multiplier=0, allow_small_or_imprecise_dtypes=True).then_inc(s["iota"], 1)

            @block.vector
            def _(dve):
                for q in range(2):
                    nc.vector.memset(ohh[:, q, :, :], 0.0).then_inc(s["hz"], 1)
                for c in range(NX):
                    a, b = xcols(c)
                    dve.wait_ge(s["xhi"], c + 1)
                    if c >= 1:
                        dve.wait_ge(s["xlo"], c)
                    nc.vector.scalar_tensor_tensor(out=xd[:, 0:b - a, :], in0=xq[:, c % 2, 0:b - a, :], scalar=UP, in1=xhl[:, a:b, 0:D],
                                                   op0=ALU.mult, op1=ALU.subtract).then_inc(s["xd"], 1)
                dve.wait_ge(s["iota"], 1)
                dve.wait_ge(s["hz"], 2)

                def onehots(m, q, h):
                    for g in range(ROUNDS // 2):
                        u = g % 2
                        if after(m, 1) or g >= 2:
                            hold(dve, s["cnt_ps"], m * ROUNDS + 2 * (g - 1))
                        cols = lambda t, a, b: t[a:b, bass.ds(m, 1), g * 2 * G:(g + 1) * 2 * G].rearrange("p a b -> p (a b)").unsqueeze(2)
                        nc.vector.tensor_tensor(ohl[:, u, :, :], cols(lot, 0, P).to_broadcast([P, 2 * G, P]),
                                                iol[:, :].unsqueeze(1).to_broadcast([P, 2 * G, P]), ALU.is_equal).then_inc(s["oh"], 1)
                        for j in range(2):
                            a, b = j * SLOT, (j + 1) * SLOT
                            nc.vector.tensor_tensor(ohh[a:b, u, :, j * NB:(j + 1) * NB], cols(hit, a, b).to_broadcast([SLOT, 2 * G, NB]),
                                                    iol[a:b, 0:NB].unsqueeze(1).to_broadcast([SLOT, 2 * G, NB]), ALU.is_equal).then_inc(s["oh"], 1)

                def sums(m, q, h):
                    for j in range(2):
                        hold(dve, s["hs"], m * 2 + (j + 1))
                        if after(m, 1):
                            hold(dve, ns_out[j], m * 16)
                        nc.vector.scalar_tensor_tensor(out=ns[:, j, :], in0=pm[:, j, D:2 * D], scalar=1.0 / (UP * DOWN), in1=hs[:, j, :],
                                                       op0=ALU.mult, op1=ALU.add).then_inc(s["ns"], 1)

                steps(dve, [(0, onehots), (1, sums)], NPAIR)

            @block.scalar
            def _(act):
                for c in range(NX):
                    a, b = xcols(c)
                    act.wait_ge(x_in[c % 2], 16 * (c // 2 + 1))
                    nc.scalar.activation(xhl[:, a:b, 0:D], xq[:, c % 2, 0:b - a, :], ACT.Copy, scale=UP).then_inc(s["xhi"], 1)
                    act.wait_ge(s["xd"], c + 1)
                    nc.scalar.activation(xhl[:, a:b, D:2 * D], xd[:, 0:b - a, :], ACT.Copy, scale=DOWN).then_inc(s["xlo"], 1)

                def counts(m, q, h):
                    if after(m, 2):
                        hold(act, s["sum_ps"], m * 2 - 2)
                    for g in range(ROUNDS):
                        hold(act, s["cnt_ps"], m * ROUNDS + (g + 1))
                        nc.scalar.copy(at[:, q, g * G:(g + 1) * G, :].rearrange("p (k a) b -> p k (a b)", k=2),
                                       pb[:, g % 2, :, 0:G * NB]).then_inc(s["cnt_ok"], 1)

                def highs(m, q, h):
                    for j in range(2):
                        hold(act, s["sum_ps"], m * 2 + (j + 1))
                        if after(m, 1):
                            hold(act, s["ns"], m * 2 + (j - 1))
                        nc.scalar.activation(hs[:, j, :], pm[:, j, 0:D], ACT.Copy, scale=1.0 / UP).then_inc(s["hs"], 1)

                steps(act, [(0, counts), (1, highs)], NPAIR)

            @block.tensor
            def _(pe):
                pe.wait_ge(s["xlo"], NX)

                def build(g):
                    def body(m, q, h):
                        if g % 2 == 0:
                            hold(pe, s["oh"], (m * (ROUNDS // 2) + (g // 2)) * 3 + 3)
                        if after(m, 1) or g >= 2:
                            hold(pe, s["cnt_ok"], m * ROUNDS + (g - 1))
                        for i in range(G):
                            c, u = (g % 2) * G + i, (g // 2) % 2
                            w = i % (G // 2) * 2 * NB
                            mm = nc.tensor.matmul(pb[:, g % 2, i // (G // 2), w:w + 2 * NB], ohl[:, u, c, :], ohh[:, u, c, :], start=True, stop=True)
                        mm.then_inc(s["cnt_ps"], 1)
                    return body

                def multiply(g):
                    def body(m, q, h):
                        if g == 0:
                            hold(pe, s["cnt_ok"], m * ROUNDS + ROUNDS)
                        for n in range(2 * NB * g // ROUNDS, 2 * NB * (g + 1) // ROUNDS):
                            j, k = n // NB, n % NB
                            if k == 0 and after(m, 1):
                                hold(pe, s["ns"], m * 2 + (j - 1))
                            mm = nc.tensor.matmul(pm[:, j, :], at[:, q, :, j * NB + k], xhl[:, k, :], start=k == 0, stop=k == NB - 1)
                            if k == NB - 1:
                                mm.then_inc(s["sum_ps"], 1)
                    return body

                steps(pe, [x for g in range(ROUNDS) for x in ((0, build(g)), (1, multiply(g)))], NPAIR)

        gst.close()

        edge_pass("sum")

        X = sb(top, "x1_rows", [P, NB, D])
        with ExitStack() as st:
            nm = sb(st, "neigh_rows", [P, 2, D + 1])
            xr = sb(st, "x_again", [P, 2, D])
            nt = sb(st, "neigh_cols", [P, 2, KD * P])
            r1 = sb(st, "gnn_rows", [P, 2, D])
            r2 = sb(st, "gnn_squares", [P, 2, D])
            u1 = sb(st, "mix_rows", [P, 2, D])
            nr = sb(st, "norms", [P, 2, 6])
            bs = sb(st, "ln_stats", [P, 2, 6])
            mv = sb(st, "ln_mean_var", [P, 2, 2])
            xn = sb(st, "x1_normed", [P, 2, D])
            xts = sb(st, "x_cols_stage2", [P, 2, KD * P])
            xt1 = sb(st, "x1_cols_stage", [P, 2, KD * P])
            ta = sb(st, "att_products", [P, NB, GW])
            pt = ps(st, "ps_turn", [P, 2, 512])
            pg = ps(st, "ps_node", [P, 2, 512])
            p1 = ps(st, "ps_turn_x1", [P, 2, 512])
            ph = ps(st, "ps_router", [P, 2, 512])
            nin = [sem("node_in0"), sem("node_in1")]
            names = ["mean", "nt_ps", "nt_ok", "g_ok", "r_ok", "u_ok", "ss", "nrm", "x1", "vps", "std", "xn", "xt_ps",
                     "xt_ok", "h_ps", "h_ok", "cA", "cB", "cC", "cD", "cE", "xts", "kept"]
            s = {k: sem(f"node_{k}") for k in names}
            block = phase(st)

            @block.sync
            def _(sp):
                def load(b, q, m):
                    if after(b, 2):
                        hold(sp, s["nt_ps"], b - 1)
                        hold(sp, s["u_ok"], b - 1)
                    sp.dma_start(nm[:, q, :], ACC[bass.ds(b * P, P), :]).then_inc(nin[q], 16)
                    sp.dma_start(xr[:, q, :], XP[bass.ds(b * P, P), :]).then_inc(nin[q], 16)

                steps(sp, [(0, load)], NB)

            @block.gpsimd
            def _(pool):
                def stage(b, q, m):
                    if after(b, 2):
                        hold(pool, s["g_ok"], b - 1)
                    nc.gpsimd.tensor_copy(xts[:, q, :].rearrange("p (k n) -> p k n", k=KD), XT[:, :, bass.ds(b * P, P)]).then_inc(s["xts"], 1)

                def keep(b, q, m):
                    hold(pool, s["xt_ok"], b + 1)
                    hold(pool, s["xts"], b + 1)
                    nc.gpsimd.tensor_copy(XT[:, :, bass.ds(b * P, P)], xt1[:, q, :].rearrange("p (k n) -> p k n", k=KD)).then_inc(s["kept"], 1)

                steps(pool, [(0, stage), (4, keep)], NB)

            @block.tensor
            def _(pe):
                def turn(b, q, m):
                    hold(pe, s["mean"], b + 1)
                    if after(b, 2):
                        hold(pe, s["nt_ok"], b - 1)
                    for k in range(KD):
                        mm = nc.tensor.transpose(pt[:, q, k * P:(k + 1) * P], nm[:, q, k * P:(k + 1) * P], ident[:, :])
                    mm.then_inc(s["nt_ps"], 1)

                def node(b, q, m):
                    hold(pe, s["nt_ok"], b + 1)
                    hold(pe, s["xts"], b + 1)
                    if after(b, 2):
                        hold(pe, s["u_ok"], b - 1)
                    for k in range(KD):
                        nc.tensor.matmul(pg[:, q, 0:D], xts[:, q, k * P:(k + 1) * P], wg[:, k, :], start=k == 0, stop=False)
                    for k in range(KD):
                        nc.tensor.matmul(pg[:, q, 0:D], nt[:, q, k * P:(k + 1) * P], wg[:, KD + k, :], start=False, stop=k == KD - 1)
                    for k in range(KD):
                        mm = nc.tensor.matmul(pg[:, q, D:2 * D], xts[:, q, k * P:(k + 1) * P], mix[:, k, :], start=k == 0, stop=k == KD - 1)
                    mm.then_inc(s["g_ok"], 1)

                def turn_x1(b, q, m):
                    hold(pe, s["xn"], b + 1)
                    if after(b, 2):
                        hold(pe, s["xt_ok"], b - 1)
                    for k in range(KD):
                        mm = nc.tensor.transpose(p1[:, q, k * P:(k + 1) * P], xn[:, q, k * P:(k + 1) * P], ident[:, :])
                    mm.then_inc(s["xt_ps"], 1)

                def router(b, q, m):
                    hold(pe, s["xt_ok"], b + 1)
                    if after(b, 2):
                        hold(pe, s["h_ok"], b - 1)
                    for k in range(KD):
                        mm = nc.tensor.matmul(ph[:, q, 0:GW], xt1[:, q, k * P:(k + 1) * P], wgat[:, k, :], start=k == 0, stop=k == KD - 1)
                    mm.then_inc(s["h_ps"], 1)

                steps(pe, [(0, turn), (1, node), (3, turn_x1), (4, router)], NB)

            @block.scalar
            def _(act):
                def columns(b, q, m):
                    hold(act, s["nt_ps"], b + 1)
                    if after(b, 2):
                        hold(act, s["g_ok"], b - 1)
                    nc.scalar.copy(nt[:, q, :], pt[:, q, 0:KD * P]).then_inc(s["nt_ok"], 1)

                def norms(b, q, m):
                    hold(act, s["r_ok"], b + 1)
                    nc.scalar.activation(r2[:, q, :], r1[:, q, :], ACT.Square, accum_out=nr[:, q, 0:1]).then_inc(s["ss"], 1)
                    hold(act, s["ss"], b + 1)
                    nc.scalar.activation(nr[:, q, 1:2], nr[:, q, 0:1], ACT.Sqrt).then_inc(s["nrm"], 1)

                def stds(b, q, m):
                    hold(act, s["vps"], b + 1)
                    nc.scalar.activation(nr[:, q, 4:5], nr[:, q, 5:6], ACT.Sqrt).then_inc(s["std"], 1)

                def columns_x1(b, q, m):
                    hold(act, s["xt_ps"], b + 1)
                    if after(b, 2):
                        hold(act, s["h_ps"], b - 1)
                        hold(act, s["kept"], b - 1)
                    nc.scalar.copy(xt1[:, q, :], p1[:, q, 0:KD * P]).then_inc(s["xt_ok"], 1)

                steps(act, [(0, columns), (1, norms), (2, stds), (3, columns_x1)], NB)

            @block.vector
            def _(dve):
                def mean(b, q, m):
                    hold(dve, nin[q], m * 32 + 32)
                    link = chain(dve, s["cA"], b, 2)
                    link(nc.vector.tensor_scalar(nm[:, q, D:D + 1], nm[:, q, D:D + 1], 1.0, None, ALU.max))
                    link(nc.vector.reciprocal(nm[:, q, D:D + 1], nm[:, q, D:D + 1]))
                    nc.vector.tensor_scalar(nm[:, q, 0:D], nm[:, q, 0:D], nm[:, q, D:D + 1], None, ALU.mult).then_inc(s["mean"], 1)

                def rows(b, q, m):
                    hold(dve, s["g_ok"], b + 1)
                    if after(b, 2):
                        hold(dve, s["ss"], b - 1)
                        hold(dve, s["x1"], b - 1)
                    link = chain(dve, s["cB"], b, 2)
                    link(nc.vector.tensor_tensor(r1[:, q, :], pg[:, q, 0:D], bg[:, :], ALU.add))
                    nc.vector.tensor_scalar(r1[:, q, :], r1[:, q, :], 0.0, None, ALU.max).then_inc(s["r_ok"], 1)
                    link(nc.vector.tensor_tensor(u1[:, q, :], pg[:, q, D:2 * D], xr[:, q, :], ALU.add))
                    nc.vector.tensor_tensor(u1[:, q, :], u1[:, q, :], bo[:, :], ALU.add).then_inc(s["u_ok"], 1)

                def update(b, q, m):
                    hold(dve, s["nrm"], b + 1)
                    hold(dve, s["u_ok"], b + 1)
                    link = chain(dve, s["cC"], b, 4)
                    link(nc.vector.tensor_scalar(nr[:, q, 2:3], nr[:, q, 1:2], GNN_EPS, None, ALU.max))
                    link(nc.vector.reciprocal(nr[:, q, 3:4], nr[:, q, 2:3]))
                    x1 = X[:, bass.ds(b, 1), :].rearrange("p a b -> p (a b)")
                    nc.vector.scalar_tensor_tensor(out=x1, in0=r1[:, q, :], scalar=nr[:, q, 3:4], in1=u1[:, q, :], op0=ALU.mult, op1=ALU.add).then_inc(s["x1"], 1)
                    hold(dve, s["x1"], b + 1)
                    link(nc.vector.bn_stats(bs[:, q, :], x1))
                    link(nc.vector.bn_aggr(mv[:, q, :], bs[:, q, :]))
                    nc.vector.tensor_scalar(nr[:, q, 5:6], mv[:, q, 1:2], LN_EPS, None, ALU.add).then_inc(s["vps"], 1)

                def norm(b, q, m):
                    hold(dve, s["std"], b + 1)
                    if after(b, 2):
                        hold(dve, s["xt_ps"], b - 1)
                    link = chain(dve, s["cD"], b, 1)
                    link(nc.vector.reciprocal(nr[:, q, 4:5], nr[:, q, 4:5]))
                    x1 = X[:, bass.ds(b, 1), :].rearrange("p a b -> p (a b)")
                    nc.vector.tensor_scalar(xn[:, q, :], x1, mv[:, q, 0:1], nr[:, q, 4:5], ALU.subtract, ALU.mult).then_inc(s["xn"], 1)

                def router(b, q, m):
                    hold(dve, s["h_ps"], b + 1)
                    nc.vector.tensor_copy(T[:, bass.ds(b, 1), 0:GW].rearrange("p a b -> p (a b)"), ph[:, q, 0:GW]).then_inc(s["h_ok"], 1)

                steps(dve, [(0, mean), (1, rows), (2, update), (3, norm), (4, router)], NB)
                dve.wait_ge(s["h_ok"], NB)
                n = 0
                for k, to in ((0, T[:, :, GW:PAY]), (1, AD[:, :, :])):
                    nc.vector.tensor_tensor(ta[:, :, :], T[:, :, 0:GW], att[:, k, :].unsqueeze(1).to_broadcast([P, NB, GW]), ALU.mult).then_inc(s["cE"], 1)
                    n += 1
                    dve.wait_ge(s["cE"], n)
                    nc.vector.tensor_reduce(to, ta[:, :, :].rearrange("p b (h e) -> p b h e", e=NE), AX, ALU.add).then_inc(s["cE"], 1)
                    n += 1
                    dve.wait_ge(s["cE"], n)

        with ExitStack() as st:
            out_ok = sem("table_out")
            block = phase(st)

            @block.sync
            def _(sp):
                sp.dma_start(by_block(TAB), T[:, :, :]).then_inc(out_ok, 16)
                sp.wait_ge(out_ok, 16)

        CT = 16
        NCT = RT // CT
        with ExitStack() as st:
            ix = sb(st, "gather_index", [P, 2, CT], I32)
            gb_ = sb(st, "gather_rows", [P, 2, CT, PAY])
            ix_in = [sem("gather_ix0"), sem("gather_ix1")]
            got = [sem("gather_got0"), sem("gather_got1")]
            outs = [sem("gather_out0"), sem("gather_out1")]
            tail = sem("gather_tail")
            block = phase(st)

            @block.sync
            def _(sp):
                for i in range(4):
                    sp.dma_start(GD[RT * P:, :].rearrange("(p a) c -> p a c", p=P)[:, i * RK // 4:(i + 1) * RK // 4, :],
                                 zero[:, 0:RK // 4 * PAY]).then_inc(tail, 16)

                def load(c, q, m):
                    if after(c, 2):
                        hold(sp, got[q], m * 16 * CT)
                    sp.dma_start(ix[:, q, :], SL[bass.ds(c * (CT * P), CT * P), :].rearrange("(p a) c -> p (a c)", p=P)).then_inc(ix_in[q], 16)

                def store(c, q, m):
                    hold(sp, got[q], m * 16 * CT + 16 * CT)
                    sp.dma_start(GD[bass.ds(c * (CT * P), CT * P), :].rearrange("(p a) c -> p (a c)", p=P),
                                 gb_[:, q, :, :].rearrange("p a c -> p (a c)")).then_inc(outs[q], 16)

                steps(sp, [(0, load), (1, store)], NCT)
                for q in range(2):
                    sp.wait_ge(outs[q], 16 * NCT // 2)
                sp.wait_ge(tail, 64)

            @block.gpsimd
            def _(pool):
                def gather(c, q, m):
                    hold(pool, ix_in[q], m * 16 + 16)
                    if after(c, 2):
                        hold(pool, outs[q], m * 16)
                    for j in range(CT):
                        nc.gpsimd.indirect_dma_start(gb_[:, q, j, :], None, TAB, bass.IndirectOffsetOnAxis(ap=ix[:, q, j:j + 1], axis=0)).then_inc(got[q], 16)

                steps(pool, [(0, gather)], NCT)

        with ExitStack() as st:
            pg = sb(st, "node_rows", [P, 2, C, RK * PAY])
            sc = sb(st, "slot_scores", [P, C, RK, GH])
            sc2 = sb(st, "slot_scores2", [P, C, RK, GH])
            vm = sb(st, "slot_mask", [P, C, RK])
            kio = sb(st, "slot_ids_r", [P, RK])
            mx2 = sb(st, "node_slope", [P, C, GH])
            a_in = [sem("att_in0"), sem("att_in1")]
            a_ch, a_io, a_z, a_e, a_done = sem("att_ch"), sem("att_io"), sem("att_z"), sem("att_e"), sem("att_done")
            block = phase(st)

            @block.gpsimd
            def _(pool):
                nc.gpsimd.iota(kio[:, :], pattern=[[1, RK]], base=0, channel_multiplier=0, allow_small_or_imprecise_dtypes=True).then_inc(a_io, 1)
                for c in range(NC):
                    if c >= 2:
                        pool.wait_ge(a_done, c - 1)
                    for i in range(C):
                        nc.gpsimd.indirect_dma_start(pg[:, c % 2, i, :], None, GD, bass.IndirectOffsetOnAxis(ap=rsi2[:, c * C + i:c * C + i + 1], axis=0)).then_inc(a_in[c % 2], 16)

            @block.scalar
            def _(act):
                for c in range(NC):
                    act.wait_ge(a_z, c + 1)
                    nc.scalar.activation(sc2[:, :, :, :], sc[:, :, :, :], ACT.Exp).then_inc(a_e, 1)

            @block.vector
            def _(dve):
                link = chain(dve, a_ch, 0, None)
                TT, TS = nc.vector.tensor_tensor, nc.vector.tensor_scalar
                dve.wait_ge(a_io, 1)
                for c in range(NC):
                    q, bl = c % 2, slice(c * C, (c + 1) * C)
                    rows = pg[:, q, :, :].rearrange("p b (k c) -> p (b k) c", c=PAY)
                    s1, s2 = (t[:, :, :, :].rearrange("p b k h -> p (b k) h") for t in (sc, sc2))
                    last = lambda t: t.rearrange("p b k h -> p b h k")
                    slot = lambda t: t.unsqueeze(2).to_broadcast([P, C, RK, GH])
                    link(TT(vm[:, :, :], kio[:, :].unsqueeze(1).to_broadcast([P, C, RK]), rdeg[:, bl].unsqueeze(2).to_broadcast([P, C, RK]), ALU.is_ge))
                    link(TS(vm[:, :, :], vm[:, :, :], LOW, None, ALU.mult))
                    dve.wait_ge(a_in[q], 16 * C * (c // 2 + 1))
                    link(TT(s1, rows[:, :, GW:PAY], vm[:, :, :].rearrange("p b k -> p (b k)").unsqueeze(2).to_broadcast([P, C * RK, GH]), ALU.add))
                    link(nc.vector.tensor_reduce(MXS[:, bl, :], last(sc[:, :, :, :]), AX, ALU.max))
                    link(TT(MXS[:, bl, :], MXS[:, bl, :], T[:, bl, GW:PAY], ALU.max))
                    link(TT(MXS[:, bl, :], MXS[:, bl, :], AD[:, bl, :], ALU.add))
                    link(TS(mx2[:, :, :], MXS[:, bl, :], SLOPE, None, ALU.mult))
                    link(TT(MXS[:, bl, :], MXS[:, bl, :], mx2[:, :, :], ALU.max))
                    link(TT(sc[:, :, :, :], sc[:, :, :, :], slot(AD[:, bl, :]), ALU.add))
                    link(TS(s2, s1, SLOPE, None, ALU.mult))
                    link(TT(s1, s1, s2, ALU.max))
                    TT(sc[:, :, :, :], sc[:, :, :, :], slot(MXS[:, bl, :]), ALU.subtract).then_inc(a_z, 1)
                    dve.wait_ge(a_e, c + 1)
                    link(nc.vector.tensor_reduce(ag[:, bl, GW:PAY], last(sc2[:, :, :, :]), AX, ALU.add))
                    hv = rows[:, :, 0:GW].rearrange("p r (h e) -> p r h e", e=NE)
                    link(TT(hv, hv, s2.unsqueeze(3).to_broadcast([P, C * RK, GH, NE]), ALU.mult))
                    nc.vector.tensor_reduce(ag[:, bl, 0:GW], pg[:, q, :, :].rearrange("p b (k c) -> p b c k", c=PAY)[:, :, 0:GW, :], AX, ALU.add).then_inc(a_done, 1)
                    dve.wait_ge(a_done, c + 1)

        edge_pass("max")

        with ExitStack() as st:
            ms = sb(st, "score_max", [P, NB, 2 * GH])
            m2 = sb(st, "score_slope", [P, NB, GH])
            m_in, m_ch, m_out = sem("shift_in"), sem("shift_chain"), sem("shift_out")
            block = phase(st)

            @block.sync
            def _(sp):
                with where(sp, 1):
                    sp.dma_start(MXS[:, :, :], by_block(MAXT)).then_inc(m_in, 16)
                    sp.wait_ge(m_ch, 6)
                    sp.dma_start(by_block(MD), ms[:, :, :]).then_inc(m_out, 16)
                    sp.wait_ge(m_out, 16)

            @block.vector
            def _(dve):
                with where(dve, 1):
                    dve.wait_ge(m_in, 16)
                    link = chain(dve, m_ch, 0, 6)
                    link(nc.vector.tensor_tensor(MXS[:, :, :], MXS[:, :, :], T[:, :, GW:PAY], ALU.max))
                    link(nc.vector.tensor_tensor(MXS[:, :, :], MXS[:, :, :], AD[:, :, :], ALU.add))
                    link(nc.vector.tensor_scalar(m2[:, :, :], MXS[:, :, :], SLOPE, None, ALU.mult))
                    link(nc.vector.tensor_tensor(MXS[:, :, :], MXS[:, :, :], m2[:, :, :], ALU.max))
                    link(nc.vector.tensor_copy(ms[:, :, 0:GH], AD[:, :, :]))
                    link(nc.vector.tensor_copy(ms[:, :, GH:2 * GH], MXS[:, :, :]))

        edge_pass("soft")

        with ExitStack() as st:
            ag_in = sem("general_in")
            block = phase(st)

            @block.sync
            def _(sp):
                with where(sp, 1):
                    sp.dma_start(ag[:, :, :], by_block(AGG)).then_inc(ag_in, 16)
                    sp.wait_ge(ag_in, 16)

        with ExitStack() as st:
            z = sb(st, "own_score", [P, NB, 2, GH])
            y = sb(st, "router_out", [P, NB, GW])
            y2 = sb(st, "router_sq", [P, NB, GW])
            v = sb(st, "router_stats", [P, 4, NB])
            sc = sb(st, "expert_scores", [P, NB, NE])
            rk = sb(st, "expert_ranks", [P, NB, NE])
            cm = sb(st, "expert_compare", [P, NB, NE])
            g_in, g_ch, e1, e2, q1 = sem("gate_in"), sem("gate_chain"), sem("gate_exp1"), sem("gate_exp2"), sem("gate_sqrt")
            a1, a2, a3 = sem("gate_at_exp1"), sem("gate_at_exp2"), sem("gate_at_sqrt")
            block = phase(st)

            @block.scalar
            def _(act):
                act.wait_ge(a1, 1)
                nc.scalar.activation(z[:, :, 0, :], z[:, :, 1, :], ACT.Exp).then_inc(e1, 1)
                act.wait_ge(a3, 1)
                nc.scalar.activation(v[:, 3, :], v[:, 2, :], ACT.Sqrt).then_inc(q1, 1)
                act.wait_ge(a2, 1)
                nc.scalar.activation(sc[:, :, :], cm[:, :, :], ACT.Exp).then_inc(e2, 1)

            @block.vector
            def _(dve):
                link = chain(dve, g_ch, 0, None)
                TT, TS = nc.vector.tensor_tensor, nc.vector.tensor_scalar
                heads = lambda t: t.rearrange("p b (h e) -> p b h e", e=NE)
                wide = lambda t, n: t.unsqueeze(len(t.shape)).to_broadcast([*t.shape, n])
                link(TT(z[:, :, 0, :], T[:, :, GW:PAY], AD[:, :, :], ALU.add))
                link(TS(z[:, :, 1, :], z[:, :, 0, :], SLOPE, None, ALU.mult))
                link(TT(z[:, :, 0, :], z[:, :, 0, :], z[:, :, 1, :], ALU.max))
                TT(z[:, :, 1, :], z[:, :, 0, :], MXS[:, :, :], ALU.subtract).then_inc(a1, 1)
                dve.wait_ge(e1, 1)
                link(TT(heads(y[:, :, :]), heads(T[:, :, 0:GW]), wide(z[:, :, 0, :], NE), ALU.mult))
                link(TT(y[:, :, :], y[:, :, :], ag[:, :, 0:GW], ALU.add))
                link(TT(z[:, :, 1, :], z[:, :, 0, :], ag[:, :, GW:PAY], ALU.add))
                link(TS(z[:, :, 1, :], z[:, :, 1, :], DEN_EPS, None, ALU.add))
                link(nc.vector.reciprocal(z[:, :, 0, :], z[:, :, 1, :]))
                link(TT(heads(y[:, :, :]), heads(y[:, :, :]), wide(z[:, :, 0, :], NE), ALU.mult))
                row = lambda k: gb[:, k, :].unsqueeze(1).to_broadcast([P, NB, GW])
                link(TT(y[:, :, :], y[:, :, :], row(0), ALU.add))
                link(nc.vector.tensor_reduce(v[:, 0, :], y[:, :, :], AX, ALU.add))
                link(TS(v[:, 1, :], v[:, 0, :], 1.0 / GW, None, ALU.mult))
                link(TT(y[:, :, :], y[:, :, :], wide(v[:, 1, :], GW), ALU.subtract))
                link(TT(y2[:, :, :], y[:, :, :], y[:, :, :], ALU.mult))
                link(nc.vector.tensor_reduce(v[:, 0, :], y2[:, :, :], AX, ALU.add))
                TS(v[:, 2, :], v[:, 0, :], 1.0 / GW, LN_EPS, ALU.mult, ALU.add).then_inc(a3, 1)
                dve.wait_ge(q1, 1)
                link(nc.vector.reciprocal(v[:, 0, :], v[:, 3, :]))
                link(TT(y[:, :, :], y[:, :, :], wide(v[:, 0, :], GW), ALU.mult))
                link(TT(y[:, :, :], y[:, :, :], row(1), ALU.mult))
                link(TT(y[:, :, :], y[:, :, :], row(2), ALU.add))
                link(nc.vector.tensor_reduce(sc[:, :, :], y[:, :, :].rearrange("p b (h e) -> p b e h", e=NE), AX, ALU.add))
                link(TS(sc[:, :, :], sc[:, :, :], 1.0 / GH, None, ALU.mult))
                link(nc.vector.memset(rk[:, :, :], 0.0))
                for j in range(NE):
                    for a, b, op in ((0, j, ALU.is_gt), (j + 1, NE, ALU.is_ge)):
                        if a < b:
                            link(TT(cm[:, :, a:b], sc[:, :, j:j + 1].to_broadcast([P, NB, b - a]), sc[:, :, a:b], op))
                            link(TT(rk[:, :, a:b], rk[:, :, a:b], cm[:, :, a:b], ALU.add))
                link(TS(rk[:, :, :], rk[:, :, :], 1.5, None, ALU.is_lt))
                link(nc.vector.tensor_reduce(v[:, 0, :], sc[:, :, :], AX, ALU.max))
                TT(cm[:, :, :], sc[:, :, :], wide(v[:, 0, :], NE), ALU.subtract).then_inc(a2, 1)
                dve.wait_ge(e2, 1)
                link(TT(gate[:, :, :], sc[:, :, :], rk[:, :, :], ALU.mult))
                link(nc.vector.tensor_reduce(v[:, 1, :], gate[:, :, :], AX, ALU.add))
                link(nc.vector.reciprocal(v[:, 2, :], v[:, 1, :]))
                link(TT(gate[:, :, :], gate[:, :, :], wide(v[:, 2, :], NE), ALU.mult))

        with ExitStack() as st:
            w1s = sb(st, "w1_sb", [P, KD, NE, FF])
            w2s = sb(st, "w2_sb", [P, HT, D])
            b1r = sb(st, "b1_rows", [HT, P])
            b1c = sb(st, "b1_cols", [P, HT])
            b2r = sb(st, "b2_row", [1, NE * D])
            one = sb(st, "ones", [1, P])
            hid = sb(st, "hidden", [P, 2, HT * P])
            phid = ps(st, "ps_hidden", [P, 4, 512])
            py = ps(st, "ps_expert_out", [P, 2, NE * D])
            names = ["b1_ps", "b1_ok", "one", "chain", "hps0", "hps1", "hps2", "hps3", "hid", "y_ps", "y_ok", "hb0", "hb1", "hb2", "hb3"]
            s = {k: sem(f"expert_{k}") for k in names}
            w_in, o_out = sem("expert_w_in"), sem("expert_out")
            block = phase(st)

            @block.sync
            def _(sp):
                for e in range(NE):
                    sp.dma_start(w1s[:, :, e, :], w1[e].rearrange("(k p) f -> p k f", p=P)).then_inc(w_in, 16)
                sp.dma_start(w2s[:, :, :], w2.rearrange("e (t p) d -> p (e t) d", p=P)).then_inc(w_in, 16)
                sp.dma_start(b1r[:, :], b1.rearrange("e (t p) -> (e t) p", p=P)).then_inc(w_in, 16)
                sp.dma_start(b2r[0:1, :], b2.rearrange("(a e) d -> a (e d)", a=1)).then_inc(w_in, 16)
                for c in range(NC):
                    sp.wait_ge(s["y_ok"], (c + 1) * C)
                    r0, r1 = c * C * P, min((c + 1) * C * P, N)
                    full = (r1 - r0) // P
                    sp.dma_start(by_block(out[r0:r0 + full * P, :]), X[:, c * C:c * C + full, :]).then_inc(o_out, 16)
                    if full < C:
                        sp.dma_start(out[(NB - 1) * P:N, :], X[0:LAST, NB - 1, :]).then_inc(o_out, 16)
                sp.wait_ge(o_out, 16 * (NC + 1))

            @block.tensor
            def _(pe):
                pe.wait_ge(w_in, 16 * (NE + 3))
                nc.tensor.transpose(py[:, 0, 0:HT], b1r[:, :], ident[0:HT, 0:HT]).then_inc(s["b1_ps"], 1)
                pe.wait_ge(s["b1_ok"], 1)
                pe.wait_ge(s["one"], 1)

                def hidden(b, q, m):
                    for g in range(4):
                        if after(b, 1):
                            hold(pe, s[f"hb{g}"], b)
                        for t in range(4 * g, 4 * g + 4):
                            for k in range(KD):
                                mm = nc.tensor.matmul(phid[:, g, (t % 4) * P:(t % 4 + 1) * P],
                                                      w1s[:, k, t // FT, (t % FT) * P:(t % FT + 1) * P],
                                                      XT[:, k, bass.ds(b * P, P)], start=k == 0, stop=k == KD - 1)
                        mm.then_inc(s[f"hps{g}"], 1)

                def outputs(b, q, m):
                    hold(pe, s["hid"], b * 16 + 16)
                    if after(b, 2):
                        hold(pe, s["y_ok"], b - 1)
                    for e in range(NE):
                        y = py[:, q, e * D:(e + 1) * D]
                        nc.tensor.matmul(y, one[0:1, :], b2r[0:1, e * D:(e + 1) * D], start=True, stop=False)
                        for t in range(FT):
                            mm = nc.tensor.matmul(y, hid[:, q, (e * FT + t) * P:(e * FT + t + 1) * P], w2s[:, e * FT + t, :], start=False, stop=t == FT - 1)
                    mm.then_inc(s["y_ps"], 1)

                steps(pe, [(0, hidden), (1, outputs)], NB)

            @block.scalar
            def _(act):
                act.wait_ge(s["b1_ps"], 1)
                nc.scalar.copy(b1c[:, :], py[:, 0, 0:HT]).then_inc(s["b1_ok"], 1)
                act.wait_ge(s["b1_ok"], 1)

                def gelu(b, q, m):
                    if after(b, 2):
                        hold(act, s["y_ps"], b - 1)
                    for g in range(4):
                        hold(act, s[f"hps{g}"], b + 1)
                        for t in range(4 * g, 4 * g + 4):
                            i = nc.scalar.activation(hid[:, q, t * P:(t + 1) * P], phid[:, g, (t % 4) * P:(t % 4 + 1) * P], ACT.Gelu, bias=b1c[:, t:t + 1])
                            i.then_inc(s["hid"], 1)
                        hold(act, s["hid"], b * 16 + (4 * g + 4))
                        act.sem_inc(s[f"hb{g}"], 1)

                steps(act, [(0, gelu)], NB)

            @block.vector
            def _(dve):
                nc.vector.memset(one[:, :], 1.0).then_inc(s["one"], 1)

                def combine(b, q, m):
                    hold(dve, s["y_ps"], b + 1)
                    link = chain(dve, s["chain"], b, 3)
                    x1 = X[:, bass.ds(b, 1), :].rearrange("p a b -> p (a b)")
                    for e in range(NE):
                        g = gate[:, bass.ds(b, 1), e:e + 1].rearrange("p a b -> p (a b)")
                        i = nc.vector.scalar_tensor_tensor(out=x1, in0=py[:, q, e * D:(e + 1) * D], scalar=g, in1=x1, op0=ALU.mult, op1=ALU.add)
                        if e < NE - 1:
                            link(i)
                        else:
                            i.then_inc(s["y_ok"], 1)

                steps(dve, [(0, combine)], NB)


_INS = ["x", "src", "dst", "L0_gnn_W", "L0_gnn_b", "L0_mix_w_qkv", "L0_mix_w_out", "L0_mix_b_out", "L0_ffn_W_gat",
        "L0_ffn_att_src", "L0_ffn_att_dst", "L0_ffn_b_gat", "L0_ffn_ln_gamma", "L0_ffn_ln_beta", "L0_ffn_W1",
        "L0_ffn_b1", "L0_ffn_W2", "L0_ffn_b2", "L0_ffn_edge_index"]
_OUTS = [((6250, 256), "float32")]


def kernel(**inputs):
    import numpy as _np
    import concourse.bacc as _bacc
    from concourse import mybir as _mybir
    from concourse.bass_utils import run_bass_kernel_spmd as _run

    nc = _bacc.Bacc("TRN2", target_bir_lowering=False, num_devices=1)
    arrays, args = {}, []
    for name in _INS:
        a = _np.ascontiguousarray(inputs[name])
        arrays[f"in_{name}_dram"] = a
        args.append(nc.dram_tensor(f"in_{name}_dram", a.shape, _mybir.dt.from_np(a.dtype), kind="ExternalInput").ap())
    for i, (shape, dtype) in enumerate(_OUTS):
        dt = _mybir.dt.from_np(_np.dtype(dtype))
        args.append(nc.dram_tensor(f"out_{i}_dram", shape, dt, kind="ExternalOutput").ap())
    build(nc, *args)
    r = _run(nc, [arrays], core_ids=[0])
    return r.results[0]["out_0_dram"]
```

```python
from contextlib import ExitStack

import concourse.bass as bass
from concourse import mybir

F32 = mybir.dt.float32
F16 = mybir.dt.float16
BF16 = mybir.dt.bfloat16
I32 = mybir.dt.int32
ALU = mybir.AluOpType
ACT = mybir.ActivationFunctionType
AX = mybir.AxisListType.X

P = 128
GNN_EPS, LN_EPS, DEN_EPS = 1e-12, 1e-5, 1e-16
SLOPE = 0.2


def hold(eng, sem, value):
    eng.wait_ge(sem, value)
    if not isinstance(value, int):
        eng.nop(nofuse=True)


def after(b, k):
    return not isinstance(b, int) or b >= k


def chain(eng, sem, b, per):
    count = [0]

    def link(ins):
        count[0] += 1
        assert per is None or count[0] <= per
        ins.then_inc(sem, 1)
        hold(eng, sem, b * (per or 0) + count[0])

    return link


def one_hot(nc, out, ids, iota):
    p, n, w = out.shape
    return nc.vector.tensor_tensor(out.rearrange("p n (w t) -> p n w t", t=2), ids.unsqueeze(2).to_broadcast([p, n, w // 2, 2]),
                                   iota.rearrange("p (w t) -> p w t", t=2).unsqueeze(1).to_broadcast([p, n, w // 2, 2]), ALU.is_equal)


def steps(eng, stages, n):
    most = max(lag for lag, _ in stages)

    def fixed(s):
        for lag, body in stages:
            if 0 <= s - lag < n:
                body(s - lag, (s - lag) % 2, (s - lag) // 2)

    rounds = (n - most - 2) // 2
    first = n - 2 * rounds
    for s in range(first):
        fixed(s)
    with eng.Fori(0, rounds) as r:
        for u in range(2):
            for lag, body in stages:
                c = first + u - lag
                body(r * 2 + c, c % 2, r + c // 2)
    for s in range(n, n + most):
        fixed(s)


def build(nc, x, src, dst, gnn_w, gnn_b, w_qkv, w_out, b_out, w_gat, att_src, att_dst, b_gat,
          ln_g, ln_b, w1, b1, w2, b2, edges, out):
    N, D = x.shape
    E = src.shape[0]
    NB = -(-N // P)
    NP = NB * P
    LAST = N - (NB - 1) * P
    KD = D // P
    INNER = w_out.shape[1]
    DH = 64
    HM = INNER // DH
    NE, _, FF = w1.shape
    FT = FF // P
    HT = NE * FT
    GH = att_src.shape[0]
    GW = GH * NE
    PAY = GW + GH
    ET = -(-E // P)
    RT = edges.shape[1] // P
    assert RT * P == edges.shape[1]
    HB = NB + NB % 2
    C = 7
    NC = NB // C
    assert NB == NC * C and KD == 2 and PAY == 20

    dram = lambda name, shape, dt=F32: nc.dram_tensor(name, shape, dt, kind="Internal").ap()
    XN = dram("xn_table", [NP, D])
    XP = dram("x_padded", [NP, D])
    SRC = dram("src_padded", [ET * P, 1], I32)
    DST = dram("dst_padded", [ET * P, 1], I32)
    RSRC = dram("router_src", [RT * P, 1], I32)
    RDST = dram("router_dst", [RT * P, 1], I32)
    EF = ET * P + P
    SRCF = dram("src_float", [EF, 1])
    DSTF = dram("dst_float", [EF, 1])
    RSD = dram("row_start", [NP + 1, 1])
    RDF = dram("router_dst_float", [RT * P])
    RDL = dram("router_dst_low", [RT * P], BF16)
    SL = dram("router_src_sorted", [RT * P, 1], I32)
    RK = 40
    GD = dram("router_rows_sorted", [RT * P + RK * P, PAY])
    Y = dram("expert_out", [NP, NE * D])
    ACC = dram("neighbour_sum", [NP + P, D + 1])
    TAB = dram("router_table", [NP, PAY])
    MAXT = dram("max_table", [NP, GH])
    MD = dram("shift_table", [NP, 2 * GH])
    AGG = dram("attention_sum", [NP, PAY])

    def where(eng, k):
        return eng.If(eng.value_load(slow[0:1, k:k + 1], min_val=0, max_val=1) != 0)

    def by_block(t):
        return t.rearrange("(b p) c -> p b c", p=P)

    top = ExitStack()
    live = []

    def sem(name):
        live.append(nc.alloc_semaphore(name=name))
        return live[-1]

    def phase(st):
        def done():
            nc.clear_and_free_semaphores(list(live))
            nc.all_engine_barrier()
            live.clear()
        st.callback(done)
        return st.enter_context(nc.Block())

    sb = lambda st, name, shape, dt=F32: st.enter_context(nc.sbuf_tensor(name, shape, dt))
    ps = lambda st, name, shape: st.enter_context(nc.psum_tensor(name, shape, F32))

    top.enter_context(nc.allow_non_contiguous_dma(reason="columns of small tables"))
    with top:
        slow = sb(top, "slow_flags", [1, 2], I32)
        ident = sb(top, "ident", [P, P])
        upper = sb(top, "upper", [P, P])
        ones = sb(top, "ones_square", [P, P])
        rsi2 = sb(top, "router_starts", [P, NB], I32)
        rdeg = sb(top, "router_degree", [P, NB])
        lower = sb(top, "lower", [P, P])
        mix = sb(top, "mix_matrix", [P, KD, D])
        zero = sb(top, "zero", [P, D + 1])
        wgat = sb(top, "w_gat_sb", [P, KD, GW])
        att = sb(top, "att_rows", [P, 2, GW])
        gb = sb(top, "gate_rows", [P, 3, GW])

        UP, DOWN = 1024.0, 2048.0
        gst = ExitStack()
        xhl = sb(gst, "x_parts", [P, NB, 2 * D], F16)
        with ExitStack() as st:
            sq = sb(st, "squares", [P, C, D])
            X = sb(st, "x_rows", [P, NB, D])
            lnm = sb(st, "ln_mean", [P, NC, C])
            lnv = sb(st, "ln_var", [P, NC, C])
            lns = sb(st, "ln_std", [P, NC, C])
            wkv_n = sb(st, "wkv_rows", [P, 8, D])
            wkv = sb(st, "wkv_cols", [P, KD, 2 * INNER])
            wkm = sb(st, "wkv_mean", [P, KD, 2 * HM])
            wq = sb(st, "wq_rows", [P, 4, D])
            wo_n = sb(st, "w_out_rows", [P, KD, INNER])
            wo = sb(st, "w_out_cols", [P, 4, D])
            kvsq = sb(st, "kv_squares", [P, 2, 2 * INNER])
            kss = sb(st, "kv_sums", [P, 2, 2 * HM])
            kpr = sb(st, "kv_var_product", [P, 2, HM])
            kst = sb(st, "kv_std_product", [P, 2, HM])
            kri = sb(st, "kv_scale", [P, 2, HM])
            ks = sb(st, "k_scaled", [P, 2, INNER])
            vs = sb(st, "v_rows", [P, 2, INNER])
            dots = sb(st, "dots_diag", [P, 4, P])
            bt = sb(st, "b_cols", [P, 4, D])
            xs = sb(st, "x_stage", [P, 2, D])
            xc_ = sb(st, "x_cols_stage", [P, 2, KD * P])
            pkv = ps(st, "ps_kv", [P, 2, 2 * INNER])
            pt = ps(st, "ps_t", [P, 2, 512])
            pd = ps(st, "ps_dots", [P, 4, P])

            x_in = [sem(f"x_in{c}") for c in range(NC)]
            w_in, pad_in, tabs_out, x_zero = sem("w_in"), sem("pad_in"), sem("tabs_out"), sem("x_zero")
            consts, ident_z, lower_z = sem("consts"), sem("ident_z"), sem("lower_z")
            dchain, ln_var_ok, ln_std_ok, ln_ok = sem("dve_chain"), sem("ln_var_ok"), sem("ln_std_ok"), sem("ln_ok")
            wt_ok, wt_used, wkv_ok = sem("wt_ok"), sem("wt_used"), sem("wkv_ok")
            xt_ps, xt_ok, xs_ok = sem("xt_ps"), sem("xt_ok"), sem("xs_ok")
            kv_ok, kvsq_ok, v_ok, kss_ok, kpr_ok = sem("kv_ok"), sem("kvsq_ok"), sem("v_ok"), sem("kss_ok"), sem("kpr_ok")
            kst_ok, kri_ok, ks_ok, dots_ok = sem("kst_ok"), sem("kri_ok"), sem("ks_ok"), sem("dots_ok")
            dd_ok, bt_ps, bt_ok, mix_ps, mix_ok = sem("dd_ok"), sem("bt_ps"), sem("bt_ok"), sem("mix_ps"), sem("mix_ok")
            dz_ok, kve_ok, fill_ok = sem("dz_ok"), sem("kve_ok"), sem("fill_ok")
            high_ok, rest_ok, low_ok, parts_kept = sem("high_ok"), sem("rest_ok"), sem("low_ok"), sem("parts_kept")
            xu = sb(st, "x_rest", [P, 2, D])
            xp = sb(st, "x_parts_stage", [P, 2, 2 * D], F16)
            e_in, e_ok, e_out = sem("redges_in"), sem("redges_ok"), sem("redges_out")
            ei = sb(st, "edges_int", [P, 2, ET], I32)
            ef = sb(st, "edges_float", [P, 2, ET])
            tail = sb(st, "edges_tail", [P, 2])
            l_in, tail_ok, l_ok, l_out = sem("list_in"), sem("list_tail"), sem("list_ok"), sem("list_out")
            re = sb(st, "router_edges", [P, 2, RT], I32)
            fill = sb(st, "edge_fill", [P, 2], I32)
            block = phase(st)

            @block.sync
            def _(sp):
                sp.dma_start(re[:, :, :], edges.rearrange("k (p t) -> p k t", p=P)).then_inc(e_in, 16)
                sp.wait_ge(x_zero, 1)
                for c in range(NC):
                    r0, r1 = c * C * P, min((c + 1) * C * P, N)
                    full = (r1 - r0) // P
                    sp.dma_start(X[:, c * C:c * C + full, :], by_block(x[r0:r0 + full * P, :])).then_inc(x_in[c], 16)
                    if full < C:
                        sp.dma_start(X[0:LAST, NB - 1, :], x[(NB - 1) * P:N, :]).then_inc(x_in[c], 16)
                full_e = (ET - 1) * P
                for a, t in ((src, SRC), (dst, DST)):
                    sp.dma_start(t[0:full_e, 0].rearrange("(a b) -> a b", b=P), a[0:full_e].rearrange("(a b) -> a b", b=P)).then_inc(pad_in, 16)
                    sp.dma_start(t[full_e:E, :], a[full_e:E].rearrange("(a b) -> a b", b=1)).then_inc(pad_in, 16)
                sp.dma_start(XP[0:N, :], x).then_inc(pad_in, 16)
                sp.wait_ge(fill_ok, 3)
                sp.dma_start(XP[N:NP, :], zero[0:NP - N, 0:D]).then_inc(pad_in, 16)
                sp.dma_start(SRC[E:ET * P, :], fill[0:ET * P - E, 0:1]).then_inc(pad_in, 16)
                sp.dma_start(DST[E:ET * P, :], fill[0:ET * P - E, 1:2]).then_inc(pad_in, 16)
                sp.wait_ge(pad_in, 16 * 8)
                for k, t in ((0, SRC), (1, DST)):
                    sp.dma_start(ei[:, k, :], t.rearrange("(p t) c -> p (t c)", p=P)).then_inc(l_in, 16)
                sp.wait_ge(e_ok, 2)
                for k, t in ((0, RSRC), (1, RDST)):
                    sp.dma_start(t.rearrange("(p t) c -> p (t c)", p=P), re[:, k, :]).then_inc(e_out, 16)
                sp.wait_ge(e_out, 32)
                for c in range(NC):
                    sp.wait_ge(ln_ok, (c + 1) * C)
                    sp.dma_start(by_block(XN[c * C * P:(c + 1) * C * P, :]), X[:, c * C:(c + 1) * C, :]).then_inc(tabs_out, 16)
                sp.wait_ge(l_ok, 2)
                for k, t in ((0, SRCF), (1, DSTF)):
                    sp.dma_start(t[0:ET * P, :].rearrange("(p t) c -> p (t c)", p=P), ef[:, k, :]).then_inc(l_out, 16)
                    sp.wait_ge(tail_ok, 2)
                    sp.dma_start(t[ET * P:EF, :], tail[:, k:k + 1]).then_inc(l_out, 16)
                sp.wait_ge(l_out, 64)
                sp.wait_ge(tabs_out, 16 * NC)

            @block.gpsimd
            def _(pool):
                nc.gpsimd.memset(ident[:, :], 0.0).then_inc(ident_z, 1)
                nc.gpsimd.memset(lower[:, :], 1.0).then_inc(lower_z, 1)
                pool.wait_ge(ident_z, 1)
                nc.gpsimd.affine_select(out=ident[:, :], in_=ident[:, :], compare_op=ALU.not_equal, fill=1.0,
                                        base=0, pattern=[[-1, P]], channel_multiplier=1).then_inc(consts, 1)
                pool.wait_ge(lower_z, 1)
                nc.gpsimd.affine_select(out=lower[:, :], in_=lower[:, :], compare_op=ALU.is_gt, fill=0.0,
                                        base=0, pattern=[[-1, P]], channel_multiplier=1).then_inc(consts, 1)
                nc.gpsimd.memset(upper[:, :], 1.0).then_inc(ident_z, 1)
                nc.gpsimd.memset(ones[:, :], 1.0).then_inc(ident_z, 1)
                pool.wait_ge(ident_z, 3)
                nc.gpsimd.affine_select(out=upper[:, :], in_=upper[:, :], compare_op=ALU.is_gt, fill=0.0,
                                        base=0, pattern=[[1, P]], channel_multiplier=-1).then_inc(consts, 1)

                def stage(b, q, m):
                    hold(pool, ln_ok, b + 1)
                    if after(b, 2):
                        hold(pool, xt_ps, b - 1)
                        hold(pool, rest_ok, b - 1)
                    nc.gpsimd.tensor_copy(xs[:, q, :], X[:, bass.ds(b, 1), :].rearrange("p a b -> p (a b)")).then_inc(xs_ok, 1)

                def keep(b, q, m):
                    hold(pool, low_ok, b + 1)
                    nc.gpsimd.tensor_copy(xhl[:, bass.ds(b, 1), :].rearrange("p a b -> p (a b)"), xp[:, q, :]).then_inc(parts_kept, 1)

                steps(pool, [(0, stage), (2, keep)], NB)

            @block.vector
            def _(dve):
                n = [0]

                def link(ins):
                    n[0] += 1
                    ins.then_inc(dchain, 1)
                    dve.wait_ge(dchain, n[0])

                nc.vector.memset(X[:, NB - 1, :], 0.0).then_inc(x_zero, 1)
                nc.vector.memset(zero[:, :], 0.0).then_inc(fill_ok, 1)
                nc.vector.memset(fill[:, 0:1], 0).then_inc(fill_ok, 1)
                nc.vector.memset(fill[:, 1:2], NP - 1).then_inc(fill_ok, 1)
                nc.vector.memset(dots[:, :, :], 0.0).then_inc(dz_ok, 1)
                nc.vector.memset(tail[:, 0:1], 0.0).then_inc(tail_ok, 1)
                nc.vector.memset(tail[:, 1:2], float(NP - 1)).then_inc(tail_ok, 1)
                dve.wait_ge(e_in, 16)
                nc.vector.tensor_scalar(re[:, 0, :], re[:, 0, :], float(N - 1), None, ALU.min).then_inc(e_ok, 1)
                nc.vector.tensor_scalar(re[:, 1, :], re[:, 1, :], float(NP - 1), None, ALU.min).then_inc(e_ok, 1)
                for c in range(NC):
                    xc = X[:, c * C:(c + 1) * C, :]
                    dve.wait_ge(x_in[c], 16 if c < NC - 1 else 32)
                    link(nc.vector.tensor_reduce(lnm[:, c, :], xc, AX, ALU.add))
                    link(nc.vector.tensor_scalar(lnm[:, c, :], lnm[:, c, :], 1.0 / D, None, ALU.mult))
                    link(nc.vector.tensor_tensor(xc, xc, lnm[:, c, :].unsqueeze(2).to_broadcast([P, C, D]), ALU.subtract))
                    link(nc.vector.tensor_tensor(sq[:, :, :], xc, xc, ALU.mult))
                    link(nc.vector.tensor_reduce(lnv[:, c, :], sq[:, :, :], AX, ALU.add))
                    nc.vector.tensor_scalar(lnv[:, c, :], lnv[:, c, :], 1.0 / D, LN_EPS, ALU.mult, ALU.add).then_inc(ln_var_ok, 1)
                    dve.wait_ge(ln_std_ok, c + 1)
                    link(nc.vector.reciprocal(lns[:, c, :], lns[:, c, :]))
                    nc.vector.tensor_tensor(xc, xc, lns[:, c, :].unsqueeze(2).to_broadcast([P, C, D]), ALU.mult).then_inc(ln_ok, C)
                dve.wait_ge(wt_used, 4)
                wh = wkv[:, :, :].rearrange("p k (h e) -> p (k h) e", e=DH)
                wm = wkm[:, :, :].rearrange("p k h -> p (k h)")
                link(nc.vector.tensor_reduce(wm, wh, AX, ALU.add))
                link(nc.vector.tensor_scalar(wm, wm, 1.0 / DH, None, ALU.mult))
                nc.vector.tensor_tensor(wh, wh, wm.unsqueeze(2).to_broadcast([P, KD * 2 * HM, DH]), ALU.subtract).then_inc(wkv_ok, 1)

                def variances(b, q, m):
                    hold(dve, kvsq_ok, b + 1)
                    nc.vector.tensor_reduce(kss[:, q, :], kvsq[:, q, :].rearrange("p (h e) -> p h e", e=DH), AX, ALU.add).then_inc(kss_ok, 1)
                    hold(dve, kss_ok, b + 1)
                    link2(nc.vector.tensor_scalar(kss[:, q, :], kss[:, q, :], 1.0 / DH, LN_EPS, ALU.mult, ALU.add), b)
                    nc.vector.tensor_tensor(kpr[:, q, :], kss[:, q, 0:HM], kss[:, q, HM:2 * HM], ALU.mult).then_inc(kpr_ok, 1)

                def link2(ins, b):
                    ins.then_inc(kve_ok, 1)
                    hold(dve, kve_ok, b + 1)

                def scale_k(b, q, m):
                    hold(dve, kst_ok, b + 1)
                    nc.vector.reciprocal(kri[:, q, :], kst[:, q, :]).then_inc(kri_ok, 1)
                    hold(dve, kri_ok, b + 1)
                    if after(b, 2):
                        hold(dve, dots_ok, b - 1)
                    nc.vector.tensor_tensor(ks[:, q, :].rearrange("p (h e) -> p h e", e=DH),
                                            pkv[:, q, 0:INNER].rearrange("p (h e) -> p h e", e=DH),
                                            kri[:, q, :].unsqueeze(2).to_broadcast([P, HM, DH]), ALU.mult).then_inc(ks_ok, 1)

                def rest(b, q, m):
                    hold(dve, high_ok, b + 1)
                    if after(b, 2):
                        hold(dve, low_ok, b - 1)
                    nc.vector.scalar_tensor_tensor(out=xu[:, q, :], in0=xs[:, q, :], scalar=UP, in1=xp[:, q, 0:D], op0=ALU.mult, op1=ALU.subtract).then_inc(rest_ok, 1)

                steps(dve, [(3, scale_k), (0, rest), (2, variances)], NB)
                dve.wait_ge(l_in, 32)
                for k in range(2):
                    nc.vector.tensor_copy(ef[:, k, :], ei[:, k, :]).then_inc(l_ok, 1)
                dve.wait_ge(dots_ok, NB)
                dve.wait_ge(dz_ok, 1)
                nc.vector.tensor_scalar(dots[0:DH, :, 0:DH], pd[0:DH, :, 0:DH], 1.0 / N, None, ALU.mult).then_inc(dd_ok, 1)
                nc.vector.tensor_scalar(dots[DH:P, :, DH:P], pd[DH:P, :, DH:P], 1.0 / N, None, ALU.mult).then_inc(dd_ok, 1)

            @block.scalar
            def _(act):
                loads = [(wkv_n[:, :, :], w_qkv[INNER:3 * INNER, :].rearrange("(j p) d -> p j d", p=P)),
                         (wq[:, :, :], w_qkv[0:INNER, :].rearrange("(j p) d -> p j d", p=P)),
                         (wo_n[:, :, :], w_out.rearrange("(j p) d -> p j d", p=P)),
                         (wgat[:, :, :], w_gat.rearrange("(j p) d -> p j d", p=P)),
                         (att[:, 0, :], att_src.rearrange("a b -> (a b)").partition_broadcast(P)),
                         (att[:, 1, :], att_dst.rearrange("a b -> (a b)").partition_broadcast(P)),
                         (gb[:, 0, :], b_gat.partition_broadcast(P)), (gb[:, 1, :], ln_g.partition_broadcast(P)),
                         (gb[:, 2, :], ln_b.partition_broadcast(P))]
                for to, fr in loads:
                    act.dma_start(to, fr).then_inc(w_in, 16)
                act.wait_ge(w_in, 16 * len(loads))
                for g in range(4):
                    act.wait_ge(wt_ok, g + 1)
                    nc.scalar.copy(wkv[:, g // 2, (g % 2) * 512:(g % 2 + 1) * 512], pt[:, g % 2, :]).then_inc(wt_used, 1)
                for g in range(2):
                    act.wait_ge(wt_ok, 5 + g)
                    nc.scalar.copy(wo[:, 2 * g:2 * g + 2, :].rearrange("p a b -> p (a b)"), pt[:, g % 2, :]).then_inc(wt_used, 1)
                for c in range(NC):
                    act.wait_ge(ln_var_ok, c + 1)
                    nc.scalar.activation(lns[:, c, :], lnv[:, c, :], ACT.Sqrt).then_inc(ln_std_ok, 1)

                def columns(b, q, m):
                    hold(act, xt_ps, b + 1)
                    if after(b, 2):
                        hold(act, kv_ok, b - 1)
                    nc.scalar.copy(xc_[:, q, :], pt[:, q, 0:KD * P]).then_inc(xt_ok, 1)

                def squares(b, q, m):
                    hold(act, kv_ok, b + 1)
                    if after(b, 2):
                        hold(act, kss_ok, b - 1)
                    nc.scalar.activation(kvsq[:, q, :], pkv[:, q, :], ACT.Square).then_inc(kvsq_ok, 1)
                    if after(b, 2):
                        hold(act, dots_ok, b - 1)
                    nc.scalar.copy(vs[:, q, :], pkv[:, q, INNER:2 * INNER]).then_inc(v_ok, 1)

                def roots(b, q, m):
                    hold(act, kpr_ok, b + 1)
                    nc.scalar.activation(kst[:, q, :], kpr[:, q, :], ACT.Sqrt).then_inc(kst_ok, 1)

                def high(b, q, m):
                    hold(act, xs_ok, b + 1)
                    if after(b, 2):
                        hold(act, parts_kept, b - 1)
                    nc.scalar.activation(xp[:, q, 0:D], xs[:, q, :], ACT.Copy, scale=UP).then_inc(high_ok, 1)

                def low(b, q, m):
                    hold(act, rest_ok, b + 1)
                    nc.scalar.activation(xp[:, q, D:2 * D], xu[:, q, :], ACT.Copy, scale=DOWN).then_inc(low_ok, 1)

                steps(act, [(2, squares), (0, columns), (0, high), (1, low), (2, roots)], NB)
                act.wait_ge(bt_ps, 1)
                nc.scalar.copy(bt[:, :, :].rearrange("p a b -> p (a b)"), pkv[:, 0, :]).then_inc(bt_ok, 1)
                act.wait_ge(mix_ps, 1)
                nc.scalar.copy(mix[:, :, :].rearrange("p a b -> p (a b)"), pt[:, 0, :]).then_inc(mix_ok, 1)
                act.wait_ge(mix_ok, 1)

            @block.tensor
            def _(pe):
                pe.wait_ge(consts, 3)
                pe.wait_ge(w_in, 16 * 9)
                for g in range(4):
                    if g >= 2:
                        pe.wait_ge(wt_used, g - 1)
                    for j in range(4):
                        mm = nc.tensor.transpose(pt[:, g % 2, j * P:(j + 1) * P],
                                                 wkv_n[:, (g % 2) * 4 + j, (g // 2) * P:(g // 2 + 1) * P], ident[:, :])
                    mm.then_inc(wt_ok, 1)
                for g in range(2):
                    pe.wait_ge(wt_used, g + 3)
                    for j in range(4):
                        mm = nc.tensor.transpose(pt[:, g % 2, j * P:(j + 1) * P],
                                                 wo_n[:, j % 2, (2 * g + j // 2) * P:(2 * g + j // 2 + 1) * P], ident[:, :])
                    mm.then_inc(wt_ok, 1)
                pe.wait_ge(wt_used, 6)

                def turn(b, q, m):
                    hold(pe, xs_ok, b + 1)
                    if after(b, 2):
                        hold(pe, xt_ok, b - 1)
                    for k in range(KD):
                        mm = nc.tensor.transpose(pt[:, q, k * P:(k + 1) * P], xs[:, q, k * P:(k + 1) * P], ident[:, :])
                    mm.then_inc(xt_ps, 1)

                pe.wait_ge(wkv_ok, 1)
                pe.wait_ge(fill_ok, 3)
                nc.tensor.matmul(pd[:, :, :].rearrange("p a b -> p (a b)"), zero[:, 0:P], wkv[:, 0, 0:512], start=True, stop=True, skip_group_check=True)

                def kv(b, q, m):
                    hold(pe, xt_ok, b + 1)
                    if after(b, 2):
                        hold(pe, v_ok, b - 1)
                        hold(pe, ks_ok, b - 1)
                    for half in range(2):
                        for k in range(KD):
                            mm = nc.tensor.matmul(pkv[:, q, half * INNER:(half + 1) * INNER], xc_[:, q, k * P:(k + 1) * P],
                                                  wkv[:, k, half * INNER:(half + 1) * INNER], start=k == 0, stop=k == KD - 1)
                    mm.then_inc(kv_ok, 1)

                def product(b, q, m):
                    hold(pe, ks_ok, b + 1)
                    hold(pe, v_ok, b + 1)
                    for h in range(4):
                        mm = nc.tensor.matmul(pd[:, h, :], ks[:, q, h * P:(h + 1) * P], vs[:, q, h * P:(h + 1) * P],
                                              start=False, stop=True, skip_group_check=True)
                    mm.then_inc(dots_ok, 1)

                steps(pe, [(4, product), (2, kv), (0, turn)], NB)
                pe.wait_ge(dd_ok, 2)
                for h in range(4):
                    mm = nc.tensor.matmul(pkv[:, 0, h * D:(h + 1) * D], dots[:, h, :], wq[:, h, :], start=True, stop=True)
                mm.then_inc(bt_ps, 1)
                pe.wait_ge(bt_ok, 1)
                for m in range(KD):
                    for h in range(4):
                        mm = nc.tensor.matmul(pt[:, 0, m * D:(m + 1) * D], bt[:, h, m * P:(m + 1) * P], wo[:, h, :], start=h == 0, stop=h == 3)
                mm.then_inc(mix_ps, 1)



        def edge_pass(kind):
            flag = 0 if kind == "sum" else 1
            table, tw = (XN, D) if kind == "sum" else (TAB, PAY)
            acc, aw = {"sum": (ACC, D + 1), "max": (MAXT, GH), "soft": (AGG, PAY)}[kind]
            esrc, edst, tiles = (SRC, DST, ET) if kind == "sum" else (RSRC, RDST, RT)
            gw = D + 1 if kind == "sum" else PAY
            with ExitStack() as st:
                si = sb(st, f"{kind}_src", [P, 1], I32)
                di = sb(st, f"{kind}_dst", [P, 1], I32)
                db = sb(st, f"{kind}_dst_row", [P, P], I32)
                ui = sb(st, f"{kind}_rows_out", [P, 1], I32)
                df = sb(st, f"{kind}_dst_f", [P, 1])
                dbf = sb(st, f"{kind}_dst_row_f", [P, P])
                same = sb(st, f"{kind}_same", [P, P])
                before = sb(st, f"{kind}_before", [P, P])
                cnt = sb(st, f"{kind}_count", [P, 2])
                got = sb(st, f"{kind}_gathered", [P, gw])
                old = sb(st, f"{kind}_old", [P, aw])
                new = sb(st, f"{kind}_new", [P, aw])
                shift = sb(st, f"{kind}_shift", [P, 2 * GH])
                pay = sb(st, f"{kind}_payload", [P, PAY])
                wts = sb(st, f"{kind}_scores", [P, 2, GH])
                spread = sb(st, f"{kind}_spread", [P, GH, P])
                low = sb(st, f"{kind}_low", [P, GH])
                psum = ps(st, f"{kind}_ps", [P, 512])
                names = ["init", "ready", "idx", "gat", "oldr", "shr", "chain", "same_ok", "rows_ok", "pay_ok", "exp_in", "exp_ok", "mm_ok", "new_ok", "scat"]
                s = {k: sem(f"{kind}_{k}") for k in names}
                block = phase(st)

                @block.sync
                def _(sp):
                    with where(sp, flag):
                        sp.wait_ge(s["ready"], 1)
                        fill = (low if kind == "max" else zero)[:, 0:aw]
                        sp.dma_start(by_block(acc[0:NP, :]), fill.unsqueeze(1).to_broadcast([P, NB, aw])).then_inc(s["init"], 16)

                        def load(t):
                            sp.dma_start(si[:, :], esrc[bass.ds(t * P, P), :]).then_inc(s["idx"], 16)
                            sp.dma_start(di[:, :], edst[bass.ds(t * P, P), :]).then_inc(s["idx"], 16)
                            sp.dma_start(db[:, :], edst[bass.ds(t * P, P), :].rearrange("a b -> (a b)").partition_broadcast(P)).then_inc(s["idx"], 16)

                        load(0)
                        with sp.Fori(1, tiles) as t:
                            hold(sp, s["scat"], t * 16)
                            load(t)
                        sp.wait_ge(s["init"], 16)
                        sp.wait_ge(s["scat"], 16 * tiles)

                @block.gpsimd
                def _(pool):
                    with where(pool, flag):
                        pool.wait_ge(s["init"], 16)
                        with pool.Fori(0, tiles) as t:
                            hold(pool, s["idx"], t * 48 + 48)
                            nc.gpsimd.indirect_dma_start(got[:, 0:tw], None, table, bass.IndirectOffsetOnAxis(ap=si[:, 0:1], axis=0)).then_inc(s["gat"], 16)
                            nc.gpsimd.indirect_dma_start(old[:, :], None, acc, bass.IndirectOffsetOnAxis(ap=di[:, 0:1], axis=0)).then_inc(s["oldr"], 16)
                            if kind == "soft":
                                nc.gpsimd.indirect_dma_start(shift[:, :], None, MD, bass.IndirectOffsetOnAxis(ap=di[:, 0:1], axis=0)).then_inc(s["shr"], 16)
                            hold(pool, s["new_ok"], t + 1)
                            nc.gpsimd.indirect_dma_start(acc, bass.IndirectOffsetOnAxis(ap=ui[:, 0:1], axis=0), new[:, :], None,
                                                         bounds_check=NP - 1, oob_is_err=False).then_inc(s["scat"], 16)

                @block.vector
                def _(dve):
                    with where(dve, flag):
                        nc.vector.memset(low[:, :], LOW)
                        nc.vector.memset(got[:, gw - 1:gw], 1.0)
                        dve.drain().then_inc(s["ready"], 1)
                        dve.wait_ge(s["ready"], 1)
                        L = {"sum": 5, "max": 7, "soft": 10}[kind]
                        with dve.Fori(0, tiles) as t:
                            k = [0]

                            def link(ins):
                                k[0] += 1
                                ins.then_inc(s["chain"], 1)
                                hold(dve, s["chain"], t * L + k[0])

                            hold(dve, s["idx"], t * 48 + 48)
                            link(nc.vector.tensor_copy(df[:, :], di[:, :]))
                            link(nc.vector.tensor_copy(dbf[:, :], db[:, :]))
                            nc.vector.tensor_scalar(same[:, :], dbf[:, :], df[:, 0:1], None, ALU.is_equal).then_inc(s["same_ok"], 1)
                            hold(dve, s["same_ok"], t + 1)
                            link(nc.vector.tensor_tensor(before[:, :], same[:, :], lower[:, :], ALU.mult))
                            link(nc.vector.tensor_reduce(cnt[:, 0:1], before[:, :], AX, ALU.max))
                            link(nc.vector.tensor_scalar(cnt[:, 1:2], cnt[:, 0:1], BIG, df[:, 0:1], ALU.mult, ALU.add))
                            nc.vector.tensor_copy(ui[:, :], cnt[:, 1:2]).then_inc(s["rows_ok"], 1)
                            hold(dve, s["gat"], t * 16 + 16)
                            if kind == "max":
                                link(nc.vector.tensor_scalar(before[:, :], same[:, :], -1.0, -LOW, ALU.add, ALU.mult))
                                hold(dve, s["mm_ok"], t + 1)
                                link(nc.vector.tensor_tensor(spread[:, :, :], psum[:, :].rearrange("p (h e) -> p h e", h=GH),
                                                             before[:, :].unsqueeze(1).to_broadcast([P, GH, P]), ALU.add))
                                nc.vector.tensor_reduce(new[:, :], spread[:, :, :], AX, ALU.max).then_inc(s["pay_ok"], 1)
                                hold(dve, s["pay_ok"], t + 1)
                                hold(dve, s["oldr"], t * 16 + 16)
                                hold(dve, s["rows_ok"], t + 1)
                                nc.vector.tensor_tensor(new[:, :], new[:, :], old[:, :], ALU.max).then_inc(s["new_ok"], 1)
                            else:
                                if kind == "soft":
                                    hold(dve, s["shr"], t * 16 + 16)
                                    link(nc.vector.tensor_tensor(wts[:, 0, :], got[:, GW:PAY], shift[:, 0:GH], ALU.add))
                                    link(nc.vector.tensor_scalar(wts[:, 1, :], wts[:, 0, :], SLOPE, None, ALU.mult))
                                    link(nc.vector.tensor_tensor(wts[:, 0, :], wts[:, 0, :], wts[:, 1, :], ALU.max))
                                    link(nc.vector.tensor_tensor(wts[:, 1, :], wts[:, 0, :], shift[:, GH:2 * GH], ALU.subtract))
                                    dve.sem_inc(s["exp_in"], 1)
                                    hold(dve, s["exp_ok"], t + 1)
                                    link(nc.vector.tensor_tensor(pay[:, 0:GW].rearrange("p (h e) -> p h e", h=GH), got[:, 0:GW].rearrange("p (h e) -> p h e", h=GH),
                                                                 pay[:, GW:PAY].unsqueeze(2).to_broadcast([P, GH, NE]), ALU.mult))
                                    dve.sem_inc(s["pay_ok"], 1)
                                hold(dve, s["mm_ok"], t + 1)
                                hold(dve, s["oldr"], t * 16 + 16)
                                hold(dve, s["rows_ok"], t + 1)
                                nc.vector.tensor_tensor(new[:, :], psum[:, 0:aw], old[:, :], ALU.add).then_inc(s["new_ok"], 1)
                            assert k[0] == L

                @block.scalar
                def _(act):
                    with where(act, flag):
                        if kind == "soft":
                            with act.Fori(0, tiles) as t:
                                hold(act, s["exp_in"], t + 1)
                                nc.scalar.activation(pay[:, GW:PAY], wts[:, 1, :], ACT.Exp).then_inc(s["exp_ok"], 1)

                @block.tensor
                def _(pe):
                    with where(pe, flag):
                        pe.wait_ge(s["ready"], 1)
                        with pe.Fori(0, tiles) as t:
                            hold(pe, s["same_ok"], t + 1)
                            hold(pe, s["gat"], t * 16 + 16)
                            if kind == "max":
                                for h in range(GH):
                                    mm = nc.tensor.matmul(psum[:, h * P:(h + 1) * P], got[:, GW + h:GW + h + 1].to_broadcast([P, P]), ident[:, :], start=True, stop=True)
                            elif kind == "sum":
                                mm = nc.tensor.matmul(psum[:, 0:aw], same[:, :], got[:, :], start=True, stop=True)
                            else:
                                hold(pe, s["pay_ok"], t + 1)
                                mm = nc.tensor.matmul(psum[:, 0:aw], same[:, :], pay[:, :], start=True, stop=True)
                            mm.then_inc(s["mm_ok"], 1)


        BIG = 1.0e6
        LOW = -1.0e30

        RUN = 512
        KEYS = ET * P // RUN
        SLOT = 64
        assert KEYS * RUN == ET * P and KEYS <= 512
        NPAIR = (NB + 1) // 2
        deg = sb(gst, "in_degree", [P, 2 * NPAIR])
        hit = sb(gst, "src_high", [P, NPAIR, P, 2], BF16)
        lot = sb(gst, "src_low", [P, NPAIR, P, 2], BF16)
        with ExitStack() as st:
            krow = sb(st, "keys", [1, KEYS])
            onesr = sb(st, "ones_row", [1, P])
            dcol = sb(st, "node_ids", [P, NB])
            junk = sb(st, "search_junk", [P, RUN])
            coarse = sb(st, "coarse_count", [P, NB])
            offf = sb(st, "run_offset", [P, NB])
            offi = sb(st, "run_offset_int", [P, NB], I32)
            fine = sb(st, "fine_count", [P, NB])
            rs = sb(st, "row_starts", [P, NB])
            rsi = sb(st, "row_starts_int", [P, NB], I32)
            rn = sb(st, "row_ends", [P, NB])
            runs = sb(st, "dst_runs", [P, 4, RUN])
            slots = sb(st, "src_slots", [P, 2 * NPAIR, SLOT])
            sint = sb(st, "src_slots_int", [P, 2 * NPAIR, SLOT], I32)
            sint2 = sb(st, "src_slots_part", [P, 2 * NPAIR, SLOT], I32)
            hi = sb(st, "slots_high", [P, 2 * NPAIR, SLOT])
            lo = sb(st, "slots_low", [P, 2 * NPAIR, SLOT])
            kio = sb(st, "slot_ids", [P, SLOT])
            ea = sb(st, "sort_check_a", [P, ET])
            eb = sb(st, "sort_check_b", [P, ET])
            bad = sb(st, "bad", [P, 4])
            ends = sb(st, "list_end", [1, 1])
            pk = ps(st, "ps_keys", [P, 512])
            ptr = ps(st, "ps_slots", [P, 4, 512])
            names = ["keys", "chk_in", "ones", "pk_ok", "iota", "coarse", "off", "fine", "ch", "rs", "rs_out", "rn_in", "rsi", "end",
                     "masked", "pt_ok", "pt_used", "badp", "badr"]
            s = {k: sem(f"search_{k}") for k in names}
            run_in = [sem(f"search_run{i}") for i in range(4)]
            slot_in = sem("search_slots")
            block = phase(st)

            @block.sync
            def _(sp):
                with nc.allow_non_contiguous_dma(reason="every 512th destination"):
                    sp.dma_start(krow[0:1, :].unsqueeze(2), DSTF[0:KEYS * RUN, :].rearrange("(j r) c -> c j r", r=RUN)[:, :, 0:1]).then_inc(s["keys"], 16)
                sp.dma_start(ea[:, :], DSTF[0:ET * P, :].rearrange("(p t) c -> p (t c)", p=P)).then_inc(s["chk_in"], 16)
                sp.dma_start(eb[:, :], DSTF[1:ET * P + 1, :].rearrange("(p t) c -> p (t c)", p=P)).then_inc(s["chk_in"], 16)
                sp.wait_ge(s["rs"], 1)
                sp.wait_ge(s["end"], 1)
                sp.dma_start(RSD[0:NP, :].rearrange("(b p) c -> p b c", p=P), rs[:, :].unsqueeze(2)).then_inc(s["rs_out"], 16)
                sp.dma_start(RSD[NP:NP + 1, :], ends[0:1, 0:1]).then_inc(s["rs_out"], 16)
                sp.wait_ge(s["rs_out"], 32)
                sp.dma_start(rn[:, :].unsqueeze(2), RSD[1:NP + 1, :].rearrange("(b p) c -> p b c", p=P)).then_inc(s["rn_in"], 16)

            @block.gpsimd
            def _(pool):
                nc.gpsimd.iota(dcol[:, :], pattern=[[P, NB]], base=0, channel_multiplier=1, allow_small_or_imprecise_dtypes=True).then_inc(s["iota"], 1)
                nc.gpsimd.iota(kio[:, :], pattern=[[1, SLOT]], base=0, channel_multiplier=0, allow_small_or_imprecise_dtypes=True).then_inc(s["iota"], 1)
                pool.wait_ge(s["off"], 1)
                for b in range(NB):
                    if b >= 4:
                        pool.wait_ge(s["fine"], b - 3)
                    nc.gpsimd.indirect_dma_start(runs[:, b % 4, :], None, DSTF[0:ET * P, :],
                                                 bass.IndirectOffsetOnAxis(ap=offi[:, b:b + 1], axis=0)).then_inc(run_in[b % 4], 16)
                pool.wait_ge(s["rsi"], 1)
                for b in range(NB):
                    nc.gpsimd.indirect_dma_start(slots[:, b, :], None, SRCF, bass.IndirectOffsetOnAxis(ap=rsi[:, b:b + 1], axis=0)).then_inc(slot_in, 16)
                pool.wait_ge(s["badp"], 1)
                nc.gpsimd.partition_all_reduce(bad[:, 3:4], bad[:, 2:3], P, bass.bass_isa.ReduceOp.max).then_inc(s["badr"], 1)

            @block.tensor
            def _(pe):
                pe.wait_ge(s["ones"], 1)
                pe.wait_ge(s["keys"], 16)
                nc.tensor.matmul(pk[:, 0:KEYS], onesr[0:1, :], krow[0:1, :], start=True, stop=True).then_inc(s["pk_ok"], 1)
                pe.wait_ge(s["masked"], 1)
                n = 0
                for part in (hi, lo):
                    for g in range(0, NPAIR, 4):
                        if n >= 4:
                            pe.wait_ge(s["pt_used"], n - 3)
                        for m in range(g, min(g + 4, NPAIR)):
                            mm = nc.tensor.transpose(ptr[:, n % 4, (m - g) * P:(m - g + 1) * P],
                                                     part[:, 2 * m:2 * m + 2, :].rearrange("p a b -> p (a b)"), ident[:, :])
                        mm.then_inc(s["pt_ok"], 1)
                        n += 1

            @block.scalar
            def _(act):
                n = 0
                for part in (hit, lot):
                    for g in range(0, NPAIR, 4):
                        w = min(4, NPAIR - g)
                        act.wait_ge(s["pt_ok"], n + 1)
                        nc.scalar.copy(part[:, g:g + w, :, :].rearrange("p a b c -> p (a b) c"), ptr[:, n % 4, 0:w * P].unsqueeze(2).to_broadcast([P, w * P, 2])).then_inc(s["pt_used"], 1)
                        n += 1

            @block.vector
            def _(dve):
                link = chain(dve, s["ch"], 0, None)
                TT, TS = nc.vector.tensor_tensor, nc.vector.tensor_scalar
                nc.vector.memset(onesr[:, :], 1.0).then_inc(s["ones"], 1)
                nc.vector.memset(ends[:, :], float(E)).then_inc(s["end"], 1)
                dve.wait_ge(s["pk_ok"], 1)
                dve.wait_ge(s["iota"], 2)
                for b in range(NB):
                    link(TS(junk[:, 0:KEYS], pk[:, 0:KEYS], dcol[:, b:b + 1], 0.0, ALU.is_lt, ALU.add, accum_out=coarse[:, b:b + 1]))
                link(TS(offf[:, :], coarse[:, :], -1.0, 0.0, ALU.add, ALU.max))
                link(TS(offf[:, :], offf[:, :], float(RUN), None, ALU.mult))
                nc.vector.tensor_copy(offi[:, :], offf[:, :]).then_inc(s["off"], 1)
                for b in range(NB):
                    dve.wait_ge(run_in[b % 4], 16 * (b // 4 + 1))
                    TS(junk[:, :], runs[:, b % 4, :], dcol[:, b:b + 1], 0.0, ALU.is_lt, ALU.add, accum_out=fine[:, b:b + 1]).then_inc(s["fine"], 1)
                    dve.wait_ge(s["fine"], b + 1)
                link(TT(rs[:, :], offf[:, :], fine[:, :], ALU.add))
                link(nc.vector.tensor_copy(rsi[:, :], rs[:, :]))
                dve.sem_inc(s["rs"], 1)
                dve.sem_inc(s["rsi"], 1)
                link(nc.vector.memset(deg[:, :], 0.0))
                dve.wait_ge(s["rn_in"], 16)
                link(TT(deg[:, 0:NB], rn[:, :], rs[:, :], ALU.subtract))
                dve.wait_ge(s["chk_in"], 32)
                link(TT(ea[:, :], ea[:, :], eb[:, :], ALU.is_gt))
                link(nc.vector.tensor_reduce(bad[:, 0:1], ea[:, :], AX, ALU.max))
                link(nc.vector.tensor_reduce(bad[:, 1:2], deg[:, 0:NB - 1], AX, ALU.max))
                link(TT(bad[0:LAST, 1:2], bad[0:LAST, 1:2], deg[0:LAST, NB - 1:NB], ALU.max))
                link(TS(bad[:, 1:2], bad[:, 1:2], float(SLOT), None, ALU.is_gt))
                TT(bad[:, 2:3], bad[:, 0:1], bad[:, 1:2], ALU.max).then_inc(s["badp"], 1)
                dve.wait_ge(s["badr"], 1)
                link(nc.vector.tensor_copy(slow[0:1, 0:1], bad[0:1, 3:4]))
                dve.wait_ge(slot_in, 16 * NB)
                link(nc.vector.memset(slots[:, NB:2 * NPAIR, :], 0.0))
                link(nc.vector.tensor_copy(sint[:, :, :], slots[:, :, :]))
                link(TS(sint2[:, :, :], sint[:, :, :], 7, None, ALU.logical_shift_right))
                link(nc.vector.tensor_copy(hi[:, :, :], sint2[:, :, :]))
                link(TS(sint2[:, :, :], sint[:, :, :], P - 1, None, ALU.bitwise_and))
                link(nc.vector.tensor_copy(lo[:, :, :], sint2[:, :, :]))
                link(TT(slots[:, :, :], kio[:, :].unsqueeze(1).to_broadcast([P, 2 * NPAIR, SLOT]),
                        deg[:, :].unsqueeze(2).to_broadcast([P, 2 * NPAIR, SLOT]), ALU.is_ge))
                link(TS(slots[:, :, :], slots[:, :, :], 64.0, None, ALU.mult))
                link(TT(hi[:, :, :], hi[:, :, :], slots[:, :, :], ALU.add))
                dve.sem_inc(s["masked"], 1)

        J = 8
        NG = RT // J
        TC = RT // P
        assert NG * J == RT and TC * P == RT and (J + 1) * NB <= 512
        sic = sb(gst, "edge_src", [P, RT], I32)
        full = sb(gst, "edge_dst", [P, RT])
        hic = sb(gst, "edge_dst_high", [P, RT, 2], BF16)
        loc = sb(gst, "edge_dst_low", [P, RT, 2], BF16)
        cp = sb(gst, "places", [P, 2, (J + 1) * NB])
        place_of = sb(gst, "edge_place", [P, RT], I32)
        with ExitStack() as st:
            en = sb(st, "edge_rows", [P, 2, TC, P], I32)
            ep = sb(st, "edge_part", [P, TC, P], I32)
            ef = sb(st, "edge_rows_f", [P, 4, TC, P])
            lob = sb(st, "edge_low_rows", [P, TC, P], BF16)
            iob = sb(st, "low_ids_s", [P, P], BF16)
            zi = sb(st, "zero_int", [P, RT], I32)
            dlo = sb(st, "dst_low_onehot", [P, 2, J, P], BF16)
            dhi = sb(st, "dst_high_onehot", [P, 2, J, HB], BF16)
            dg = sb(st, "dst_counts", [P, NB])
            cs = sb(st, "block_counts", [P, 2, NB])
            on = sb(st, "ones_nb", [P, NB])
            bad = sb(st, "router_bad", [P, 4])
            ptr = ps(st, "ps_edges", [P, 2, 512])
            pcn = ps(st, "ps_node_counts", [P, 512])
            prs = ps(st, "ps_starts", [P, 2, 64])
            names = ["in", "ch", "parts", "tabs", "pt_ok", "pt_used", "iota", "dz", "oh", "cnt", "rs_ps", "sl0", "badp", "badr", "cntall"]
            s = {k: sem(f"sort_{k}") for k in names}
            block = phase(st)

            @block.sync
            def _(sp):
                for k in range(2):
                    sp.dma_start(en[:, k, :, :], edges[k:k + 1, :].rearrange("k (c t p) -> t (k c) p", p=P, c=TC)).then_inc(s["in"], 16)
                sp.wait_ge(s["parts"], 1)
                sp.dma_start(RDF.rearrange("(c t p) -> t c p", p=P, c=TC), ef[:, 1, :, :]).then_inc(s["tabs"], 16)
                sp.dma_start(RDL.rearrange("(c t p) -> t c p", p=P, c=TC), lob[:, :, :]).then_inc(s["tabs"], 16)
                sp.wait_ge(s["dz"], 1)
                sp.dma_start(SL.rearrange("(p t) c -> p (t c)", p=P), zi[:, :]).then_inc(s["sl0"], 16)
                sp.wait_ge(s["tabs"], 32)
                sp.wait_ge(s["sl0"], 16)

            @block.gpsimd
            def _(pool):
                nc.gpsimd.iota(iob[:, :], pattern=[[1, P]], base=0, channel_multiplier=0, allow_small_or_imprecise_dtypes=True).then_inc(s["iota"], 1)
                pool.wait_ge(s["badp"], 1)
                nc.gpsimd.partition_all_reduce(bad[:, 3:4], bad[:, 2:3], P, bass.bass_isa.ReduceOp.max).then_inc(s["badr"], 1)

            @block.vector
            def _(dve):
                link = chain(dve, s["ch"], 0, None)
                TT, TS = nc.vector.tensor_tensor, nc.vector.tensor_scalar
                nc.vector.memset(zi[:, :], 0).then_inc(s["dz"], 1)
                link(nc.vector.memset(on[:, :], 1.0))
                dve.wait_ge(s["in"], 32)
                link(TS(en[:, 0, :, :], en[:, 0, :, :], float(N - 1), None, ALU.min))
                link(TS(en[:, 1, :, :], en[:, 1, :, :], float(NP - 1), None, ALU.min))
                link(nc.vector.tensor_copy(ef[:, 0:2, :, :].rearrange("p a b c -> p (a b c)"), en[:, :, :, :].rearrange("p a b c -> p (a b c)")))
                link(TS(ef[:, 2, :, :], ef[:, 1, :, :], float(N), float(NP), ALU.is_ge, ALU.mult))
                link(TT(ef[:, 1, :, :], ef[:, 1, :, :], ef[:, 2, :, :], ALU.add))
                link(TS(ef[:, 1, :, :], ef[:, 1, :, :], float(NP - 1), None, ALU.min))
                link(nc.vector.tensor_copy(en[:, 1, :, :], ef[:, 1, :, :]))
                link(TS(ep[:, :, :], en[:, 1, :, :], 7, None, ALU.logical_shift_right))
                link(nc.vector.tensor_copy(ef[:, 2, :, :], ep[:, :, :]))
                link(TS(ep[:, :, :], en[:, 1, :, :], P - 1, None, ALU.bitwise_and))
                link(nc.vector.tensor_copy(ef[:, 3, :, :], ep[:, :, :]))
                link(nc.vector.tensor_copy(lob[:, :, :], ep[:, :, :]))
                dve.sem_inc(s["parts"], 1)
                dve.wait_ge(s["pt_used"], 4 * TC // 4)
                dve.wait_ge(s["iota"], 1)

                def onehots(g, q, sem_):
                    one_hot(nc, dlo[:, q, :, :], loc[:, bass.ds(g * J, J), :], iob[:, :]).then_inc(sem_, 1)
                    one_hot(nc, dhi[:, q, :, :], hic[:, bass.ds(g * J, J), :], iob[:, 0:HB]).then_inc(sem_, 1)

                def count(g, q, m):
                    if after(g, 2):
                        hold(dve, s["cnt"], g - 1)
                    onehots(g, q, s["oh"])

                steps(dve, [(0, count)], NG)
                dve.wait_ge(s["cnt"], NG)
                dve.wait_ge(s["cntall"], 1)
                link(nc.vector.memset(dg[:, :], 0.0))
                link(nc.vector.tensor_copy(dg[:, 0:NB - 1], pcn[:, 0:NB - 1]))
                link(nc.vector.tensor_copy(dg[0:LAST, NB - 1:NB], pcn[0:LAST, NB - 1:NB]))
                link(nc.vector.tensor_copy(rdeg[:, :], dg[:, :]))
                link(nc.vector.tensor_reduce(bad[:, 1:2], dg[:, :], AX, ALU.max))
                TS(bad[:, 2:3], bad[:, 1:2], float(RK), None, ALU.is_gt).then_inc(s["badp"], 1)
                dve.wait_ge(s["rs_ps"], 1)
                link(nc.vector.tensor_copy(cs[:, 0, :], prs[:, 1, 0:NB]))
                link(nc.vector.tensor_tensor_scan(cs[:, 1, :], on[:, :], cs[:, 0, :], 0.0, ALU.mult, ALU.add))
                link(TT(cs[:, 1, :], cs[:, 1, :], cs[:, 0, :], ALU.subtract))
                link(TT(cs[:, 0, :], cs[:, 1, :], prs[:, 0, 0:NB], ALU.add))
                link(nc.vector.tensor_copy(rsi2[:, :], cs[:, 0, :]))
                link(nc.vector.tensor_copy(cp[:, 1, J * NB:(J + 1) * NB], cs[:, 0, :]))
                dve.wait_ge(s["badr"], 1)
                link(nc.vector.tensor_copy(slow[0:1, 1:2], bad[0:1, 3:4]))
            @block.scalar
            def _(act):
                n = 0
                for to in (sic, full, hic, loc):
                    for c in range(0, TC, 4):
                        act.wait_ge(s["pt_ok"], n + 1)
                        if to is hic or to is loc:
                            nc.scalar.copy(to[:, c * P:(c + 4) * P, :], ptr[:, n % 2, :].unsqueeze(2).to_broadcast([P, 4 * P, 2])).then_inc(s["pt_used"], 1)
                        else:
                            nc.scalar.copy(to[:, c * P:(c + 4) * P], ptr[:, n % 2, :]).then_inc(s["pt_used"], 1)
                        n += 1
            @block.tensor
            def _(pe):
                pe.wait_ge(s["parts"], 1)
                n = 0
                for k in range(4):
                    for c in range(0, TC, 4):
                        if n >= 2:
                            pe.wait_ge(s["pt_used"], n - 1)
                        for i in range(4):
                            mm = nc.tensor.transpose(ptr[:, n % 2, i * P:(i + 1) * P], ef[:, k, c + i, :], ident[:, :])
                        mm.then_inc(s["pt_ok"], 1)
                        n += 1
                nc.tensor.matmul(pcn[:, 0:NB], ident[:, :], zero[:, 0:NB], start=True, stop=True, skip_group_check=True)

                def count(g, q, m):
                    hold(pe, s["oh"], g * 2 + 2)
                    for j in range(J):
                        mm = nc.tensor.matmul(pcn[:, 0:NB], dlo[:, q, j, :], dhi[:, q, j, 0:NB], start=False, stop=True, skip_group_check=True)
                    mm.then_inc(s["cnt"], 1)

                steps(pe, [(0, count)], NG)
                pe.drain().then_inc(s["cntall"], 1)
                pe.wait_ge(s["badp"], 1)
                nc.tensor.matmul(prs[:, 0, 0:NB], upper[:, :], dg[:, :], start=True, stop=True)
                nc.tensor.matmul(prs[:, 1, 0:NB], ones[:, :], dg[:, :], start=True, stop=True).then_inc(s["rs_ps"], 1)
        G = 8
        ROUNDS = P // G
        with ExitStack() as st:
            at = sb(st, "counts", [P, 2, P, 2 * HB], F16)
            ohl = sb(st, "low_onehot", [P, 2, 2 * G, P], BF16)
            ohh = sb(st, "high_onehot", [P, 2, 2 * G, 2 * HB], BF16)
            iol = sb(st, "low_ids", [P, P], BF16)
            dlt = sb(st, "dst_low_onehot_cols", [P, 2, J * P])
            brf = sb(st, "dst_spread", [P, 2, J * P])
            brl = sb(st, "dst_low_spread", [P, 2, J * P], BF16)
            r0 = sb(st, "rank_in_tile", [P, 2, J])
            tz = sb(st, "looked_up", [P, 2, J * NB])
            z = sb(st, "rank_before", [P, 2, J])
            junk = sb(st, "sort_junk", [P, J, P], BF16)
            pid = sb(st, "partition_ids", [P, 1])
            dlo = sb(st, "dst_low_onehot_s", [P, 2, J, P], BF16)
            dhi = sb(st, "dst_high_onehot_s", [P, 2, J, HB], BF16)
            pc = ps(st, "ps_places", [P, 512])
            pz = ps(st, "ps_lookup", [P, 512])
            r = {k: sem(f"place_{k}") for k in ("iota", "oh2", "pc", "cp", "pz", "tz", "rk", "po")}
            br_in = [sem("place_spread0"), sem("place_spread1")]
            po = sb(st, "place_stage", [P, 2, J], I32)
            sv = sb(st, "src_stage", [P, 2, J], I32)
            staged, sc_ok = sem("scatter_staged"), [sem("scatter_done0"), sem("scatter_done1")]
            hs = sb(st, "sum_high", [P, 2, D])
            ns = sb(st, "sums", [P, 2, D])
            pb = ps(st, "ps_counts", [P, 2, 2, 512])
            pm = ps(st, "ps_sums", [P, 2, 512])
            names = ["iota", "hz", "oh", "cnt_ps", "cnt_ok", "sum_ps", "hs", "ns", "deg_out"]
            s = {k: sem(f"sum_{k}f") for k in names}
            ns_out = [sem("sum_out0"), sem("sum_out1")]
            block = phase(st)
            PG = NG // NPAIR
            assert PG % 2 == 1

            def group_steps(stages, i):
                def body(b, q, m):
                    for lag, work in stages:
                        c = i - lag
                        if after(b, 1) or c >= 0:
                            work(b * PG + c, (q + c) % 2, m * PG + (q * PG + c) // 2)
                return body

            def group_rest(stages):
                for t in range(NPAIR * PG, NG + max(lag for lag, _ in stages)):
                    for lag, work in stages:
                        if t - lag < NG:
                            work(t - lag, (t - lag) % 2, (t - lag) // 2)

            @block.sync
            def _(sp):
                with nc.allow_non_contiguous_dma(reason="a column of degrees"):
                    sp.dma_start(ACC[:, D:D + 1].rearrange("(b p) c -> p b c", p=P), deg[:, :].unsqueeze(2)).then_inc(s["deg_out"], 16)

                def store(m, q, h):
                    for j in range(2):
                        hold(sp, s["ns"], m * 2 + (j + 1))
                        sp.dma_start(ACC[bass.ds((m * 2 + j) * P, P), 0:D], ns[:, j, :]).then_inc(ns_out[j], 16)


                def spread(g, q, m):
                    if after(g, 2):
                        hold(sp, r["oh2"], g * 11 - 11)
                    sp.dma_start(brf[:, q, :], RDF[bass.ds(g * (J * P), J * P)].partition_broadcast(P)).then_inc(br_in[q], 16)
                    sp.dma_start(brl[:, q, :], RDL[bass.ds(g * (J * P), J * P)].partition_broadcast(P)).then_inc(br_in[q], 16)

                steps(sp, [*((0, group_steps([(0, spread)], i)) for i in range(PG)), (1, store)], NPAIR)
                group_rest([(0, spread)])
                for j in range(2):
                    sp.wait_ge(ns_out[j], 16 * NPAIR)
                sp.wait_ge(s["deg_out"], 16)

            @block.gpsimd
            def _(pool):
                nc.gpsimd.iota(iol[:, :], pattern=[[1, P]], base=0, channel_multiplier=0, allow_small_or_imprecise_dtypes=True).then_inc(s["iota"], 1)
                nc.gpsimd.iota(pid[:, :], pattern=[[0, 1]], base=0, channel_multiplier=1, allow_small_or_imprecise_dtypes=True).then_inc(s["iota"], 1)

                def stage(g, q, m):
                    if after(g, 2):
                        hold(pool, sc_ok[q], m * 16 * J)
                    hold(pool, r["po"], g + 1)
                    nc.gpsimd.tensor_copy(po[:, q, :], place_of[:, bass.ds(g * J, J)]).then_inc(staged, 1)
                    nc.gpsimd.tensor_copy(sv[:, q, :], sic[:, bass.ds(g * J, J)]).then_inc(staged, 1)

                def scatter(g, q, m):
                    hold(pool, staged, g * 2 + 2)
                    for j in range(J):
                        nc.gpsimd.indirect_dma_start(SL, bass.IndirectOffsetOnAxis(ap=po[:, q, j:j + 1], axis=0), sv[:, q, j:j + 1], None,
                                                     bounds_check=RT * P - 1, oob_is_err=False).then_inc(sc_ok[q], 16)

                steps(pool, [(1, scatter), (0, stage)], NG)
                for q in range(2):
                    pool.wait_ge(sc_ok[q], 16 * J * NG // 2)

            @block.vector
            def _(dve):
                for q in range(2):
                    nc.vector.memset(ohh[:, q, :, :], 0.0).then_inc(s["hz"], 1)
                dve.wait_ge(s["iota"], 2)
                dve.wait_ge(s["hz"], 2)
                TT, TS = nc.vector.tensor_tensor, nc.vector.tensor_scalar

                def onehots(g):
                    def body(m, q, h):
                        u = g % 2
                        if after(m, 1) or g >= 2:
                            hold(dve, s["cnt_ps"], m * ROUNDS + 2 * (g - 1))
                        ids = lambda t, a, b: t[a:b, bass.ds(m, 1), g * 2 * G:(g + 1) * 2 * G, :].rearrange("p a b c -> p (a b) c")
                        one_hot(nc, ohl[:, u, :, :], ids(lot, 0, P), iol[:, :]).then_inc(s["oh"], 1)
                        for j in range(2):
                            a, b = j * SLOT, (j + 1) * SLOT
                            one_hot(nc, ohh[a:b, u, :, j * HB:(j + 1) * HB], ids(hit, a, b), iol[a:b, 0:HB]).then_inc(s["oh"], 1)
                    return body

                def sums(m, q, h):
                    for j in range(2):
                        hold(dve, s["hs"], m * 2 + (j + 1))
                        if after(m, 1):
                            hold(dve, ns_out[j], m * 16)
                        nc.vector.scalar_tensor_tensor(out=ns[:, j, :], in0=pm[:, j, D:2 * D], scalar=1.0 / (UP * DOWN), in1=hs[:, j, :],
                                                       op0=ALU.mult, op1=ALU.add).then_inc(s["ns"], 1)


                def dst_onehots(g, q):
                    one_hot(nc, dlo[:, q, :, :], loc[:, bass.ds(g * J, J), :], iol[:, :]).then_inc(r["oh2"], 1)
                    one_hot(nc, dhi[:, q, :, :], hic[:, bass.ds(g * J, J), :], iol[:, 0:HB]).then_inc(r["oh2"], 1)

                def place(g, q, m):
                    if after(g, 2):
                        hold(dve, r["po"], g - 1)
                        hold(dve, r["pz"], g - 1)
                    hold(dve, br_in[q], m * 32 + 32)
                    dst_onehots(g, q)
                    TS(dlt[:, q, :], brl[:, q, :], pid[:, 0:1], None, ALU.is_equal).then_inc(r["oh2"], 1)
                    if after(g, 1):
                        hold(dve, r["oh2"], g * 11)
                    for j in range(J):
                        nc.vector.scalar_tensor_tensor(out=junk[:, j, :], in0=brf[:, q, j * P:(j + 1) * P], scalar=fcol(g, j), in1=lower[:, :],
                                                       op0=ALU.is_equal, op1=ALU.mult, accum_out=r0[:, q, j:j + 1]).then_inc(r["oh2"], 1)

                def fcol(g, j):
                    return full[:, bass.ds(g * J + j, 1)]

                def rank(g, q, m):
                    hold(dve, r["pz"], g + 1)
                    hold(dve, r["oh2"], g * 11 + 11)
                    TT(tz[:, q, :].rearrange("p (a b) -> p a b", a=J), dhi[:, q, :, 0:NB], pz[:, 0:J * NB].rearrange("p (a b) -> p a b", a=J), ALU.mult).then_inc(r["tz"], 1)
                    hold(dve, r["tz"], g + 1)
                    l = chain(dve, r["rk"], g, 1)
                    l(nc.vector.tensor_reduce(z[:, q, :], tz[:, q, :].rearrange("p (a b) -> p a b", a=J), AX, ALU.add))
                    TT(place_of[:, bass.ds(g * J, J)], z[:, q, :], r0[:, q, :], ALU.add).then_inc(r["po"], 1)

                work, i = [(0, place), (1, rank)], 0
                stages = []
                for g in range(ROUNDS // 2):
                    stages.append((0, onehots(g)))
                    if i < PG and g >= (3 * i + 3) // 2:
                        stages.append((0, group_steps(work, i)))
                        i += 1
                assert i == PG
                steps(dve, [*stages, (1, sums)], NPAIR)
                group_rest(work)

            @block.scalar
            def _(act):
                def counts(g):
                    def body(m, q, h):
                        if g == 0 and after(m, 2):
                            hold(act, s["sum_ps"], m * 2 - 2)
                        hold(act, s["cnt_ps"], m * ROUNDS + (g + 1))
                        nc.scalar.copy(at[:, q, g * G:(g + 1) * G, :].rearrange("p (k a) b -> p k (a b)", k=2),
                                       pb[:, g % 2, :, 0:G * HB]).then_inc(s["cnt_ok"], 1)
                    return body

                def highs(m, q, h):
                    for j in range(2):
                        hold(act, s["sum_ps"], m * 2 + (j + 1))
                        if after(m, 1):
                            hold(act, s["ns"], m * 2 + (j - 1))
                        nc.scalar.activation(hs[:, j, :], pm[:, j, 0:D], ACT.Copy, scale=1.0 / UP).then_inc(s["hs"], 1)


                def places(g, q, m):
                    hold(act, r["pc"], g + 1)
                    if after(g, 2):
                        hold(act, r["pz"], g - 1)
                    nc.scalar.copy(cp[:, q, :], pc[:, 0:(J + 1) * NB]).then_inc(r["cp"], 1)

                stages = []
                for g in range(ROUNDS):
                    stages.append((0, counts(g)))
                    if g % 3 == 0 and g > 0:
                        stages.append((0, group_steps([(0, places)], g // 3 - 1)))
                steps(act, [*stages, (1, highs)], NPAIR)
                group_rest([(0, places)])

            @block.tensor
            def _(pe):
                def build(g):
                    def body(m, q, h):
                        if g % 2 == 0:
                            hold(pe, s["oh"], (m * (ROUNDS // 2) + (g // 2)) * 3 + 3)
                        if after(m, 1) or g >= 2:
                            hold(pe, s["cnt_ok"], m * ROUNDS + (g - 1))
                        for i in range(G):
                            c, u = (g % 2) * G + i, (g // 2) % 2
                            w = i % (G // 2) * 2 * HB
                            mm = nc.tensor.matmul(pb[:, g % 2, i // (G // 2), w:w + 2 * HB], ohl[:, u, c, :], ohh[:, u, c, :], start=True, stop=True)
                        mm.then_inc(s["cnt_ps"], 1)
                    return body

                def multiply(g):
                    def body(m, q, h):
                        if g == 0:
                            hold(pe, s["cnt_ok"], m * ROUNDS + ROUNDS)
                        for n in range(2 * NB * g // ROUNDS, 2 * NB * (g + 1) // ROUNDS):
                            j, k = n // NB, n % NB
                            if k == 0 and after(m, 1):
                                hold(pe, s["ns"], m * 2 + (j - 1))
                            mm = nc.tensor.matmul(pm[:, j, :], at[:, q, :, j * HB + k], xhl[:, k, :], start=k == 0, stop=k == NB - 1)
                            if k == NB - 1:
                                mm.then_inc(s["sum_ps"], 1)
                    return body


                def prefix(g, q, m):
                    if after(g, 1):
                        hold(pe, r["cp"], g)
                    hold(pe, r["oh2"], g * 11 + 2)
                    nc.tensor.matmul(pc[:, 0:(J + 1) * NB].rearrange("p (a b) -> p a b", b=NB), ident[:, :],
                                     cp[:, 1 - q, J * NB:(J + 1) * NB].unsqueeze(1).to_broadcast([P, J + 1, NB]), start=True, stop=True, skip_group_check=True)
                    for j in range(J):
                        mm = nc.tensor.matmul(pc[:, (j + 1) * NB:(J + 1) * NB].rearrange("p (a b) -> p a b", b=NB), dlo[:, q, j, :],
                                              dhi[:, q, j:j + 1, 0:NB].to_broadcast([P, J - j, NB]), start=False, stop=True, skip_group_check=True)
                    mm.then_inc(r["pc"], 1)

                def lookup(g, q, m):
                    hold(pe, r["cp"], g + 1)
                    hold(pe, r["oh2"], g * 11 + 3)
                    if after(g, 1):
                        hold(pe, r["tz"], g)
                    for j in range(J):
                        mm = nc.tensor.matmul(pz[:, j * NB:(j + 1) * NB], dlt[:, q, j * P:(j + 1) * P], cp[:, q, j * NB:(j + 1) * NB], start=True, stop=True)
                    mm.then_inc(r["pz"], 1)

                stages = []
                for g in range(ROUNDS):
                    stages += [(0, build(g)), (1, multiply(g))]
                    if g % 3 == 1 and g < ROUNDS - 1:
                        stages.append((0, group_steps([(1, lookup)], g // 3)))
                    if g % 3 == 0 and g > 0:
                        stages.append((0, group_steps([(0, prefix)], g // 3 - 1)))
                steps(pe, stages, NPAIR)
                group_rest([(1, lookup), (0, prefix)])


        gst.close()

        edge_pass("sum")

        X = sb(top, "x1_rows", [P, NB, D])
        ag = sb(top, "attention", [P, NB, PAY])
        T = sb(top, "router_rows", [P, NB, PAY])
        AD = sb(top, "a_dst_rows", [P, NB, GH])
        MXS = sb(top, "max_rows", [P, NB, GH])
        gate = sb(top, "gates", [P, NB, NE])
        xst = ExitStack()
        XT = sb(xst, "x1n_cols", [P, KD, NP])
        with ExitStack() as st:
            wg = sb(st, "gnn_w_sb", [P, 2 * KD, D])
            bias = sb(st, "bias_row", [1, 2 * D])
            nm = sb(st, "neigh_rows", [P, 2, D])
            xg = sb(st, "xn_again", [P, 2, D])
            nt = sb(st, "node_cols", [P, 2, 2 * KD * P])
            dgi = sb(st, "degree_inverse", [P, NB])
            R = sb(st, "gnn_rows", [P, NB, D])
            rsq = sb(st, "gnn_squares", [P, 2, C, D])
            rn = sb(st, "gnn_row_norms", [P, 3, NB])
            bs = sb(st, "ln_stats", [P, NB, 6])
            mv = sb(st, "ln_mean_var", [P, NB, 2])
            sd = sb(st, "x1_std", [P, 3, NB])
            ta = sb(st, "att_products", [P, NB, GW])
            pt = ps(st, "ps_turn", [P, 2, 512])
            pg = ps(st, "ps_node", [P, 2, 512])
            p1 = ps(st, "ps_turn_x1", [P, 2, 512])
            ph = ps(st, "ps_router", [P, 2, 512])
            nin = [sem("node_in0"), sem("node_in1")]
            names = ["w_in", "x_in", "deg_in", "deg", "mean", "nt_ps", "nt_ok", "g_ok", "r_ok", "u_ok", "sq", "ss", "nrm", "inv", "x1", "bn", "mv",
                     "var", "std", "rstd", "xn", "xt_ps", "xt_ok", "h_ps", "h_ok", "att", "tab_out"]
            s = {k: sem(f"node_{k}") for k in names}
            block = phase(st)
            row = lambda t, b: t[:, bass.ds(b, 1), :].rearrange("p a b -> p (a b)")

            @block.sync
            def _(sp):
                sp.dma_start(dgi[:, :].unsqueeze(2), by_block(ACC[0:NP, D:D + 1])).then_inc(s["deg_in"], 16)
                for to, fr in ((wg[:, :, :], gnn_w.rearrange("(j p) d -> p j d", p=P)), (bias[0:1, 0:D], gnn_b.unsqueeze(0)),
                               (bias[0:1, D:2 * D], b_out.unsqueeze(0))):
                    sp.dma_start(to, fr).then_inc(s["w_in"], 16)

                def load(b, q, m):
                    if after(b, 2):
                        hold(sp, s["nt_ps"], b - 1)
                    sp.dma_start(nm[:, q, :], ACC[bass.ds(b * P, P), 0:D]).then_inc(nin[q], 16)
                    sp.dma_start(xg[:, q, :], XN[bass.ds(b * P, P), :]).then_inc(nin[q], 16)

                steps(sp, [(0, load)], NB)
                sp.wait_ge(s["att"], 4)
                sp.dma_start(by_block(TAB), T[:, :, :]).then_inc(s["tab_out"], 16)
                sp.wait_ge(s["tab_out"], 16)

            @block.tensor
            def _(pe):
                pe.wait_ge(s["w_in"], 48)

                def turn(b, q, m):
                    hold(pe, s["mean"], b + 1)
                    if after(b, 2):
                        hold(pe, s["nt_ok"], b - 1)
                    for k in range(2 * KD):
                        rows_ = xg if k < KD else nm
                        mm = nc.tensor.transpose(pt[:, q, k * P:(k + 1) * P], rows_[:, q, k % KD * P:(k % KD + 1) * P], ident[:, :])
                    mm.then_inc(s["nt_ps"], 1)

                def node(b, q, m):
                    hold(pe, s["nt_ok"], b + 1)
                    if after(b, 2):
                        hold(pe, s["r_ok"], b - 1)
                        hold(pe, s["u_ok"], b - 1)
                    nc.tensor.matmul(pg[:, q, :], ones[0:1, :], bias[0:1, :], start=True, stop=True, skip_group_check=True)
                    for k in range(2 * KD):
                        nc.tensor.matmul(pg[:, q, 0:D], nt[:, q, k * P:(k + 1) * P], wg[:, k, :], start=False, stop=True, skip_group_check=True)
                    for k in range(KD):
                        mm = nc.tensor.matmul(pg[:, q, D:2 * D], nt[:, q, k * P:(k + 1) * P], mix[:, k, :], start=False, stop=True, skip_group_check=True)
                    mm.then_inc(s["g_ok"], 1)

                steps(pe, [(2, node), (0, turn)], NB)

                for b in range(NB + 1):
                    if b < NB:
                        pe.wait_ge(s["xn"], b + 1)
                        if b >= 2:
                            pe.wait_ge(s["xt_ok"], b - 1)
                        for k in range(KD):
                            mm = nc.tensor.transpose(p1[:, b % 2, k * P:(k + 1) * P], R[:, b, k * P:(k + 1) * P], ident[:, :])
                        mm.then_inc(s["xt_ps"], 1)
                    if b:
                        d = b - 1
                        c, i = d // C, d % C
                        pe.wait_ge(s["xt_ok"], d + 1)
                        if i == 0 and c >= 2:
                            pe.wait_ge(s["h_ok"], c - 1)
                        for k in range(KD):
                            mm = nc.tensor.matmul(ph[:, c % 2, i * GW:(i + 1) * GW], XT[:, k, d * P:(d + 1) * P], wgat[:, k, :], start=k == 0, stop=k == KD - 1)
                        if i == C - 1:
                            mm.then_inc(s["h_ps"], 1)

            @block.scalar
            def _(act):
                def columns(b, q, m):
                    hold(act, s["nt_ps"], b + 1)
                    if after(b, 2):
                        hold(act, s["g_ok"], b - 1)
                    nc.scalar.copy(nt[:, q, :], pt[:, q, :]).then_inc(s["nt_ok"], 1)

                for c in range(NC):
                    act.dma_start(X[:, c * C:(c + 1) * C, :], by_block(XP[c * C * P:(c + 1) * C * P, :])).then_inc(s["x_in"], 16)
                steps(act, [(0, columns)], NB)
                for c in range(NC):
                    act.wait_ge(s["r_ok"], (c + 1) * C)
                    if c >= 2:
                        act.wait_ge(s["ss"], c - 1)
                    nc.scalar.activation(rsq[:, c % 2, :, :], R[:, c * C:(c + 1) * C, :], ACT.Square).then_inc(s["sq"], 1)
                act.wait_ge(s["ss"], NC)
                nc.scalar.activation(rn[:, 1, :], rn[:, 0, :], ACT.Sqrt).then_inc(s["nrm"], 1)
                for c in range(NC + 1):
                    if c < NC:
                        act.wait_ge(s["var"], c + 1)
                        nc.scalar.activation(sd[:, 1, c * C:(c + 1) * C], sd[:, 0, c * C:(c + 1) * C], ACT.Sqrt).then_inc(s["std"], 1)
                    if c:
                        for b in range((c - 1) * C, c * C):
                            act.wait_ge(s["xt_ps"], b + 1)
                            nc.scalar.copy(XT[:, :, b * P:(b + 1) * P], p1[:, b % 2, 0:KD * P].rearrange("p (k n) -> p k n", k=KD)).then_inc(s["xt_ok"], 1)

            @block.vector
            def _(dve):
                TT, TS = nc.vector.tensor_tensor, nc.vector.tensor_scalar
                dve.wait_ge(s["deg_in"], 16)
                link = chain(dve, s["deg"], 0, 2)
                link(TS(dgi[:, :], dgi[:, :], 1.0, None, ALU.max))
                link(nc.vector.reciprocal(dgi[:, :], dgi[:, :]))

                def mean(b, q, m):
                    hold(dve, nin[q], m * 32 + 32)
                    TS(nm[:, q, :], nm[:, q, :], dgi[:, bass.ds(b, 1)], None, ALU.mult).then_inc(s["mean"], 1)

                def rows(b, q, m):
                    if not after(b, 1):
                        dve.wait_ge(s["x_in"], 16 * NC)
                    hold(dve, s["g_ok"], b + 1)
                    TS(row(R, b), pg[:, q, 0:D], 0.0, None, ALU.max).then_inc(s["r_ok"], 1)
                    TT(row(X, b), pg[:, q, D:2 * D], row(X, b), ALU.add).then_inc(s["u_ok"], 1)

                steps(dve, [(0, mean), (2, rows)], NB)
                for c in range(NC):
                    dve.wait_ge(s["sq"], c + 1)
                    nc.vector.tensor_reduce(rn[:, 0, c * C:(c + 1) * C], rsq[:, c % 2, :, :], AX, ALU.add).then_inc(s["ss"], 1)
                dve.wait_ge(s["nrm"], 1)
                link = chain(dve, s["inv"], 0, 2)
                link(TS(rn[:, 1, :], rn[:, 1, :], GNN_EPS, None, ALU.max))
                link(nc.vector.reciprocal(rn[:, 2, :], rn[:, 1, :]))
                dve.wait_ge(s["u_ok"], NB)
                for c in range(NC + 2):
                    if c < NC:
                        bl = range(c * C, (c + 1) * C)
                        for b in bl:
                            nc.vector.scalar_tensor_tensor(out=X[:, b, :], in0=R[:, b, :], scalar=rn[:, 2, b:b + 1], in1=X[:, b, :], op0=ALU.mult, op1=ALU.add).then_inc(s["x1"], 1)
                        dve.wait_ge(s["x1"], (c + 1) * C)
                        for b in bl:
                            nc.vector.bn_stats(bs[:, b, :], X[:, b, :]).then_inc(s["bn"], 1)
                        dve.wait_ge(s["bn"], (c + 1) * C)
                        for b in bl:
                            nc.vector.bn_aggr(mv[:, b, :], bs[:, b, :]).then_inc(s["mv"], 1)
                        dve.wait_ge(s["mv"], (c + 1) * C)
                        TS(sd[:, 0, c * C:(c + 1) * C], mv[:, c * C:(c + 1) * C, 1], LN_EPS, None, ALU.add).then_inc(s["var"], 1)
                    if 1 <= c <= NC:
                        d = c - 1
                        dve.wait_ge(s["std"], d + 1)
                        nc.vector.reciprocal(sd[:, 2, d * C:(d + 1) * C], sd[:, 1, d * C:(d + 1) * C]).then_inc(s["rstd"], 1)
                        dve.wait_ge(s["rstd"], d + 1)
                        for b in range(d * C, (d + 1) * C):
                            TS(R[:, b, :], X[:, b, :], mv[:, b, 0:1], sd[:, 2, b:b + 1], ALU.subtract, ALU.mult).then_inc(s["xn"], 1)
                    if c >= 2:
                        d = c - 2
                        dve.wait_ge(s["h_ps"], d + 1)
                        nc.vector.tensor_copy(T[:, d * C:(d + 1) * C, 0:GW], ph[:, d % 2, 0:C * GW].rearrange("p (b g) -> p b g", b=C)).then_inc(s["h_ok"], 1)
                dve.wait_ge(s["h_ok"], NC)
                link = chain(dve, s["att"], 0, 4)
                for k, to in ((0, T[:, :, GW:PAY]), (1, AD[:, :, :])):
                    link(TT(ta[:, :, :], T[:, :, 0:GW], att[:, k, :].unsqueeze(1).to_broadcast([P, NB, GW]), ALU.mult))
                    link(nc.vector.tensor_reduce(to, ta[:, :, :].rearrange("p b (h e) -> p b h e", e=NE), AX, ALU.add))

        CT = 16
        NCT = RT // CT
        with ExitStack() as st:
            w1s = sb(st, "w1_sb", [P, KD, NE, FF])
            w2s = sb(st, "w2_sb", [P, HT, D])
            b1r = sb(st, "b1_rows", [HT, P])
            b1c = sb(st, "b1_cols", [P, HT])
            b2r = sb(st, "b2_row", [1, NE * D])
            one = sb(st, "ones", [1, P])
            hid = sb(st, "hidden", [P, 2, HT * P])
            phid = ps(st, "ps_hidden", [P, 4, 512])
            py = ps(st, "ps_expert_out", [P, 2, NE * D])
            ys = sb(st, "expert_rows", [P, 2, NE * D])
            ix = sb(st, "gather_index", [P, 2, CT], I32)
            row_buf = sb(st, "gather_rows", [P, 2, CT, PAY])
            ix_in = [sem("gather_ix0"), sem("gather_ix1")]
            got = [sem("gather_got0"), sem("gather_got1")]
            outs = [sem("gather_out0"), sem("gather_out1")]
            tail = sem("gather_tail")
            names = ["b1_ps", "b1_ok", "one", "hps0", "hps1", "hps2", "hps3", "hid", "y_ps", "y_ok", "hb0", "hb1", "hb2", "hb3"]
            s = {k: sem(f"expert_{k}") for k in names}
            w_in, y_out = sem("expert_w_in"), [sem("expert_out0"), sem("expert_out1")]
            block = phase(st)

            @block.sync
            def _(sp):
                for e in range(NE):
                    sp.dma_start(w1s[:, :, e, :], w1[e].rearrange("(k p) f -> p k f", p=P)).then_inc(w_in, 16)
                sp.dma_start(w2s[:, :, :], w2.rearrange("e (t p) d -> p (e t) d", p=P)).then_inc(w_in, 16)
                sp.dma_start(b1r[:, :], b1.rearrange("e (t p) -> (e t) p", p=P)).then_inc(w_in, 16)
                sp.dma_start(b2r[0:1, :], b2.rearrange("(a e) d -> a (e d)", a=1)).then_inc(w_in, 16)
                for i in range(4):
                    sp.dma_start(GD[RT * P:, :].rearrange("(p a) c -> p a c", p=P)[:, i * RK // 4:(i + 1) * RK // 4, :],
                                 zero[:, 0:RK // 4 * PAY]).then_inc(tail, 16)

                def load(c, q, m):
                    if after(c, 2):
                        hold(sp, got[q], m * 16 * CT)
                    sp.dma_start(ix[:, q, :], SL[bass.ds(c * (CT * P), CT * P), :].rearrange("(p a) c -> p (a c)", p=P)).then_inc(ix_in[q], 16)

                def store(c, q, m):
                    hold(sp, got[q], m * 16 * CT + 16 * CT)
                    sp.dma_start(GD[bass.ds(c * (CT * P), CT * P), :].rearrange("(p a) c -> p (a c)", p=P),
                                 row_buf[:, q, :, :].rearrange("p a c -> p (a c)")).then_inc(outs[q], 16)

                steps(sp, [(0, load), (1, store)], NCT)
                for q in range(2):
                    sp.wait_ge(outs[q], 16 * NCT // 2)
                sp.wait_ge(tail, 64)

            @block.gpsimd
            def _(pool):
                def gather(c, q, m):
                    hold(pool, ix_in[q], m * 16 + 16)
                    if after(c, 2):
                        hold(pool, outs[q], m * 16)
                    for j in range(CT):
                        nc.gpsimd.indirect_dma_start(row_buf[:, q, j, :], None, TAB, bass.IndirectOffsetOnAxis(ap=ix[:, q, j:j + 1], axis=0)).then_inc(got[q], 16)

                steps(pool, [(0, gather)], NCT)

            @block.tensor
            def _(pe):
                pe.wait_ge(w_in, 16 * (NE + 3))
                nc.tensor.transpose(py[:, 0, 0:HT], b1r[:, :], ident[0:HT, 0:HT]).then_inc(s["b1_ps"], 1)
                pe.wait_ge(s["b1_ok"], 1)
                pe.wait_ge(s["one"], 1)

                def hidden(b, q, m):
                    for g in range(4):
                        if after(b, 1):
                            hold(pe, s[f"hb{g}"], b)
                        for t in range(4 * g, 4 * g + 4):
                            for k in range(KD):
                                mm = nc.tensor.matmul(phid[:, g, (t % 4) * P:(t % 4 + 1) * P],
                                                      w1s[:, k, t // FT, (t % FT) * P:(t % FT + 1) * P],
                                                      XT[:, k, bass.ds(b * P, P)], start=k == 0, stop=k == KD - 1)
                        mm.then_inc(s[f"hps{g}"], 1)

                def outputs(b, q, m):
                    hold(pe, s["hid"], b * 16 + 16)
                    if after(b, 2):
                        hold(pe, s["y_ok"], b - 1)
                    for e in range(NE):
                        y = py[:, q, e * D:(e + 1) * D]
                        nc.tensor.matmul(y, one[0:1, :], b2r[0:1, e * D:(e + 1) * D], start=True, stop=False)
                        for t in range(FT):
                            mm = nc.tensor.matmul(y, hid[:, q, (e * FT + t) * P:(e * FT + t + 1) * P], w2s[:, e * FT + t, :], start=False, stop=t == FT - 1)
                    mm.then_inc(s["y_ps"], 1)

                steps(pe, [(0, hidden), (1, outputs)], NB)

            @block.scalar
            def _(act):
                act.wait_ge(s["b1_ps"], 1)
                nc.scalar.copy(b1c[:, :], py[:, 0, 0:HT]).then_inc(s["b1_ok"], 1)
                act.wait_ge(s["b1_ok"], 1)

                def gelu(b, q, m):
                    if after(b, 2):
                        hold(act, s["y_ps"], b - 1)
                    for g in range(4):
                        hold(act, s[f"hps{g}"], b + 1)
                        for t in range(4 * g, 4 * g + 4):
                            i = nc.scalar.activation(hid[:, q, t * P:(t + 1) * P], phid[:, g, (t % 4) * P:(t % 4 + 1) * P], ACT.Gelu, bias=b1c[:, t:t + 1])
                            i.then_inc(s["hid"], 1)
                        hold(act, s["hid"], b * 16 + (4 * g + 4))
                        act.sem_inc(s[f"hb{g}"], 1)

                def store(b, q, m):
                    hold(act, s["y_ok"], b + 1)
                    act.dma_start(Y[bass.ds(b * P, P), :], ys[:, q, :]).then_inc(y_out[q], 16)

                steps(act, [(0, gelu), (2, store)], NB)
                for q in range(2):
                    act.wait_ge(y_out[q], 16 * ((NB + 1 - q) // 2))

            @block.vector
            def _(dve):
                nc.vector.memset(one[:, :], 1.0).then_inc(s["one"], 1)

                def rows(b, q, m):
                    hold(dve, s["y_ps"], b + 1)
                    if after(b, 2):
                        hold(dve, y_out[q], m * 16)
                    nc.vector.tensor_copy(ys[:, q, :], py[:, q, :]).then_inc(s["y_ok"], 1)

                steps(dve, [(0, rows)], NB)


        xst.close()
        yb = sb(top, "expert_chunk", [P, 2, C, NE * D])

        with ExitStack() as st:
            ahead = sem("mixed_ahead")
            pg = sb(st, "node_rows", [P, 2, C, RK * PAY])
            sc = sb(st, "slot_scores", [P, C, RK, GH])
            sc2 = sb(st, "slot_scores2", [P, C, RK, GH])
            vm = sb(st, "slot_mask", [P, C, RK])
            kio = sb(st, "slot_ids_r", [P, RK])
            mx2 = sb(st, "node_slope", [P, C, GH])
            a_in = [sem("att_in0"), sem("att_in1")]
            a_ch, a_io, a_z, a_e, a_done = sem("att_ch"), sem("att_io"), sem("att_z"), sem("att_e"), sem("att_done")
            block = phase(st)

            @block.sync
            def _(sp):
                for c in range(2):
                    sp.dma_start(yb[:, c, :, :], by_block(Y[c * C * P:(c + 1) * C * P, :])).then_inc(ahead, 16)
                sp.wait_ge(ahead, 32)

            @block.gpsimd
            def _(pool):
                nc.gpsimd.iota(kio[:, :], pattern=[[1, RK]], base=0, channel_multiplier=0, allow_small_or_imprecise_dtypes=True).then_inc(a_io, 1)
                for c in range(NC):
                    if c >= 2:
                        pool.wait_ge(a_done, c - 1)
                    for i in range(C):
                        nc.gpsimd.indirect_dma_start(pg[:, c % 2, i, :], None, GD, bass.IndirectOffsetOnAxis(ap=rsi2[:, c * C + i:c * C + i + 1], axis=0)).then_inc(a_in[c % 2], 16)

            @block.scalar
            def _(act):
                for c in range(NC):
                    act.wait_ge(a_z, c + 1)
                    nc.scalar.activation(sc2[:, :, :, :], sc[:, :, :, :], ACT.Exp).then_inc(a_e, 1)

            @block.vector
            def _(dve):
                link = chain(dve, a_ch, 0, None)
                TT, TS = nc.vector.tensor_tensor, nc.vector.tensor_scalar
                dve.wait_ge(a_io, 1)
                for c in range(NC):
                    q, bl = c % 2, slice(c * C, (c + 1) * C)
                    rows = pg[:, q, :, :].rearrange("p b (k c) -> p (b k) c", c=PAY)
                    s1, s2 = (t[:, :, :, :].rearrange("p b k h -> p (b k) h") for t in (sc, sc2))
                    last = lambda t: t.rearrange("p b k h -> p b h k")
                    slot = lambda t: t.unsqueeze(2).to_broadcast([P, C, RK, GH])
                    link(TT(vm[:, :, :], kio[:, :].unsqueeze(1).to_broadcast([P, C, RK]), rdeg[:, bl].unsqueeze(2).to_broadcast([P, C, RK]), ALU.is_ge))
                    link(TS(vm[:, :, :], vm[:, :, :], LOW, None, ALU.mult))
                    dve.wait_ge(a_in[q], 16 * C * (c // 2 + 1))
                    link(TT(s1, rows[:, :, GW:PAY], vm[:, :, :].rearrange("p b k -> p (b k)").unsqueeze(2).to_broadcast([P, C * RK, GH]), ALU.add))
                    link(nc.vector.tensor_reduce(MXS[:, bl, :], last(sc[:, :, :, :]), AX, ALU.max))
                    link(TT(MXS[:, bl, :], MXS[:, bl, :], T[:, bl, GW:PAY], ALU.max))
                    link(TT(MXS[:, bl, :], MXS[:, bl, :], AD[:, bl, :], ALU.add))
                    link(TS(mx2[:, :, :], MXS[:, bl, :], SLOPE, None, ALU.mult))
                    link(TT(MXS[:, bl, :], MXS[:, bl, :], mx2[:, :, :], ALU.max))
                    link(TT(sc[:, :, :, :], sc[:, :, :, :], slot(AD[:, bl, :]), ALU.add))
                    link(TS(s2, s1, SLOPE, None, ALU.mult))
                    link(TT(s1, s1, s2, ALU.max))
                    TT(sc[:, :, :, :], sc[:, :, :, :], slot(MXS[:, bl, :]), ALU.subtract).then_inc(a_z, 1)
                    dve.wait_ge(a_e, c + 1)
                    link(nc.vector.tensor_reduce(ag[:, bl, GW:PAY], last(sc2[:, :, :, :]), AX, ALU.add))
                    hv = rows[:, :, 0:GW].rearrange("p r (h e) -> p r h e", e=NE)
                    link(TT(hv, hv, s2.unsqueeze(3).to_broadcast([P, C * RK, GH, NE]), ALU.mult))
                    nc.vector.tensor_reduce(ag[:, bl, 0:GW], pg[:, q, :, :].rearrange("p b (k c) -> p b c k", c=PAY)[:, :, 0:GW, :], AX, ALU.add).then_inc(a_done, 1)
                    dve.wait_ge(a_done, c + 1)

        edge_pass("max")

        with ExitStack() as st:
            ms = sb(st, "score_max", [P, NB, 2 * GH])
            m2 = sb(st, "score_slope", [P, NB, GH])
            m_in, m_ch, m_out = sem("shift_in"), sem("shift_chain"), sem("shift_out")
            block = phase(st)

            @block.sync
            def _(sp):
                with where(sp, 1):
                    sp.dma_start(MXS[:, :, :], by_block(MAXT)).then_inc(m_in, 16)
                    sp.wait_ge(m_ch, 6)
                    sp.dma_start(by_block(MD), ms[:, :, :]).then_inc(m_out, 16)
                    sp.wait_ge(m_out, 16)

            @block.vector
            def _(dve):
                with where(dve, 1):
                    dve.wait_ge(m_in, 16)
                    link = chain(dve, m_ch, 0, 6)
                    link(nc.vector.tensor_tensor(MXS[:, :, :], MXS[:, :, :], T[:, :, GW:PAY], ALU.max))
                    link(nc.vector.tensor_tensor(MXS[:, :, :], MXS[:, :, :], AD[:, :, :], ALU.add))
                    link(nc.vector.tensor_scalar(m2[:, :, :], MXS[:, :, :], SLOPE, None, ALU.mult))
                    link(nc.vector.tensor_tensor(MXS[:, :, :], MXS[:, :, :], m2[:, :, :], ALU.max))
                    link(nc.vector.tensor_copy(ms[:, :, 0:GH], AD[:, :, :]))
                    link(nc.vector.tensor_copy(ms[:, :, GH:2 * GH], MXS[:, :, :]))

        edge_pass("soft")

        with ExitStack() as st:
            ag_in = sem("general_in")
            block = phase(st)

            @block.sync
            def _(sp):
                with where(sp, 1):
                    sp.dma_start(ag[:, :, :], by_block(AGG)).then_inc(ag_in, 16)
                    sp.wait_ge(ag_in, 16)

        with ExitStack() as st:
            z = sb(st, "own_score", [P, NB, 2, GH])
            y = sb(st, "router_out", [P, NB, GW])
            y2 = sb(st, "router_sq", [P, NB, GW])
            v = sb(st, "router_stats", [P, 4, NB])
            sc = sb(st, "expert_scores", [P, NB, NE])
            rk = sb(st, "expert_ranks", [P, NB, NE])
            cm = sb(st, "expert_compare", [P, NB, NE])
            g_in, g_ch, e1, e2, q1 = sem("gate_in"), sem("gate_chain"), sem("gate_exp1"), sem("gate_exp2"), sem("gate_sqrt")
            a1, a2, a3 = sem("gate_at_exp1"), sem("gate_at_exp2"), sem("gate_at_sqrt")
            block = phase(st)

            @block.scalar
            def _(act):
                act.wait_ge(a1, 1)
                nc.scalar.activation(z[:, :, 0, :], z[:, :, 1, :], ACT.Exp).then_inc(e1, 1)
                act.wait_ge(a3, 1)
                nc.scalar.activation(v[:, 3, :], v[:, 2, :], ACT.Sqrt).then_inc(q1, 1)
                act.wait_ge(a2, 1)
                nc.scalar.activation(sc[:, :, :], cm[:, :, :], ACT.Exp).then_inc(e2, 1)

            @block.vector
            def _(dve):
                link = chain(dve, g_ch, 0, None)
                TT, TS = nc.vector.tensor_tensor, nc.vector.tensor_scalar
                heads = lambda t: t.rearrange("p b (h e) -> p b h e", e=NE)
                wide = lambda t, n: t.unsqueeze(len(t.shape)).to_broadcast([*t.shape, n])
                link(TT(z[:, :, 0, :], T[:, :, GW:PAY], AD[:, :, :], ALU.add))
                link(TS(z[:, :, 1, :], z[:, :, 0, :], SLOPE, None, ALU.mult))
                link(TT(z[:, :, 0, :], z[:, :, 0, :], z[:, :, 1, :], ALU.max))
                TT(z[:, :, 1, :], z[:, :, 0, :], MXS[:, :, :], ALU.subtract).then_inc(a1, 1)
                dve.wait_ge(e1, 1)
                link(TT(heads(y[:, :, :]), heads(T[:, :, 0:GW]), wide(z[:, :, 0, :], NE), ALU.mult))
                link(TT(y[:, :, :], y[:, :, :], ag[:, :, 0:GW], ALU.add))
                link(TT(z[:, :, 1, :], z[:, :, 0, :], ag[:, :, GW:PAY], ALU.add))
                link(TS(z[:, :, 1, :], z[:, :, 1, :], DEN_EPS, None, ALU.add))
                link(nc.vector.reciprocal(z[:, :, 0, :], z[:, :, 1, :]))
                link(TT(heads(y[:, :, :]), heads(y[:, :, :]), wide(z[:, :, 0, :], NE), ALU.mult))
                row = lambda k: gb[:, k, :].unsqueeze(1).to_broadcast([P, NB, GW])
                link(TT(y[:, :, :], y[:, :, :], row(0), ALU.add))
                link(nc.vector.tensor_reduce(v[:, 0, :], y[:, :, :], AX, ALU.add))
                link(TS(v[:, 1, :], v[:, 0, :], 1.0 / GW, None, ALU.mult))
                link(TT(y[:, :, :], y[:, :, :], wide(v[:, 1, :], GW), ALU.subtract))
                link(TT(y2[:, :, :], y[:, :, :], y[:, :, :], ALU.mult))
                link(nc.vector.tensor_reduce(v[:, 0, :], y2[:, :, :], AX, ALU.add))
                TS(v[:, 2, :], v[:, 0, :], 1.0 / GW, LN_EPS, ALU.mult, ALU.add).then_inc(a3, 1)
                dve.wait_ge(q1, 1)
                link(nc.vector.reciprocal(v[:, 0, :], v[:, 3, :]))
                link(TT(y[:, :, :], y[:, :, :], wide(v[:, 0, :], GW), ALU.mult))
                link(TT(y[:, :, :], y[:, :, :], row(1), ALU.mult))
                link(TT(y[:, :, :], y[:, :, :], row(2), ALU.add))
                link(nc.vector.tensor_reduce(sc[:, :, :], y[:, :, :].rearrange("p b (h e) -> p b e h", e=NE), AX, ALU.add))
                link(TS(sc[:, :, :], sc[:, :, :], 1.0 / GH, None, ALU.mult))
                link(nc.vector.memset(rk[:, :, :], 0.0))
                for j in range(NE):
                    for a, b, op in ((0, j, ALU.is_gt), (j + 1, NE, ALU.is_ge)):
                        if a < b:
                            link(TT(cm[:, :, a:b], sc[:, :, j:j + 1].to_broadcast([P, NB, b - a]), sc[:, :, a:b], op))
                            link(TT(rk[:, :, a:b], rk[:, :, a:b], cm[:, :, a:b], ALU.add))
                link(TS(rk[:, :, :], rk[:, :, :], 1.5, None, ALU.is_lt))
                link(nc.vector.tensor_reduce(v[:, 0, :], sc[:, :, :], AX, ALU.max))
                TT(cm[:, :, :], sc[:, :, :], wide(v[:, 0, :], NE), ALU.subtract).then_inc(a2, 1)
                dve.wait_ge(e2, 1)
                link(TT(gate[:, :, :], sc[:, :, :], rk[:, :, :], ALU.mult))
                link(nc.vector.tensor_reduce(v[:, 1, :], gate[:, :, :], AX, ALU.add))
                link(nc.vector.reciprocal(v[:, 2, :], v[:, 1, :]))
                link(TT(gate[:, :, :], gate[:, :, :], wide(v[:, 2, :], NE), ALU.mult))

        with ExitStack() as st:
            y_in, o_out = [sem("mixed_in0"), sem("mixed_in1")], sem("mixed_out")
            done = sem("mixed")
            block = phase(st)

            @block.sync
            def _(sp):
                def load(c, q, m):
                    if not after(c, 2):
                        return
                    hold(sp, done, (c - 1) * (NE * C))
                    sp.dma_start(yb[:, q, :, :], by_block(Y[bass.ds(c * (C * P), C * P), :])).then_inc(y_in[q], 16)

                def store(c, q, m):
                    hold(sp, done, c * (NE * C) + NE * C)
                    n = C if not isinstance(c, int) or c < NC - 1 else C - 1
                    sp.dma_start(by_block(out[bass.ds(c * (C * P), n * P), :]), X[:, bass.ds(c * C, n), :]).then_inc(o_out, 16)
                    if n < C:
                        sp.dma_start(out[(NB - 1) * P:N, :], X[0:LAST, NB - 1, :]).then_inc(o_out, 16)

                steps(sp, [(0, load), (1, store)], NC)
                sp.wait_ge(o_out, 16 * (NC + 1))

            @block.vector
            def _(dve):
                def combine(c, q, m):
                    if after(c, 2):
                        hold(dve, y_in[q], m * 16)
                    for e in range(NE):
                        if e:
                            hold(dve, done, c * (NE * C) + e * C)
                        for i in range(C):
                            x1 = X[:, bass.ds(c * C + i, 1), :].rearrange("p a b -> p (a b)")
                            g = gate[:, bass.ds(c * C + i, 1), e:e + 1].rearrange("p a b -> p (a b)")
                            nc.vector.scalar_tensor_tensor(out=x1, in0=yb[:, q, i, e * D:(e + 1) * D], scalar=g, in1=x1, op0=ALU.mult, op1=ALU.add).then_inc(done, 1)

                steps(dve, [(0, combine)], NC)


_INS = ["x", "src", "dst", "L0_gnn_W", "L0_gnn_b", "L0_mix_w_qkv", "L0_mix_w_out", "L0_mix_b_out", "L0_ffn_W_gat",
        "L0_ffn_att_src", "L0_ffn_att_dst", "L0_ffn_b_gat", "L0_ffn_ln_gamma", "L0_ffn_ln_beta", "L0_ffn_W1",
        "L0_ffn_b1", "L0_ffn_W2", "L0_ffn_b2", "L0_ffn_edge_index"]
_OUTS = [((6250, 256), "float32")]


def kernel(**inputs):
    import numpy as _np
    import concourse.bacc as _bacc
    from concourse import mybir as _mybir
    from concourse.bass_utils import run_bass_kernel_spmd as _run

    nc = _bacc.Bacc("TRN2", target_bir_lowering=False, num_devices=1)
    arrays, args = {}, []
    for name in _INS:
        a = _np.ascontiguousarray(inputs[name])
        arrays[f"in_{name}_dram"] = a
        args.append(nc.dram_tensor(f"in_{name}_dram", a.shape, _mybir.dt.from_np(a.dtype), kind="ExternalInput").ap())
    for i, (shape, dtype) in enumerate(_OUTS):
        dt = _mybir.dt.from_np(_np.dtype(dtype))
        args.append(nc.dram_tensor(f"out_{i}_dram", shape, dt, kind="ExternalOutput").ap())
    build(nc, *args)
    r = _run(nc, [arrays], core_ids=[0])
    return r.results[0]["out_0_dram"]
```
